# Optimizing a Trainium2 kernel written in Bass

```python
import numpy as np
import jax
import jax.numpy as jnp

def _softmax(x, axis=-1):
    return jax.nn.softmax(x, axis=axis)

def _gelu(x):
    return jax.nn.gelu(x, approximate=True)

def _silu(x):
    return jax.nn.silu(x)

def _sigmoid(x):
    return jax.nn.sigmoid(x)

def _layernorm(x, axis=-1, eps=1e-05):
    m = jnp.mean(x, axis=axis, keepdims=True)
    v = jnp.var(x, axis=axis, keepdims=True)
    return (x - m) / jnp.sqrt(v + eps)

def _scatter_add(tgt, idx, src, axis=0):
    return tgt.at[idx].add(src)

def _segment_sum(src, seg, n):
    return jax.ops.segment_sum(src, seg, n)
kernel_name = 'mk_macaron_d2_jaxref_r8_4763ae'

def setup_inputs(seed: int=0):
    np.random.seed(seed)
    _w = jnp.asarray

    def _L0_attn_setup():
        import jax, jax.numpy as jnp
        import numpy as np
        B, T, E, H, L = (1, 256, 256, 16, 64)
        D = E // H
        RA_WINDOW = 64
        RA_ALPHA = 0.5
        key = jax.random.key(seed)
        ks = jax.random.split(key, 7)

        def w(k, shape, fan_in):
            return jax.random.normal(k, shape, dtype=jnp.float32) / np.sqrt(fan_in)
        return {'hidden_states': jax.random.normal(ks[0], (B, T, E), dtype=jnp.float32), 'w_q': w(ks[1], (E, E), E), 'w_k_down': w(ks[2], (L, E), E), 'w_v_down': w(ks[3], (L, E), E), 'q_to_latent': w(ks[4], (H, D, L), D), 'v_up': w(ks[5], (H, L, D), L), 'w_out': w(ks[6], (E, E), E)}
    _L0_attn_in = _L0_attn_setup()

    def _L0_ffn_setup():
        import jax, jax.numpy as jnp
        import numpy as np
        HIDDEN = 256
        INTER = 1024
        SCALE = 64.0

        def fwht(x):
            orig_shape = x.shape
            n = orig_shape[-1]
            x = x.reshape(-1, n)
            h = 1
            while h < n:
                x = x.reshape(-1, n // (2 * h), 2, h)
                a, b = (x[:, :, 0, :], x[:, :, 1, :])
                x = jnp.stack([a + b, a - b], axis=2).reshape(-1, n)
                h *= 2
            return (x / jnp.sqrt(jnp.asarray(n, x.dtype))).reshape(orig_shape)
        key = jax.random.key(seed)
        ks = jax.random.split(key, 8)
        inp = jax.random.normal(ks[0], (4, 256, HIDDEN), dtype=jnp.float32)
        SU_ug = jnp.where(jax.random.bernoulli(ks[1], 0.5, (HIDDEN,)), 1.0, -1.0).astype(jnp.float32)
        SU_dp = jnp.where(jax.random.bernoulli(ks[2], 0.5, (INTER,)), 1.0, -1.0).astype(jnp.float32)
        Wscale_ug = jax.random.uniform(ks[3], (2 * INTER,), jnp.float32, 0.5, 1.5)
        Wscale_dp = jax.random.uniform(ks[4], (HIDDEN,), jnp.float32, 0.5, 1.5)
        W_up = jax.random.normal(ks[5], (INTER, HIDDEN), dtype=jnp.float32) * 0.02
        W_gate = jax.random.normal(ks[6], (INTER, HIDDEN), dtype=jnp.float32) * 0.02
        W_down = jax.random.normal(ks[7], (HIDDEN, INTER), dtype=jnp.float32) * 0.02
        return {'input': inp, 'SU_ug': SU_ug, 'SU_dp': SU_dp, 'Wscale_ug': Wscale_ug, 'Wscale_dp': Wscale_dp, 'W_up': W_up, 'W_gate': W_gate, 'W_down': W_down}
    _L0_ffn_in = _L0_ffn_setup()

    def _L1_attn_setup():
        import jax, jax.numpy as jnp
        import numpy as np
        H = 256
        NH = 16
        HD = H // NH
        B, T = (2, 256)
        key = jax.random.key(seed)
        ks = jax.random.split(key, 5)
        s = 1.0 / np.sqrt(H)
        return {'x': jax.random.normal(ks[0], (B, T, H), dtype=jnp.float32), 'wq': jax.random.normal(ks[1], (H, H), dtype=jnp.float32) * s, 'bq': jnp.zeros((H,), dtype=jnp.float32), 'wk': jax.random.normal(ks[2], (H, H), dtype=jnp.float32) * s, 'bk': jnp.zeros((H,), dtype=jnp.float32), 'wv': jax.random.normal(ks[3], (H, H), dtype=jnp.float32) * s, 'bv': jnp.zeros((H,), dtype=jnp.float32), 'wo': jax.random.normal(ks[4], (H, H), dtype=jnp.float32) * s, 'bo': jnp.zeros((H,), dtype=jnp.float32)}
    _L1_attn_in = _L1_attn_setup()

    def _L1_ffn_setup():
        import jax, jax.numpy as jnp
        import numpy as np
        TOPK = 6
        CAP = 128
        ROUTE_SCALE = 1.0
        key = jax.random.key(seed)
        k = jax.random.split(key, 6)
        B, T, C = (2, 256, 256)
        E, H, HS = (64, 32, 64)
        std = 0.01
        return {'x': jax.random.normal(k[0], (B, T, C), jnp.float32), 'w_gate': jax.random.normal(k[1], (C, E), jnp.float32) * std, 'w_shared_up': jax.random.normal(k[2], (C, 2 * HS), jnp.float32) * std, 'w_shared_down': jax.random.normal(k[3], (HS, C), jnp.float32) * std, 'w_up': jax.random.normal(k[4], (E, C, 2 * H), jnp.float32) * std, 'w_down': jax.random.normal(k[5], (E, H, C), jnp.float32) * std}
    _L1_ffn_in = _L1_ffn_setup()
    _d = {'L0_attn_hidden_states': _L0_attn_in['hidden_states'], 'L0_attn_w_q': _L0_attn_in['w_q'], 'L0_attn_w_k_down': _L0_attn_in['w_k_down'], 'L0_attn_w_v_down': _L0_attn_in['w_v_down'], 'L0_attn_q_to_latent': _L0_attn_in['q_to_latent'], 'L0_attn_v_up': _L0_attn_in['v_up'], 'L0_attn_w_out': _L0_attn_in['w_out'], 'L0_ffn_SU_ug': _L0_ffn_in['SU_ug'], 'L0_ffn_SU_dp': _L0_ffn_in['SU_dp'], 'L0_ffn_Wscale_ug': _L0_ffn_in['Wscale_ug'], 'L0_ffn_Wscale_dp': _L0_ffn_in['Wscale_dp'], 'L0_ffn_W_up': _L0_ffn_in['W_up'], 'L0_ffn_W_gate': _L0_ffn_in['W_gate'], 'L0_ffn_W_down': _L0_ffn_in['W_down'], 'L1_attn_wq': _L1_attn_in['wq'], 'L1_attn_bq': _L1_attn_in['bq'], 'L1_attn_wk': _L1_attn_in['wk'], 'L1_attn_bk': _L1_attn_in['bk'], 'L1_attn_wv': _L1_attn_in['wv'], 'L1_attn_bv': _L1_attn_in['bv'], 'L1_attn_wo': _L1_attn_in['wo'], 'L1_attn_bo': _L1_attn_in['bo'], 'L1_ffn_w_gate': _L1_ffn_in['w_gate'], 'L1_ffn_w_shared_up': _L1_ffn_in['w_shared_up'], 'L1_ffn_w_shared_down': _L1_ffn_in['w_shared_down'], 'L1_ffn_w_up': _L1_ffn_in['w_up'], 'L1_ffn_w_down': _L1_ffn_in['w_down']}
    _x0 = _d['L0_attn_hidden_states']
    _d['L0_attn_hidden_states'] = jax.random.normal(jax.random.fold_in(jax.random.key(seed), 1), (8, 256, 256), dtype=_x0.dtype)
    del _x0
    return _d

def reference(L0_attn_hidden_states, L0_attn_w_q, L0_attn_w_k_down, L0_attn_w_v_down, L0_attn_q_to_latent, L0_attn_v_up, L0_attn_w_out, L0_ffn_SU_ug, L0_ffn_SU_dp, L0_ffn_Wscale_ug, L0_ffn_Wscale_dp, L0_ffn_W_up, L0_ffn_W_gate, L0_ffn_W_down, L1_attn_wq, L1_attn_bq, L1_attn_wk, L1_attn_bk, L1_attn_wv, L1_attn_bv, L1_attn_wo, L1_attn_bo, L1_ffn_w_gate, L1_ffn_w_shared_up, L1_ffn_w_shared_down, L1_ffn_w_up, L1_ffn_w_down):

    def _L0_attn_ref(hidden_states, w_q, w_k_down, w_v_down, q_to_latent, v_up, w_out):
        import jax, jax.numpy as jnp
        import numpy as np
        B, T, E, H, L = (1, 256, 256, 16, 64)
        D = E // H
        RA_WINDOW = 64
        RA_ALPHA = 0.5
        b, t, e = hidden_states.shape
        h, d, l = q_to_latent.shape
        Q = (hidden_states @ w_q.T).reshape(b, t, h, d)
        latent_k = hidden_states @ w_k_down.T
        latent_v = hidden_states @ w_v_down.T
        q_latent = jnp.einsum('bthd,hdl->bthl', Q, q_to_latent)
        raw = jnp.einsum('bthl,bsl->bhts', q_latent, latent_k) / jnp.sqrt(jnp.float32(l))
        pos = jnp.arange(t)
        causal = pos[None, :] <= pos[:, None]
        band = jnp.abs(pos[:, None] - pos[None, :]) < RA_WINDOW
        logits = jnp.where(causal, raw, -jnp.inf)
        logits = jnp.where(band & causal, raw * (1.0 + RA_ALPHA), logits)
        attn = jax.nn.softmax(logits, axis=-1)
        V = jnp.einsum('btl,hld->bthd', latent_v, v_up)
        ctx = jnp.einsum('bhts,bshd->bthd', attn, V)
        out = ctx.reshape(b, t, h * d) @ w_out.T
        return out

    def _L0_ffn_ref(input, SU_ug, SU_dp, Wscale_ug, Wscale_dp, W_up, W_gate, W_down):
        import jax, jax.numpy as jnp
        import numpy as np
        HIDDEN = 256
        INTER = 1024
        SCALE = 64.0

        def fwht(x):
            orig_shape = x.shape
            n = orig_shape[-1]
            x = x.reshape(-1, n)
            h = 1
            while h < n:
                x = x.reshape(-1, n // (2 * h), 2, h)
                a, b = (x[:, :, 0, :], x[:, :, 1, :])
                x = jnp.stack([a + b, a - b], axis=2).reshape(-1, n)
                h *= 2
            return (x / jnp.sqrt(jnp.asarray(n, x.dtype))).reshape(orig_shape)
        n = SU_ug.shape[0]
        x = input.reshape(-1, n)
        x = fwht(x * SU_ug) / SCALE
        x_up = x @ W_up.T * (Wscale_ug[:INTER] * SCALE)
        x_gate = x @ W_gate.T * (Wscale_ug[INTER:] * SCALE)
        x = jax.nn.silu(x_gate) * x_up
        x = fwht(x * SU_dp) / SCALE
        x = x @ W_down.T * (Wscale_dp * SCALE)
        return x.reshape(input.shape)

    def _L1_attn_ref(x, wq, bq, wk, bk, wv, bv, wo, bo):
        import jax, jax.numpy as jnp
        import numpy as np
        H = 256
        NH = 16
        HD = H // NH
        B, T = (2, 256)
        Bx, Tx, C = x.shape
        q = x @ wq.T + bq
        k = x @ wk.T + bk
        v = x @ wv.T + bv
        q = q.reshape(Bx, Tx, NH, HD).transpose(0, 2, 1, 3)
        k = k.reshape(Bx, Tx, NH, HD).transpose(0, 2, 1, 3)
        v = v.reshape(Bx, Tx, NH, HD).transpose(0, 2, 1, 3)
        scale = 1.0 / np.sqrt(HD).astype(np.float32)
        scores = jnp.einsum('bhqd,bhkd->bhqk', q, k) * scale
        causal = jnp.tril(jnp.ones((Tx, Tx), dtype=bool))
        scores = jnp.where(causal[None, None], scores, -jnp.inf)
        attn = jax.nn.softmax(scores, axis=-1)
        out = jnp.einsum('bhqk,bhkd->bhqd', attn, v)
        out = out.transpose(0, 2, 1, 3).reshape(Bx, Tx, C)
        return out @ wo.T + bo

    def _L1_ffn_ref(x, w_gate, w_shared_up, w_shared_down, w_up, w_down):
        import jax, jax.numpy as jnp
        import numpy as np
        TOPK = 6
        CAP = 128
        ROUTE_SCALE = 1.0
        B, T, C = x.shape
        E = w_gate.shape[1]
        x_flat = x.reshape(-1, C)
        N = x_flat.shape[0]
        su = x_flat @ w_shared_up
        y_s, g_s = jnp.split(su, 2, axis=-1)
        shared = jax.nn.silu(g_s) * y_s @ w_shared_down
        scores = jax.nn.sigmoid(x_flat @ w_gate)
        _, topk_idx = jax.lax.top_k(scores, TOPK)
        w = jnp.take_along_axis(scores, topk_idx, axis=-1)
        w = w / w.sum(-1, keepdims=True) * ROUTE_SCALE
        flat_e = topk_idx.reshape(-1)
        oh = jax.nn.one_hot(flat_e, E, dtype=jnp.int32)
        pos = jnp.take_along_axis(jnp.cumsum(oh, axis=0), flat_e[:, None], axis=1)[:, 0] - 1
        valid = pos < CAP
        pos_c = jnp.where(valid, pos, CAP - 1)
        token_ids = jnp.repeat(jnp.arange(N), TOPK)
        x_disp = jnp.zeros((E, CAP, C), x.dtype).at[flat_e, pos].set(x_flat[token_ids], mode='drop')
        up = jnp.einsum('ecd,edh->ech', x_disp, w_up)
        g_r, v_r = jnp.split(up, 2, axis=-1)
        h_r = jax.nn.silu(g_r) * v_r
        out_r = jnp.einsum('ech,ehd->ecd', h_r, w_down)
        y_ts = out_r[flat_e, pos_c]
        y_ts = jnp.where(valid[:, None], y_ts, 0.0)
        routed = (y_ts.reshape(N, TOPK, C) * w[:, :, None]).sum(axis=1)
        return (shared + routed).reshape(B, T, C)
    x = L0_attn_hidden_states
    x = x + 0.5 * _L0_ffn_ref(_layernorm(x, axis=-1), L0_ffn_SU_ug, L0_ffn_SU_dp, L0_ffn_Wscale_ug, L0_ffn_Wscale_dp, L0_ffn_W_up, L0_ffn_W_gate, L0_ffn_W_down)
    x = x + _L0_attn_ref(_layernorm(x, axis=-1), L0_attn_w_q, L0_attn_w_k_down, L0_attn_w_v_down, L0_attn_q_to_latent, L0_attn_v_up, L0_attn_w_out)
    x = x + 0.5 * _L0_ffn_ref(_layernorm(x, axis=-1), L0_ffn_SU_ug, L0_ffn_SU_dp, L0_ffn_Wscale_ug, L0_ffn_Wscale_dp, L0_ffn_W_up, L0_ffn_W_gate, L0_ffn_W_down)
    x = x + 0.5 * _L1_ffn_ref(_layernorm(x, axis=-1), L1_ffn_w_gate, L1_ffn_w_shared_up, L1_ffn_w_shared_down, L1_ffn_w_up, L1_ffn_w_down)
    x = x + _L1_attn_ref(_layernorm(x, axis=-1), L1_attn_wq, L1_attn_bq, L1_attn_wk, L1_attn_bk, L1_attn_wv, L1_attn_bv, L1_attn_wo, L1_attn_bo)
    x = x + 0.5 * _L1_ffn_ref(_layernorm(x, axis=-1), L1_ffn_w_gate, L1_ffn_w_shared_up, L1_ffn_w_shared_down, L1_ffn_w_up, L1_ffn_w_down)
    return x

_drawn_inputs = setup_inputs


def setup_inputs(seed=0):
    import zlib

    import numpy as np

    out = dict(_drawn_inputs(seed))
    spreads = {'L1_attn_bq': (0.0, 1.259),
     'L1_attn_bk': (0.0, 2.0),
     'L1_attn_bv': (0.0, 0.1),
     'L1_attn_bo': (0.0, 0.269)}
    factors = {'L0_ffn_Wscale_ug': 4.01,
     'L0_ffn_Wscale_dp': 5.558,
     'L1_ffn_w_gate': 8.0,
     'L1_ffn_w_shared_up': 8.0,
     'L1_ffn_w_shared_down': 8.0,
     'L1_ffn_w_up': 8.0,
     'L1_ffn_w_down': 8.0}
    for name, (base, spread) in spreads.items():
        noise = np.random.default_rng([zlib.crc32(name.encode()), seed]).standard_normal(out[name].shape)
        drawn = base * np.exp(spread * noise) if base else spread * noise
        out[name] = jnp.asarray(drawn.astype(out[name].dtype))
    for name, factor in factors.items():
        out[name] = (out[name] * factor).astype(out[name].dtype)
    return out
```

```python
import concourse.bass as bass
from concourse import mybir
from contextlib import ExitStack

TOKENS, C = 2048, 256
BATCH = 256
INTER = 1024
HEADS, HD = 16, 16
LATENT = 64
EXPERTS, EH, CAP, TOPK = 64, 32, 128, 6
SHARED = 64
WINDOW, ALPHA = 64, 0.5
EPS = 1e-5

P = 128
CK = C // P
TILES = TOKENS // P
GROUP = 512
GT = GROUP // P
GROUPS = TOKENS // GROUP
FJ = INTER // P
MJ = EXPERTS * EH // P
KEYS = 3 * P
BIG = 3.0e38

STAGES = ["F", "A0", "F", "E", "A1", "E"]

USES = {
    "G": {"F": FJ, "A": 4 * 2 + 2 * HEADS, "E": MJ},
    "U": {"F": FJ, "A": 2 * HEADS, "E": MJ},
    "T": {"F": 2, "A": 6, "E": 6},
    "Tf": {"F": 0, "A": 4, "E": 4},
    "A": {"F": 2, "A": 4, "E": 2},
    "h": {"F": FJ, "A": 0, "E": MJ},
    "w": {"F": 0, "A": 0, "E": MJ},
    "head": {"F": 0, "A": 2 * HEADS, "E": 0},
    "quarter": {"F": 0, "A": 4, "E": 0},
    "half": {"F": 0, "A": 2, "E": 0},
    "moe": {"F": 0, "A": 0, "E": 1},
    "unit": {"F": 1, "A": 1, "E": 1},
    "Af": {"F": 0, "A": 2, "E": 0},
}
BEFORE = {"U": 14, "T": 2}
N_T_STEPS = 3


def butterflies():
    where, spare, levels = [P * j for j in range(FJ)], [P * (FJ + j) for j in range(FJ // 2)], []
    for step in (1, 2, 4):
        level, freed = [], []
        for q, (a, b) in enumerate((a, a + step) for a in range(FJ) if not a & step):
            level.append((where[a], where[b], spare[q]))
            freed.append(where[b])
            where[b] = spare[q]
        levels.append(level)
        spare = freed
    return levels, where


BUTTERFLIES, CHUNK_AT = butterflies()


def build(nc, x, fgate, fup, fdown, su_ug, su_dp, ws_ug, ws_dp, q0, o0, kd0, vd0, ql0, vu0,
          q1, k1, v1, o1, bq, bk, bv, bo, mgate, mshup, mshdown, mup, mdown,
          had, ident, before, bandm, causal, hilo, out):
    F32, R32, BF16 = mybir.dt.float32, mybir.dt.float32r, mybir.dt.bfloat16
    I32 = mybir.dt.int32
    ALU, ACT, AX = mybir.AluOpType, mybir.ActivationFunctionType, mybir.AxisListType

    ctx = ExitStack()
    with ctx:
        def sb(name, shape, dt=F32):
            return ctx.enter_context(nc.sbuf_tensor(name, shape, dt))

        def sem(name):
            return ctx.enter_context(nc.semaphore(name))

        xs = sb("xs", [P, TILES * C])
        WA = sb("WA", [P, 12288], R32)
        WM = sb("WM", [P, 4 * MJ * P * CK], R32)
        WT = sb("WT", [P, 6144], R32)
        xn = sb("xn", [P, 2 * 2 * CK * GROUP], R32)
        WR = sb("WR", [P, 4096], R32)
        WF = sb("WF", [P, 3584])
        xh = sb("xh", [P, GT, C])
        aux = sb("aux", [P, 2 * C])
        identf = sb("identf", [P, P])
        hadf = xh[:, 2, :].rearrange("p (s n) -> p s n", s=2)
        identb = sb("identb", [P, P], BF16)
        beforeb = sb("beforeb", [P, P], BF16)
        onesb = sb("onesb", [P, P], BF16)
        causalb = sb("causalb", [P, P], BF16)
        countb = sb("countb", [P, EXPERTS], BF16)
        maskb = sb("maskb", [P, GT, EXPERTS], BF16)
        zero = sb("zero", [P, 1])
        hilos = sb("hilos", [P, 1])
        suc = sb("suc", [P, CK + FJ])
        bqk = sb("bqk", [P, 2, 4])
        st = sb("st", [P, GT, 6])
        mv = sb("mv", [P, GT, 2])
        ve = sb("ve", [P, GT])
        y = sb("y", [P, GT])
        yt = sb("yt", [P, GT])
        nmax = sb("nmax", [P, 3, 2])
        den = sb("den", [P, 2, 2, HEADS])
        top = sb("top", [P, GT, 8])
        tot = sb("tot", [P, GT])

        fg = WA[:, 0:4096].rearrange("p (s c n) -> p s c n", s=2, c=CK)
        fu = WA[:, 4096:8192].rearrange("p (s c n) -> p s c n", s=2, c=CK)
        fd = WA[:, 8192:12288].rearrange("p (s j n) -> p s j n", s=2, j=FJ)
        md = WA[:, 0:8192].rearrange("p (s j n) -> p s j n", s=2, j=MJ)
        shu = WA[:, 8192:8704].rearrange("p (s c n) -> p s c n", s=2, c=CK)
        mg = WA[:, 8704:8960].rearrange("p (s c n) -> p s c n", s=2, c=CK)
        shd = WA[:, 8960:9472].rearrange("p (s n) -> p s n", s=2)
        mw = WM[:, :].rearrange("p (s c v j n) -> p s c v j n", s=2, c=CK, v=2, j=MJ)
        wq = WT[:, 0:2048].rearrange("p (s c n) -> p s c n", s=2, c=CK)
        wk = WT[:, 2048:4096].rearrange("p (s c n) -> p s c n", s=2, c=CK)
        wv = WT[:, 4096:5120].rearrange("p (s c n) -> p s c n", s=2, c=CK)
        wo = WT[:, 5120:6144].rearrange("p (s c n) -> p s c n", s=2, c=CK)
        xnv = xn[:, :].rearrange("p (b s c n) -> p b s c n", b=2, s=2, c=CK)
        hid = WR[:, 0:2048].rearrange("p (b s n) -> p b s n", b=2, s=2)
        shh = WR[:, 2048:3072].rearrange("p (s n) -> p s n", s=2)
        Qs = WR[:, 0:1024].rearrange("p (t n) -> p t n", t=4)
        KA = WR[:, 1024:2048].rearrange("p (t n) -> p t n", t=4)
        KB = WR[:, 2048:3072].rearrange("p (t n) -> p t n", t=4)
        cT = WR[:, 3072:4096].rearrange("p (s c n) -> p s c n", s=2, c=CK)
        sw = WF[:, 0:1024].rearrange("p (b n) -> p b n", b=2)
        wrep = WF[:, 1024:1536]
        sh = WF[:, 1536:2048]
        w2 = WF[:, 2048:2560].rearrange("p (t d e) -> p t d e", t=GT, d=2)
        lg = WF[:, 2560:2824].rearrange("p (t e) -> p t e", t=GT)
        lr = WF[:, 2824:3088].rearrange("p (t e) -> p t e", t=GT)
        sg = WF[:, 3088:3344].rearrange("p (t e) -> p t e", t=GT)
        Vs = WF[:, 0:512].rearrange("p (t n) -> p t n", t=2)
        Pr = WF[:, 512:1280].rearrange("p (b n) -> p b n", b=2)
        PT = WF[:, 1280:2048].rearrange("p (b n) -> p b n", b=2)
        cn = WF[:, 2048:2560].rearrange("p (t n) -> p t n", t=2)
        qf = WF[:, 2560:3072].rearrange("p (t n) -> p t n", t=2)
        kf = WF[:, 3072:3584].rearrange("p (t n) -> p t n", t=2)
        SLOT = 1536
        tmp = [WF[:, 3072:3584], xh[:, 0:2, :].rearrange("p a n -> p (a n)")]

        banks = [ctx.enter_context(nc.psum_tensor(f"bank{n}", [P, 512], F32)) for n in range(8)]

        def G(n): return banks[n % 2]
        def U(n): return banks[2 + n % 2]
        def T(n): return banks[4 + n % 2]
        def A(n): return banks[6 + n % 2]

        def S(n): return banks[(0, 1, 3)[n % 3]]
        TURNED = banks[2]

        def score_use(k):
            return k + 4 + 2 * (k >= 8) + 2 * (k >= 16)

        PROJECTION_USE = (0, 2, 12, 22)

        consts = sem("consts")
        xload = sem("xload")
        set_up = sem("set_up")
        cast = sem("cast")
        stage_full = [sem("stage_full0"), sem("stage_full1")]
        stage_done = sem("stage_done")
        w_high = sem("w_high")
        weights = sem("weights")
        g_full, g_done = sem("g_full"), sem("g_done")
        u_full, u_done = sem("u_full"), sem("u_done")
        t_full, t_done = sem("t_full"), sem("t_done")
        a_full, a_done = sem("a_full"), sem("a_done")
        stats = sem("stats")
        rstd = sem("rstd")
        xh_full, xh_read = sem("xh_full"), sem("xh_read")
        xn_high = sem("xn_high")
        xn_read = sem("xn_read")
        h_high = sem("h_high")
        h_ready = sem("h_ready")
        h_read = sem("h_read")
        weighted = sem("weighted")
        chosen = sem("chosen")
        sigm = sem("sigm")
        wmade = sem("wmade")
        sh_act, sh_high, sh_ready = sem("sh_act"), sem("sh_high"), sem("sh_ready")
        qk_ready = sem("qk_ready")
        maxed = sem("maxed")
        pv_done = sem("pv_done")
        ctx_high = sem("ctx_high")
        stored = sem("stored")
        banded = sem("banded")
        auxl = sem("auxl")

        RING = 2

        def kind(s):
            return STAGES[s][0]

        def base(what, s):
            return BEFORE.get(what, 0) + GROUPS * sum(USES[what][kind(r)] for r in range(s))

        def at(what, s, i, p, n=0):
            per = USES[what][kind(s)]
            return i * (2 * per) + (base(what, s) + p * per + n)

        def static(what, s, p, n=0):
            return base(what, s) + p * USES[what][kind(s)] + n

        def filled(index, k=1):
            return index + k

        def free(index):
            return index + 1

        def made(index):
            return index + 1 + RING

        def score_free(s, i, p, n):
            return at("G", s, i, p, max(0, n - 3 + 1)) + RING

        def group(i, p):
            return i * 2 + p

        def following(i, p):
            return i * 2 + 1 if p == 0 else 2 - i * 2

        def xt(g, t, n=1):
            return xs[:, bass.ds(g * (GT * C) + t * C, n * C)]

        block = ctx.enter_context(nc.Block())

        def spread(src, lo, n):
            return src[lo:lo + n].partition_broadcast(P)

        pieces = []
        for m, w in ((0, fgate), (1, fup)):
            for jh in range(2):
                pieces.append([(0, 1024, P, w.rearrange("(c p) n -> p c n", p=P)[:, :, jh * 512:(jh + 1) * 512]),
                               (1024, 512, P, spread(ws_ug, m * INTER + jh * 512, 512))])
        for ch in range(2):
            pieces.append([(0, 1024, P, fdown.rearrange("(j p) n -> p j n", p=P)[:, :, ch * P:(ch + 1) * P]),
                           (1024, P, P, spread(ws_dp, ch * P, P))])
        pieces.append([(0, 512, P, q0.rearrange("(c p) n -> p c n", p=P)),
                       (512, 512, P, o0.rearrange("(c p) n -> p c n", p=P))])
        pieces.append([(k * C, C, LATENT, w) for k, w in enumerate((kd0, vd0, ql0, vu0))])
        mupv = mup.rearrange("(c p) n -> p c n", p=P)
        for c in range(CK):
            for k in range(4):
                pieces.append([(0, 1024, P, mupv[:, c, k * 1024:(k + 1) * 1024])])
        FIRST_PIECES = len(pieces)
        pieces.append([(0, 512, P, q1.rearrange("(c p) n -> p c n", p=P)), (512, 512, P, k1.rearrange("(c p) n -> p c n", p=P))])
        pieces.append([(0, 512, P, v1.rearrange("(c p) n -> p c n", p=P)), (512, 512, P, o1.rearrange("(c p) n -> p c n", p=P))])
        mdv = mdown.rearrange("(j p) n -> p j n", p=P)
        for k in range(4):
            pieces.append([(0, 1024, P, mdv[:, 4 * k:4 * k + 4, :])])
        pieces.append([(0, 256, P, mshup.rearrange("(c p) n -> p c n", p=P)),
                       (256, 128, P, mgate.rearrange("(c p) n -> p c n", p=P)),
                       (384, 256, SHARED, mshdown)])

        def slot(n):
            return WF[:, (n % 2) * SLOT:(n % 2 + 1) * SLOT]

        def stage_value(n):
            return 16 * sum(len(pieces[m]) for m in range(n % 2, n + 1, 2))

        def load_pieces(eng, first, last):
            for n in range(first, last):
                eng.wait_ge(stage_done, free(n))
                for lo, w, parts, src in pieces[n]:
                    dst = slot(n)[0:parts, lo:lo + w]
                    if len(src.shape) == 3:
                        dst = dst.rearrange("p (a n) -> p a n", a=src.shape[1])
                    eng.dma_start(dst, src).then_inc(stage_full[n % 2], 16)

        def three(v, a):
            return v.rearrange("p (a n) -> p a n", a=a)

        def doubled(w, c):
            return [w[:, s, c, :].rearrange("p (h r d) -> p h r d", h=HEADS, r=2) for s in range(2)]

        def splits(n):
            v = slot(n)
            if n == 6 or n == FIRST_PIECES or n == FIRST_PIECES + 1:
                todo = []
                mats = {6: (("q", 0.125), ("o", 1.0)), FIRST_PIECES: (("q", 0.25), ("k", 1.0)),
                        FIRST_PIECES + 1: (("v", 1.0), ("o", 1.0))}[n]
                for m, (name, scale) in enumerate(mats):
                    src = v[:, m * 512:(m + 1) * 512]
                    if name in "qk":
                        w = wq if name == "q" else wk
                        for c in range(CK):
                            sv = src[:, c * C:(c + 1) * C].rearrange("p (h d) -> p h d", h=HEADS)
                            hi, lo = doubled(w, c)
                            for r in range(2):
                                todo.append((sv, hi[:, :, r, :], lo[:, :, r, :], scale))
                    else:
                        w = wv if name == "v" else wo
                        todo.append((three(src, CK), w[:, 0, :, :], w[:, 1, :, :], scale))
                return todo
            if 8 <= n < FIRST_PIECES:
                c, k = (n - 8) // 4, (n - 8) % 4
                hi, lo = (mw[:, s, c, k // 2, (k % 2) * 8:(k % 2) * 8 + 8, :].rearrange("p j n -> p (j n)") for s in range(2))
                return [(v[:, 0:1024], hi, lo, 1.0)]
            if n < FIRST_PIECES + 6:
                k = n - FIRST_PIECES - 2
                hi, lo = (md[:, s, 4 * k:4 * k + 4, :].rearrange("p j n -> p (j n)") for s in range(2))
                return [(v[:, 0:1024], hi, lo, 0.5)]
            return [(three(v[:, 0:256], CK), shu[:, 0, :, :], shu[:, 1, :, :], 1.0),
                    (three(v[:, 256:384], CK), mg[:, 0, :, :], mg[:, 1, :, :], 1.0),
                    (v[0:SHARED, 384:640], shd[0:SHARED, 0, :], shd[0:SHARED, 1, :], 0.5)]

        DERIVED = [2, 2, 2, 2, 8, 8, None, 8]

        def highs(n):
            return sum((DERIVED[m] if m < 8 and m != 6 else len(splits(m))) for m in range(n))

        def split_high(eng, n):
            eng.wait_ge(stage_full[n % 2], stage_value(n))
            for src, hi, lo, scale in splits(n):
                eng.activation(hi, src, ACT.Copy, scale=scale).then_inc(w_high, 1)

        def split_low(eng, n):
            todo = splits(n)
            for k, (src, hi, lo, scale) in enumerate(todo):
                eng.wait_ge(w_high, highs(n) + k + 1)
                ins = eng.scalar_tensor_tensor(lo, src, scale, hi.bitcast(F32), ALU.mult, ALU.subtract)
            ins.then_inc(stage_done, 1)

        @block.sync
        def _(sp):
            sp.dma_start(identf[:, :], ident).then_inc(consts, 16)
            sp.dma_start(hadf[:, 0, :], had).then_inc(consts, 16)
            sp.dma_start(aux[:, 0:KEYS], bandm).then_inc(consts, 16)
            sp.dma_start(hilos[:, :], hilo).then_inc(consts, 16)
            sp.dma_start(suc[:, 0:CK], su_ug).then_inc(consts, 16)
            sp.dma_start(suc[:, CK:CK + FJ], su_dp).then_inc(consts, 16)
            sp.dma_start(xh[:, 0, 0:P], before).then_inc(consts, 16)
            sp.dma_start(xh[:, 0, P:2 * P], causal).then_inc(consts, 16)
            load_pieces(sp, 0, 2)
            sp.dma_start(xs[:, :].rearrange("p (t n) -> p t n", t=TILES),
                         x.rearrange("(t p) n -> p t n", p=P)).then_inc(xload, 16)
            load_pieces(sp, 2, FIRST_PIECES)
            if len(STAGES) > 3:
                sp.wait_ge(a_done, made(base("A", 3) - 1))
                sp.dma_start(aux[:, 0:C], bv.partition_broadcast(P)).then_inc(auxl, 16)
                sp.dma_start(aux[:, C:2 * C], bo.partition_broadcast(P)).then_inc(auxl, 16)
                sp.dma_start(bqk[:, 0, :], bq).then_inc(auxl, 16)
                sp.dma_start(bqk[:, 1, :], bk).then_inc(auxl, 16)
                load_pieces(sp, FIRST_PIECES, len(pieces))
            s = len(STAGES) - 1
            outv = out.rearrange("(t p) n -> p t n", p=P)
            per = USES["A"][kind(s)]
            with sp.Fori(0, GROUPS // 2) as i:
                for p in range(2):
                    sp.wait_ge(a_done, made(at("A", s, i, p, per - 1)))
                    sp.dma_start(outv[:, bass.ds(group(i, p) * GT, GT), :],
                                 xt(group(i, p), 0, GT).rearrange("p (t n) -> p t n", t=GT)).then_inc(stored, 16)
            sp.wait_ge(stored, 16 * GROUPS)

        @block.gpsimd
        def _(pool):
            pool.memset(onesb[:, :], 1.0)
            pool.memset(bqk[:, :, :], 0.0)
            pool.memset(zero[:, :], 0.0)
            pool.memset(yt[:, :], 1.0).then_inc(set_up, 1)
            pool.wait_ge(consts, 16 * 8)

            def newton(s, i, p):
                pool.wait_ge(stats, filled(at("unit", s, i, p) + 1))
                for _ in range(N_T_STEPS):
                    pool.tensor_tensor(yt[:, :], y[:, :], y[:, :], ALU.mult)
                    pool.drain()
                    pool.tensor_tensor(yt[:, :], yt[:, :], ve[:, :], ALU.mult)
                    pool.drain()
                    pool.tensor_scalar(yt[:, :], yt[:, :], -0.5, 1.5, ALU.mult, ALU.add)
                    pool.drain()
                    last = pool.tensor_tensor(y[:, :], y[:, :], yt[:, :], ALU.mult)
                    if _ < N_T_STEPS - 1:
                        pool.drain()
                last.then_inc(rstd, 1)
                pool.drain()

            def stack(s, i, p, q):
                n = PROJECTION_USE[q]
                pair = slice(2 * (q % 2), 2 * (q % 2) + 2)
                pool.wait_ge(g_done, made(at("G", s, i, p, n + 1)))
                pool.tensor_tensor(Qs[:, pair, :], qf[:, :, :], zero[:, 0:1].unsqueeze(2).broadcast_to([P, 2, C]), ALU.add)
                pool.tensor_scalar(KA[:, pair, :], kf[:, :, :], 1.0, None, ALU.mult)
                pool.drain()
                pool.tensor_scalar(Qs[:, pair, :], Qs[:, pair, :].bitcast(F32), hilos[:, 0:1], None, ALU.mult)
                pool.tensor_tensor(KB[:, pair, :], kf[:, :, :], KA[:, pair, :].bitcast(F32), ALU.subtract)
                pool.drain()
                pool.tensor_tensor(Qs[:, pair, :], Qs[:, pair, :].bitcast(F32), qf[:, :, :], ALU.add).then_inc(qk_ready, 1)

            newton(0, 0, -1)
            for s in range(len(STAGES)):
                with pool.Fori(0, GROUPS // 2) as i:
                    for p in range(2):
                        if kind(s) == "A":
                            for q in range(4):
                                stack(s, i, p, q)
                        newton(s, i, p)

        def normalise(s, i, p, first=False):
            return 0 if first else at("unit", s, i, p) + 1

        @block.scalar
        def _(act):
            act.wait_ge(consts, 16 * 8)
            act.activation(identb[:, :], identf[:, :], ACT.Copy)
            act.activation(beforeb[:, :], xh[:, 0, 0:P], ACT.Copy)
            act.activation(causalb[:, :], xh[:, 0, P:2 * P], ACT.Copy)
            act.activation(hadf[:, 1, :], hadf[:, 0, :], ACT.Copy, scale=-1.0).then_inc(cast, 1)
            act.wait_ge(set_up, 1)

            for n in range(4):
                m, jh = n // 2, n % 2
                w = fg if m == 0 else fu
                for c in range(CK):
                    k = 2 * n + c
                    act.wait_ge(u_done, made(k))
                    act.activation(w[:, 0, c, jh * 512:(jh + 1) * 512], tmp[k % 2], ACT.Copy).then_inc(w_high, 1)
            for ch in range(2):
                for j in range(FJ):
                    act.wait_ge(banded, 8 * ch + j + 1)
                    act.activation(fd[:, 0, j, ch * P:(ch + 1) * P], tmp[j % 2][:, 0:P], ACT.Copy,
                                   scale=0.25).then_inc(w_high, 1)
            split_high(act, 6)
            for m in range(2):
                act.wait_ge(u_full, 12 + m + 1)
                for c in range(CK):
                    src = U(12 + m)[:, c * C:(c + 1) * C]
                    if m == 0:
                        hi = doubled(wk, c)[0]
                        for r in range(2):
                            act.activation(hi[:, :, r, :], src.rearrange("p (h d) -> p h d", h=HEADS), ACT.Copy)\
                               .then_inc(w_high, 1)
                    else:
                        for r in range(2):
                            act.activation(wv[:, 0, c, r * P:(r + 1) * P], src[:, r * P:(r + 1) * P], ACT.Copy)\
                               .then_inc(w_high, 1)
            for n in range(8, FIRST_PIECES):
                split_high(act, n)

            def xn_highs(s, i, p, first=False):
                v = 0 if first else at("unit", s, i, p) + 1
                buf = 0 if first else (p + 1) % 2
                tn = 0 if first else static("T", s, p, {"F": 0, "A": 3, "E": 4}[kind(s)])
                act.wait_ge(xh_read, made(v * GT + GT - 1))
                act.wait_ge(xn_read, free(v))
                for c in range(CK):
                    act.activation(xnv[:, buf, 0, c, :], T(tn + c)[:, :], ACT.Copy).then_inc(xn_high, 1)

            def chunk(s, i, p, j):
                n, h = at("G", s, i, p, j), at("h", s, i, p, j)
                ns, b = static("G", s, p, j), static("h", s, p, j) % 2
                act.wait_ge(g_full, filled(n))
                act.wait_ge(h_ready, free(h))
                act.activation(sw[:, b, :], G(ns)[:, :], ACT.Silu).then_inc(g_done, 1)

            def chunk_high(s, i, p, j):
                h, b = at("h", s, i, p, j), static("h", s, p, j) % 2
                if kind(s) == "F":
                    act.wait_ge(u_done, made(at("U", s, i, p, j)))
                else:
                    act.wait_ge(weighted, filled(at("w", s, i, p, j)))
                act.wait_ge(h_read, free(h))
                act.activation(hid[:, b, 0, :], sw[:, b, :], ACT.Copy).then_inc(h_high, 1)

            def ffn(s, i, p):
                for j in range(FJ):
                    chunk(s, i, p, j)
                    chunk_high(s, i, p, j)
                    if j == 5:
                        xn_highs(s, i, p)

            def experts(s, i, p):
                act.wait_ge(t_done, made(at("T", s, i, p, 0)))
                act.activation(sg[:, :, :], lg[:, :, 0:EXPERTS], ACT.Sigmoid).then_inc(sigm, 1)
                act.wait_ge(t_full, filled(at("Tf", s, i, p, 1)))
                act.activation(sh[0:SHARED, :], T(static("T", s, p, 1))[SHARED:2 * SHARED, :], ACT.Silu)\
                   .then_inc(sh_act, 1)
                act.wait_ge(t_done, made(at("T", s, i, p, 1)))
                act.activation(shh[0:SHARED, 0, :], sh[0:SHARED, :], ACT.Copy).then_inc(sh_high, 1)
                for j in range(MJ):
                    chunk(s, i, p, j)
                    chunk_high(s, i, p, j)
                    if j == 12:
                        xn_highs(s, i, p)

            def projected(s, i, p, q):
                n = PROJECTION_USE[q]
                act.wait_ge(qk_ready, free(at("quarter", s, i, p, q)) )
                for m, dst in ((0, qf), (1, kf)):
                    act.wait_ge(g_full, filled(at("G", s, i, p, n + m)))
                    bank = S(n + m)
                    for t in range(2):
                        col = 2 * (q % 2) + t
                        ins = act.activation(dst[:, t, :], bank[:, t * C:(t + 1) * C], ACT.Identity,
                                             bias=bqk[:, m, col:col + 1])
                    ins.then_inc(g_done, 1)

            def exps(s, i, p, k):
                sc = S(score_use(k))
                b, h = k // HEADS, k % HEADS
                act.wait_ge(maxed, filled(at("head", s, i, p, k)))
                act.wait_ge(u_full, at("U", s, i, p, k) - 1)
                act.activation(Pr[:, k % 2, 0:P], sc[:, 0:P], ACT.Exp, bias=nmax[:, k % 3, 0:1],
                               accum_out=den[:, b, 0, h:h + 1])
                act.activation(Pr[:, k % 2, P:KEYS], sc[:, P:KEYS], ACT.Exp, bias=nmax[:, k % 3, 1:2],
                               accum_out=den[:, b, 1, h:h + 1]).then_inc(g_done, 1)

            def ctx_highs(s, i, p, b):
                n = (2, 5)[b]
                act.wait_ge(t_full, filled(at("Tf", s, i, p, (2, 3)[b])))
                act.activation(cT[:, 0, :, :].rearrange("p c n -> p (c n)"), T(static("T", s, p, n))[:, :],
                               ACT.Copy).then_inc(ctx_high, 1)

            def evacuate(s, i, p, k):
                act.wait_ge(u_full, filled(at("U", s, i, p, k)))
                act.wait_ge(pv_done, free(at("head", s, i, p, k)))
                act.activation(PT[:, k % 2, :], TURNED[:, 0:KEYS], ACT.Copy).then_inc(u_done, 1)

            def attention(s, i, p):
                projected(s, i, p, 0)
                if p == 1:
                    ctx_highs(s, i, 0, 1)
                projected(s, i, p, 1)
                for k in range(2 * HEADS):
                    if k == 8:
                        projected(s, i, p, 2)
                    if k == 16:
                        projected(s, i, p, 3)
                    exps(s, i, p, k)
                    if STAGES[s] == "A0" and k >= 1:
                        evacuate(s, i, p, k - 1)
                    if k == 18:
                        ctx_highs(s, i, p, 0)
                    if k == 26:
                        xn_highs(s, i, p)
                if STAGES[s] == "A0":
                    evacuate(s, i, p, 2 * HEADS - 1)
                if p == 1:
                    ctx_highs(s, i, p, 1)

            xn_highs(0, 0, 0, first=True)
            for s in range(len(STAGES)):
                if s == 3:
                    for n in range(FIRST_PIECES, len(pieces)):
                        split_high(act, n)
                if STAGES[s] == "A1":
                    act.wait_ge(auxl, 64)
                    act.activation(bqk[:, 0, :], bqk[:, 0, :], ACT.Copy, scale=0.25)
                    act.drain()
                with act.Fori(0, GROUPS // 2) as i:
                    for p in range(2):
                        {"F": ffn, "A": attention, "E": experts}[kind(s)](s, i, p)

        @block.vector
        def _(dve):
            for ring in (g_done, u_done, t_done, a_done, xh_read, xn_read, h_ready, h_read, pv_done, stage_done):
                dve.sem_inc(ring, RING)
            dve.sem_inc(qk_ready, 1)
            dve.memset(countb[:, :], 0.0)

            def scale_up(n):
                m, jh = n // 2, n % 2
                w = fg if m == 0 else fu
                for c in range(CK):
                    k = 2 * n + c
                    dve.wait_ge(u_full, k + 1)
                    if c == 0:
                        dve.wait_ge(stage_full[n % 2], stage_value(n))
                    dve.scalar_tensor_tensor(tmp[k % 2], U(k)[:, :], suc[:, c:c + 1], slot(n)[:, 1024:SLOT],
                                             ALU.mult, ALU.mult).then_inc(u_done, 1)
                    dve.wait_ge(w_high, k + 1)
                    ins = dve.tensor_tensor(w[:, 1, c, jh * 512:(jh + 1) * 512], tmp[k % 2],
                                            w[:, 0, c, jh * 512:(jh + 1) * 512].bitcast(F32), ALU.subtract)
                ins.then_inc(stage_done, 1)

            dve.wait_ge(consts, 16 * 8)
            dve.wait_ge(cast, 1)
            for n in range(4):
                scale_up(n)

            for ch in range(2):
                n = 4 + ch
                v = slot(n)
                dve.wait_ge(stage_full[n % 2], stage_value(n))
                dve.drain()
                dve.tensor_copy(tmp[1][:, 256:384], v[:, 1024:1024 + P])
                dve.drain()
                for level in BUTTERFLIES:
                    for a, b, d in level:
                        dve.tensor_tensor(v[:, d:d + P], v[:, a:a + P], v[:, b:b + P], ALU.subtract)
                    dve.drain()
                    for a, b, d in level:
                        ins = dve.tensor_tensor(v[:, a:a + P], v[:, a:a + P], v[:, b:b + P], ALU.add)
                    if level is not BUTTERFLIES[-1]:
                        dve.drain()
                ins.then_inc(weights, 1)
                for j in range(FJ):
                    bank, col = 8 + 2 * ch + j // 4, (j % 4) * P
                    if j % 4 == 0:
                        dve.wait_ge(u_full, bank + 1)
                    ins = dve.scalar_tensor_tensor(tmp[j % 2][:, 0:P], U(bank)[:, col:col + P],
                                                   suc[:, CK + j:CK + j + 1], tmp[1][:, 256:384],
                                                   ALU.mult, ALU.mult).then_inc(banded, 1)
                    dve.wait_ge(w_high, 8 + 8 * ch + j + 1)
                    ins = dve.scalar_tensor_tensor(fd[:, 1, j, ch * P:(ch + 1) * P], tmp[j % 2][:, 0:P], 0.25,
                                                   fd[:, 0, j, ch * P:(ch + 1) * P].bitcast(F32),
                                                   ALU.mult, ALU.subtract)
                    if j % 4 == 3:
                        ins.then_inc(u_done, 1)
                dve.drain()
                dve.sem_inc(stage_done, 1)
            split_low(dve, 6)
            for m in range(2):
                for c in range(CK):
                    src = U(12 + m)[:, c * C:(c + 1) * C]
                    for r in range(2):
                        dve.wait_ge(w_high, highs(7) + 4 * m + 2 * c + r + 1)
                        if c == 0 and r == 0:
                            dve.wait_ge(w_high, highs(7) + 4 * m + 4)
                        if m == 0:
                            hi, lo = doubled(wk, c)
                            ins = dve.tensor_tensor(lo[:, :, r, :], src.rearrange("p (h d) -> p h d", h=HEADS),
                                                    hi[:, :, r, :].bitcast(F32), ALU.subtract)
                        else:
                            ins = dve.tensor_tensor(wv[:, 1, c, r * P:(r + 1) * P], src[:, r * P:(r + 1) * P],
                                                    wv[:, 0, c, r * P:(r + 1) * P].bitcast(F32), ALU.subtract)
                ins.then_inc(u_done, 1)
            dve.drain()
            dve.sem_inc(stage_done, 1)
            for n in range(8, FIRST_PIECES):
                split_low(dve, n)
            dve.drain()

            def group_stats(g):
                dve.drain()
                for t in range(GT):
                    dve.bn_stats(st[:, t, :], xt(g, t))
                dve.drain()
                for t in range(GT):
                    dve.bn_aggr(mv[:, t, :], st[:, t, :])
                dve.drain()
                dve.tensor_scalar(ve[:, :], mv[:, :, 1], EPS, None, ALU.add)
                dve.drain()
                dve.tensor_scalar(y[:, :].bitcast(I32), ve[:, :].bitcast(I32), 1, None, ALU.arith_shift_right)
                dve.drain()
                dve.tensor_scalar(y[:, :].bitcast(I32), y[:, :].bitcast(I32), -1.0, float(0x5F3759DF),
                                  ALU.mult, ALU.add).then_inc(stats, 1)

            def xhats(s, i, p, first=False):
                v = 0 if first else at("unit", s, i, p) + 1
                g = 0 if first else following(i, p)
                dve.wait_ge(xh_read, v * GT + RING)
                dve.wait_ge(rstd, v + 1)
                for t in range(GT):
                    dve.tensor_scalar(xh[:, t, :], xt(g, t), mv[:, t, 0:1], y[:, t:t + 1],
                                      ALU.subtract, ALU.mult).then_inc(xh_full, 1)

            def xn_lows(s, i, p, first=False):
                v = 0 if first else at("unit", s, i, p) + 1
                buf = 0 if first else (p + 1) % 2
                tn = 0 if first else static("T", s, p, {"F": 0, "A": 3, "E": 4}[kind(s)])
                for c in range(CK):
                    dve.wait_ge(xn_high, v * CK + c + 1)
                    dve.tensor_tensor(xnv[:, buf, 1, c, :], T(tn + c)[:, :], xnv[:, buf, 0, c, :].bitcast(F32),
                                      ALU.subtract).then_inc(t_done, 1)

            def product(s, i, p, j):
                n, b = static("U", s, p, j), static("h", s, p, j) % 2
                dve.wait_ge(g_done, made(at("G", s, i, p, j)))
                dve.wait_ge(u_full, filled(at("U", s, i, p, j)))
                dve.tensor_tensor(sw[:, b, :], sw[:, b, :], U(n)[:, :], ALU.mult).then_inc(u_done, 1)

            def low(s, i, p, j):
                b = static("h", s, p, j) % 2
                dve.wait_ge(h_high, filled(at("h", s, i, p, j)))
                dve.tensor_tensor(hid[:, b, 1, :], sw[:, b, :], hid[:, b, 0, :].bitcast(F32), ALU.subtract)\
                   .then_inc(h_ready, 1)

            def residual(s, i, p, n, pair):
                if kind(s) == "A":
                    dve.wait_ge(a_full, filled(at("Af", s, i, p, pair)))
                else:
                    dve.wait_ge(h_read, made(at("h", s, i, p, USES["h"][kind(s)] - 1)))
                dve.tensor_tensor(xt(group(i, p), 2 * pair, 2), xt(group(i, p), 2 * pair, 2),
                                  A(static("A", s, p, n))[:, :], ALU.add).then_inc(a_done, 1)

            def ffn(s, i, p):
                for j in range(FJ):
                    product(s, i, p, j)
                    low(s, i, p, j)
                    if j == 0 and p == 1:
                        residual(s, i, 0, 0, 0)
                        residual(s, i, 0, 1, 1)
                    if j == 1:
                        group_stats(following(i, p))
                    if j == 3:
                        xhats(s, i, p)
                    if j == 5:
                        xn_lows(s, i, p)
                if p == 1:
                    residual(s, i, p, 0, 0)
                    residual(s, i, p, 1, 1)

            def route(s, i, p):
                dve.drain()
                dve.memset(lg[:, :, EXPERTS:EXPERTS + 2], BIG)
                dve.wait_ge(t_full, filled(at("Tf", s, i, p, 0)))
                dve.tensor_scalar(lg[:, :, 0:EXPERTS], three(T(static("T", s, p, 0))[:, 0:GT * EXPERTS], GT), 17.5, None,
                                  ALU.min).then_inc(t_done, 1)
                dve.drain()
                for t in range(GT):
                    dve.max(top[:, t, :], lg[:, t, :])
                dve.drain()
                for t in range(GT):
                    dve.match_replace(out=lr[:, t, :], in_to_replace=top[:, t, :], in_values=lg[:, t, :],
                                      imm_value=-BIG)
                dve.drain()
                dve.tensor_tensor(maskb[:, :, :], lr[:, :, 0:EXPERTS], lg[:, :, 0:EXPERTS], ALU.not_equal)\
                   .then_inc(chosen, 1)

            def share(s, i, p):
                dve.wait_ge(sh_act, filled(at("moe", s, i, p)))
                dve.tensor_tensor(sh[0:SHARED, :], sh[0:SHARED, :], T(static("T", s, p, 1))[0:SHARED, :], ALU.mult)\
                   .then_inc(t_done, 1)

            def share_low(s, i, p):
                dve.wait_ge(sh_high, filled(at("moe", s, i, p)))
                dve.tensor_tensor(shh[0:SHARED, 1, :], sh[0:SHARED, :], shh[0:SHARED, 0, :].bitcast(F32), ALU.subtract)\
                   .then_inc(sh_ready, 1)

            def weigh(s, i, p):
                dve.wait_ge(sigm, filled(at("moe", s, i, p)))
                dve.tensor_tensor(sg[:, :, :], sg[:, :, :], maskb[:, :, :], ALU.mult)
                dve.drain()
                dve.tensor_reduce(tot[:, :], sg[:, :, :], AX.X, ALU.add)
                dve.drain()
                dve.reciprocal(tot[:, :], tot[:, :])
                dve.drain()
                dve.tensor_tensor(sg[:, :, :], sg[:, :, :], tot[:, :].unsqueeze(2).broadcast_to([P, GT, EXPERTS]), ALU.mult)
                dve.drain()
                dve.wait_ge(t_full, filled(at("Tf", s, i, p, 2)))
                pos = three(T(static("T", s, p, 2))[:, 0:GT * EXPERTS], GT)
                for d in range(2):
                    ins = dve.scalar_tensor_tensor(w2[:, :, d, :], pos, float(CAP), sg[:, :, :], ALU.is_lt, ALU.mult)
                ins.then_inc(t_done, 1)
                dve.tensor_reduce(lr[:, 0, 0:EXPERTS], maskb[:, :, :].rearrange("p t e -> p e t"), AX.X, ALU.add)
                dve.drain()
                dve.tensor_tensor(countb[:, :], countb[:, :], lr[:, 0, 0:EXPERTS], ALU.add).then_inc(wmade, 1)

            def weights_across(s, i, p):
                dve.wait_ge(t_full, filled(at("Tf", s, i, p, 3)))
                dve.tensor_copy(wrep, T(static("T", s, p, 3))[:, :]).then_inc(t_done, 1)
                dve.drain()

            def experts(s, i, p):
                route(s, i, p)
                if p == 1:
                    residual(s, i, 0, 0, 0)
                    residual(s, i, 0, 1, 1)
                share(s, i, p)
                share_low(s, i, p)
                weigh(s, i, p)
                weights_across(s, i, p)
                for j in range(MJ):
                    b = static("h", s, p, j) % 2
                    product(s, i, p, j)
                    dve.wait_ge(u_done, made(at("U", s, i, p, j)))
                    dve.tensor_tensor(sw[:, b, :], sw[:, b, :], wrep, ALU.mult).then_inc(weighted, 1)
                    low(s, i, p, j)
                    if j == 6:
                        group_stats(following(i, p))
                    if j == 9:
                        xhats(s, i, p)
                    if j == 12:
                        xn_lows(s, i, p)
                if p == 1:
                    residual(s, i, p, 0, 0)
                    residual(s, i, p, 1, 1)

            def maxima(s, i, p, k):
                sc = S(score_use(k))
                dve.wait_ge(g_full, filled(at("G", s, i, p, score_use(k))))
                if STAGES[s] == "A0":
                    dve.tensor_tensor(sc[:, 0:KEYS], sc[:, 0:KEYS], aux[:, 0:KEYS], ALU.mult)
                    dve.drain()
                dve.tensor_reduce(nmax[:, k % 3, 0:1], sc[:, 0:P], AX.X, ALU.max, negate=True)
                dve.tensor_reduce(nmax[:, k % 3, 1:2], sc[:, P:KEYS], AX.X, ALU.max, negate=True).then_inc(maxed, 1)

            def evacuate(s, i, p, k):
                dve.wait_ge(u_full, filled(at("U", s, i, p, k)))
                dve.wait_ge(pv_done, free(at("head", s, i, p, k)))
                dve.tensor_copy(PT[:, k % 2, :], TURNED[:, 0:KEYS]).then_inc(u_done, 1)

            def values(s, i, p, b):
                src = three(T(static("T", s, p, b))[:, :], 2)
                dve.wait_ge(t_full, filled(at("Tf", s, i, p, b)))
                if STAGES[s] == "A0":
                    dve.tensor_copy(Vs[:, :, :], src).then_inc(t_done, 1)
                else:
                    dve.tensor_tensor(Vs[:, :, :], src, aux[:, 0:C].unsqueeze(1).broadcast_to([P, 2, C]), ALU.add)\
                       .then_inc(t_done, 1)

            def context(s, i, p, b):
                dve.wait_ge(pv_done, made(at("head", s, i, p, HEADS * b + HEADS - 1)))
                dve.reciprocal(den[:, b, :, :], den[:, b, :, :])
                dve.drain()
                dve.tensor_tensor(cn[:, :, :].rearrange("p t (h d) -> p (t h) d", h=HEADS),
                                  A(static("A", s, p, 2 * b))[:, :].rearrange("p (t d) -> p t d", d=HD),
                                  den[:, b, :, :].rearrange("p t h -> p (t h)").unsqueeze(2).broadcast_to([P, 2 * HEADS, HD]),
                                  ALU.mult).then_inc(a_done, 1)

            def ctx_lows(s, i, p, b):
                n = (2, 5)[b]
                dve.wait_ge(ctx_high, filled(at("half", s, i, p, b)))
                dve.tensor_tensor(cT[:, 1, :, :].rearrange("p c n -> p (c n)"), T(static("T", s, p, n))[:, :],
                                  cT[:, 0, :, :].rearrange("p c n -> p (c n)").bitcast(F32), ALU.subtract)\
                   .then_inc(t_done, 1)

            def output(s, i, p, b):
                if STAGES[s] == "A1":
                    pair = xt(group(i, p), 2 * b, 2)
                    dve.tensor_tensor(pair.rearrange("p (t n) -> p t n", t=2), pair.rearrange("p (t n) -> p t n", t=2),
                                      aux[:, C:2 * C].unsqueeze(1).broadcast_to([P, 2, C]), ALU.add)
                    dve.drain()
                residual(s, i, p, 2 * b + 1, b)

            def attention(s, i, p):
                if p == 1:
                    ctx_lows(s, i, 0, 1)
                values(s, i, p, 0)
                if p == 1:
                    output(s, i, 0, 1)
                maxima(s, i, p, 0)
                maxima(s, i, p, 1)
                for k in range(2 * HEADS):
                    if k + 2 < 2 * HEADS:
                        maxima(s, i, p, k + 2)
                    if STAGES[s] == "A1":
                        evacuate(s, i, p, k)
                    if k == 16:
                        context(s, i, p, 0)
                        values(s, i, p, 1)
                    if k == 18:
                        ctx_lows(s, i, p, 0)
                    if k == 20:
                        output(s, i, p, 0)
                    if k == 22:
                        group_stats(following(i, p))
                    if k == 24:
                        xhats(s, i, p)
                    if k == 26:
                        xn_lows(s, i, p)
                context(s, i, p, 1)
                if p == 1:
                    ctx_lows(s, i, p, 1)
                    output(s, i, p, 1)

            dve.wait_ge(xload, 16)
            group_stats(0)
            xhats(0, 0, 0, first=True)
            xn_lows(0, 0, 0, first=True)
            for s in range(len(STAGES)):
                if s == 3:
                    for n in range(FIRST_PIECES, len(pieces)):
                        split_low(dve, n)
                    dve.drain()
                if STAGES[s] == "A1":
                    dve.wait_ge(auxl, 64)
                if kind(s) == "E":
                    dve.drain()
                    dve.memset(countb[:, :], 0.0)
                with dve.Fori(0, GROUPS // 2) as i:
                    for p in range(2):
                        {"F": ffn, "A": attention, "E": experts}[kind(s)](s, i, p)

        @block.tensor
        def _(pe):
            pe.wait_ge(cast, 1)
            pe.wait_ge(set_up, 1)
            pe.wait_ge(consts, 16 * 8)
            for n in range(4):
                v = slot(n)
                pe.wait_ge(stage_full[n % 2], stage_value(n))
                for a in range(CK):
                    pe.wait_ge(u_done, free(2 * n + a))
                    for b in range(CK):
                        mm = pe.matmul(U(2 * n + a)[:, :], hadf[:, a & b, :], v[:, b * 512:(b + 1) * 512],
                                       start=(b == 0), stop=(b == CK - 1))
                    mm.then_inc(u_full, 1)
            for ch in range(2):
                v = slot(4 + ch)
                pe.wait_ge(weights, ch + 1)
                for half in range(2):
                    pe.wait_ge(u_done, free(8 + 2 * ch + half))
                    for q in range(4):
                        at_col = CHUNK_AT[4 * half + q]
                        mm = pe.matmul(U(8 + 2 * ch + half)[:, q * P:(q + 1) * P], hadf[:, 0, :],
                                       v[:, at_col:at_col + P], start=True, stop=True)
                    mm.then_inc(u_full, 1)
            v = slot(7)
            pe.wait_ge(stage_full[1], stage_value(7))
            for m in range(2):
                pe.wait_ge(u_done, free(12 + m))
                for c in range(CK):
                    mm = pe.matmul(U(12 + m)[:, c * C:(c + 1) * C], v[0:LATENT, m * C + c * P:m * C + (c + 1) * P],
                                   v[0:LATENT, (2 + m) * C:(3 + m) * C], start=True, stop=True)
                mm.then_inc(u_full, 1)

            def transposes(s, i, p, first=False):
                v = 0 if first else at("unit", s, i, p) + 1
                n = 0 if first else {"F": 0, "A": 3, "E": 4}[kind(s)]
                ti = 0 if first else at("T", s, i, p, n)
                tn = 0 if first else static("T", s, p, n)
                pe.wait_ge(t_done, free(ti + 1))
                for t in range(GT):
                    pe.wait_ge(xh_full, v * GT + t + 1)
                    for c in range(CK):
                        mm = pe.transpose(T(tn + c)[:, t * P:(t + 1) * P], xh[:, t, c * P:(c + 1) * P], identf[:, :])
                    mm.then_inc(xh_read, 1)

            def xn_ready(s, i, p):
                last = 1 if kind(s) == "A" and p == 1 else 0
                pe.wait_ge(t_done, made(at("T", s, i, p) - 1 - last))

            PASSES = ((0, 0), (1, 0), (0, 1))

            def up(bank, w, c_of, rhs, n):
                k = 0
                for c in range(CK):
                    for a, b in PASSES:
                        mm = pe.matmul(bank, c_of(w, a, c), rhs(b, c), start=(k == 0), stop=(k == 3 * CK - 1))
                        k += 1
                return mm

            def down(bank_of, src_of, w_of, first, last, before_low=None):
                for a, b in ((0, 0), (0, 1), (1, 0)):
                    if a == 1 and before_low is not None:
                        before_low()
                    for t in range(GT):
                        mm = pe.matmul(bank_of(t // 2)[:, (t % 2) * C:(t % 2 + 1) * C], src_of(a, t), w_of(b),
                                       start=(first and a == 0 and b == 0 and t % 2 == 0),
                                       stop=(last and a == 1), skip_group_check=True)
                        yield mm

            def ups(s, i, p, j, gate, upw):
                buf = p
                rhs = lambda b, c: xnv[:, buf, b, c, :]
                pe.wait_ge(g_done, free(at("G", s, i, p, j)))
                up(G(static("G", s, p, j))[:, :], gate, lambda w, a, c: w[:, a, c, j * P:(j + 1) * P], rhs, 0)\
                    .then_inc(g_full, 1)
                pe.wait_ge(u_done, free(at("U", s, i, p, j)))
                up(U(static("U", s, p, j))[:, :], upw, lambda w, a, c: w[:, a, c, j * P:(j + 1) * P], rhs, 0)\
                    .then_inc(u_full, 1)

            def downs(s, i, p, j, w, first, last):
                b = static("h", s, p, j) % 2
                h = at("h", s, i, p, j)
                n = static("A", s, p)
                if first:
                    pe.wait_ge(a_done, free(at("A", s, i, p, 1)))
                pe.wait_ge(h_high, filled(h))
                k = 0
                for mm in down(lambda pair: A(n + pair), lambda a, t: hid[:, b, a, t * P:(t + 1) * P],
                               lambda part: w[:, part, j, :], first, last,
                               lambda: pe.wait_ge(h_ready, made(h))):
                    k += 1
                    if last and k == 1:
                        mm.then_inc(xn_read, 1)
                mm.then_inc(h_read, 1)

            def ffn(s, i, p):
                xn_ready(s, i, p)
                for j in range(FJ):
                    ups(s, i, p, j, fg, fu)
                    if j == 0 and p == 1:
                        downs(s, i, 0, FJ - 1, fd, False, True)
                    if j >= 1:
                        downs(s, i, p, j - 1, fd, j == 1, False)
                    if j == 5:
                        transposes(s, i, p)
                if p == 1:
                    downs(s, i, p, FJ - 1, fd, False, True)

            def experts(s, i, p):
                xn_ready(s, i, p)
                pe.wait_ge(t_done, free(at("T", s, i, p, 0)))
                for t in range(GT):
                    k = 0
                    for c in range(CK):
                        for a, b in PASSES:
                            mm = pe.matmul(T(static("T", s, p, 0))[:, t * EXPERTS:(t + 1) * EXPERTS],
                                           xnv[:, p, a, c, t * P:(t + 1) * P], mg[:, b, c, :],
                                           start=(k == 0), stop=(k == 3 * CK - 1))
                            k += 1
                mm.then_inc(t_full, 1)
                pe.wait_ge(t_done, free(at("T", s, i, p, 1)))
                up(T(static("T", s, p, 1))[:, :], shu, lambda w, a, c: w[:, a, c, :], lambda b, c: xnv[:, p, b, c, :], 0)\
                    .then_inc(t_full, 1)
                mj = lambda w, a, c, v, j: w[:, a, c, v, j, :]

                def ups_m(j):
                    rhs = lambda b, c: xnv[:, p, b, c, :]
                    pe.wait_ge(g_done, free(at("G", s, i, p, j)))
                    up(G(static("G", s, p, j))[:, :], mw, lambda w, a, c: w[:, a, c, 0, j, :], rhs, 0).then_inc(g_full, 1)
                    pe.wait_ge(u_done, free(at("U", s, i, p, j)))
                    up(U(static("U", s, p, j))[:, :], mw, lambda w, a, c: w[:, a, c, 1, j, :], rhs, 0).then_inc(u_full, 1)

                if p == 1:
                    downs(s, i, 0, MJ - 1, md, False, True)
                ups_m(0)
                pe.wait_ge(t_done, free(at("T", s, i, p, 2)))
                pe.wait_ge(chosen, filled(at("moe", s, i, p)))
                for t in range(GT):
                    dst = T(static("T", s, p, 2))[:, t * EXPERTS:(t + 1) * EXPERTS]
                    pe.matmul(dst, onesb[:, :], countb[:, :], start=True, stop=False)
                    for r in range(t):
                        pe.matmul(dst, onesb[:, :], maskb[:, r, :], start=False, stop=False)
                    mm = pe.matmul(dst, beforeb[:, :], maskb[:, t, :], start=False, stop=True)
                mm.then_inc(t_full, 1)
                ups_m(1)
                pe.wait_ge(t_done, free(at("T", s, i, p, 3)))
                pe.wait_ge(wmade, filled(at("moe", s, i, p)))
                for t in range(GT):
                    mm = pe.transpose(T(static("T", s, p, 3))[:, t * P:(t + 1) * P],
                                      w2[:, t, :, :].rearrange("p d e -> p (d e)"), identf[:, :])
                mm.then_inc(t_full, 1)
                n = static("A", s, p)
                pe.wait_ge(a_done, free(at("A", s, i, p, 1)))
                pe.wait_ge(sh_ready, filled(at("moe", s, i, p)))
                for mm in down(lambda pair: A(n + pair), lambda a, t: shh[0:SHARED, a, t * P:(t + 1) * P],
                               lambda part: shd[0:SHARED, part, :], True, False):
                    pass
                for j in range(MJ):
                    if j >= 2:
                        ups_m(j)
                    if j >= 1:
                        downs(s, i, p, j - 1, md, False, False)
                    if j == 12:
                        transposes(s, i, p)
                if p == 1:
                    downs(s, i, p, MJ - 1, md, False, True)

            def project(s, i, p, q):
                n, b = PROJECTION_USE[q], q // 2
                for m, w in ((0, wq), (1, wk)):
                    pe.wait_ge(g_done, score_free(s, i, p, n + m))
                    for t in range(2):
                        col = 2 * (q % 2) + t
                        mm = up(S(n + m)[:, t * C:(t + 1) * C], w,
                                lambda w_, a, c: w_[:, a, c, col * P:(col + 1) * P],
                                lambda r, c: xnv[:, p, r, c, b * BATCH:(b + 1) * BATCH], 0)
                    mm.then_inc(g_full, 1)

            def values(s, i, p, b):
                pe.wait_ge(t_done, free(at("T", s, i, p, b)))
                for t in range(2):
                    k = 0
                    for c in range(CK):
                        for a, r in PASSES:
                            lo = b * BATCH + t * P
                            mm = pe.matmul(T(static("T", s, p, b))[:, t * C:(t + 1) * C], xnv[:, p, a, c, lo:lo + P],
                                           wv[:, r, c, :], start=(k == 0), stop=(k == 3 * CK - 1))
                            k += 1
                mm.then_inc(t_full, 1)

            def scores(s, i, p, k):
                n = score_use(k)
                h = k % HEADS
                t, rows = h // 4, slice(32 * (h % 4), 32 * (h % 4) + 32)
                bank = S(n)
                pe.wait_ge(g_done, score_free(s, i, p, n))
                if k % 8 == 0:
                    pe.wait_ge(qk_ready, at("quarter", s, i, p, k // 8) + 2)
                queries = [Qs[rows, t, q * P:(q + 1) * P] for q in range(2)]
                pe.matmul(bank[:, 0:P], queries[0], KA[rows, t, 0:P], start=True, stop=False, skip_group_check=True)
                pe.matmul(bank[:, P:KEYS], queries[1], KA[rows, t, :], start=False, stop=False, skip_group_check=True)
                diagonals = bank[:, 0:2 * BATCH].rearrange("p (a n) -> p a n", a=2)[:, :, 0:P]
                pe.matmul(diagonals, identb[:, :], causalb[:, :].unsqueeze(1).broadcast_to([P, 2, P]), start=False,
                          stop=False, skip_group_check=True)
                pe.matmul(bank[:, 0:P], queries[0], KB[rows, t, 0:P], start=False, stop=True, skip_group_check=True)
                pe.matmul(bank[:, P:KEYS], queries[1], KB[rows, t, :], start=False, stop=True, skip_group_check=True)\
                    .then_inc(g_full, 1)

            def turn(s, i, p, k):
                pe.wait_ge(g_done, made(at("G", s, i, p, score_use(k))))
                pe.wait_ge(u_done, at("U", s, i, p, k) + RING)
                for c in range(3):
                    mm = pe.transpose(TURNED[:, c * P:(c + 1) * P], Pr[:, k % 2, c * P:(c + 1) * P], identf[:, :])
                mm.then_inc(u_full, 1)

            def mix(s, i, p, k):
                b, h = k // HEADS, k % HEADS
                bank = A(static("A", s, p, 2 * b))
                if h == 0:
                    pe.wait_ge(a_done, free(at("A", s, i, p, 2 * b)))
                    pe.wait_ge(t_done, made(at("T", s, i, p, b)))
                pe.wait_ge(u_done, made(at("U", s, i, p, k)))
                cols = slice(h * HD, (h + 1) * HD)
                pe.matmul(bank[:, h * HD:(h + 1) * HD], PT[:, k % 2, 0:P], Vs[:, 0, cols], start=True, stop=True)
                pe.matmul(bank[:, C + h * HD:C + (h + 1) * HD], PT[:, k % 2, P:2 * P], Vs[:, 0, cols],
                          start=True, stop=False)
                pe.matmul(bank[:, C + h * HD:C + (h + 1) * HD], PT[:, k % 2, 2 * P:KEYS], Vs[:, 1, cols],
                          start=False, stop=True).then_inc(pv_done, 1)

            def turn_context(s, i, p, b):
                n = (2, 5)[b]
                pe.wait_ge(a_done, made(at("A", s, i, p, 2 * b)))
                pe.wait_ge(t_done, free(at("T", s, i, p, n)))
                for c in range(CK):
                    for t in range(2):
                        lo = c * BATCH + t * P
                        mm = pe.transpose(T(static("T", s, p, n))[:, lo:lo + P], cn[:, t, c * P:(c + 1) * P], identf[:, :])
                mm.then_inc(t_full, 1)

            def project_out(s, i, p, b, last):
                n = 2 * b + 1
                pe.wait_ge(t_done, made(at("T", s, i, p, (2, 5)[b])))
                pe.wait_ge(a_done, free(at("A", s, i, p, n)))
                for t in range(2):
                    k = 0
                    for c in range(CK):
                        for a, r in PASSES:
                            mm = pe.matmul(A(static("A", s, p, n))[:, t * C:(t + 1) * C], cT[:, a, c, t * P:(t + 1) * P],
                                           wo[:, r, c, :], start=(k == 0), stop=(k == 3 * CK - 1))
                            if last and t == 0 and k == 0:
                                mm.then_inc(xn_read, 1)
                            k += 1
                mm.then_inc(a_full, 1)

            def attention(s, i, p):
                xn_ready(s, i, p)
                project(s, i, p, 0)
                if p == 1:
                    turn_context(s, i, 0, 1)
                values(s, i, p, 0)
                project(s, i, p, 1)
                if p == 1:
                    project_out(s, i, 0, 1, True)
                scores(s, i, p, 0)
                scores(s, i, p, 1)
                for k in range(2 * HEADS):
                    if k + 2 == 8:
                        project(s, i, p, 2)
                    if k + 2 == 16:
                        project(s, i, p, 3)
                    if k + 2 < 2 * HEADS:
                        scores(s, i, p, k + 2)
                    turn(s, i, p, k)
                    if k >= 1:
                        mix(s, i, p, k - 1)
                    if k == 16:
                        values(s, i, p, 1)
                    if k == 18:
                        turn_context(s, i, p, 0)
                    if k == 20:
                        project_out(s, i, p, 0, False)
                    if k == 26:
                        transposes(s, i, p)
                mix(s, i, p, 2 * HEADS - 1)
                if p == 1:
                    turn_context(s, i, p, 1)
                    project_out(s, i, p, 1, True)

            transposes(0, 0, 0, first=True)
            for s in range(len(STAGES)):
                if s == 0:
                    pe.wait_ge(stage_done, FIRST_PIECES + RING)
                if s == 3:
                    pe.wait_ge(stage_done, len(pieces) + RING)
                with pe.Fori(0, GROUPS // 2) as i:
                    for p in range(2):
                        {"F": ffn, "A": attention, "E": experts}[kind(s)](s, i, p)


def kernel(**inputs):
    import numpy as np
    import concourse.bacc as bacc
    from concourse.bass_utils import run_bass_kernel_spmd as run

    g = {k: np.asarray(v) for k, v in inputs.items()}

    def stacked(b):
        return np.repeat(b.reshape(4, 4, 1, HD), 2, axis=2).reshape(4, P).T

    up = g["L1_ffn_w_up"].reshape(EXPERTS, C, 2, MJ, 2).transpose(1, 2, 3, 4, 0).reshape(C, 2 * MJ * P)
    down = g["L1_ffn_w_down"].reshape(EXPERTS, MJ, 2, C).transpose(1, 2, 0, 3).reshape(MJ * P, C)

    n = np.arange(P)
    bits = np.array([[bin(a & b).count("1") % 2 for b in range(P)] for a in range(P)])
    had = np.where(bits == 1, -1.0, 1.0) / np.sqrt(C)
    query, key = n[:, None], n[None, :]
    diagonal = np.where(np.abs(query - key) < WINDOW, 1.0 + ALPHA, 1.0)
    below = np.where(query + P - key < WINDOW, 1.0 + ALPHA, 1.0)
    f = np.float32
    arrays = {
        "x": g["L0_attn_hidden_states"].reshape(TOKENS, C),
        "fgate": g["L0_ffn_W_gate"].T, "fup": g["L0_ffn_W_up"].T, "fdown": g["L0_ffn_W_down"].T,
        "su_ug": g["L0_ffn_SU_ug"].reshape(CK, P).T, "su_dp": g["L0_ffn_SU_dp"].reshape(FJ, P).T,
        "ws_ug": np.concatenate([g["L0_ffn_Wscale_ug"][INTER:], g["L0_ffn_Wscale_ug"][:INTER]]),
        "ws_dp": g["L0_ffn_Wscale_dp"],
        "q0": g["L0_attn_w_q"].T, "o0": g["L0_attn_w_out"].T,
        "kd0": g["L0_attn_w_k_down"], "vd0": g["L0_attn_w_v_down"],
        "ql0": g["L0_attn_q_to_latent"].transpose(2, 0, 1).reshape(LATENT, C),
        "vu0": g["L0_attn_v_up"].transpose(1, 0, 2).reshape(LATENT, C),
        "q1": g["L1_attn_wq"].T, "k1": g["L1_attn_wk"].T, "v1": g["L1_attn_wv"].T, "o1": g["L1_attn_wo"].T,
        "bq": stacked(g["L1_attn_bq"]), "bk": stacked(g["L1_attn_bk"]), "bv": g["L1_attn_bv"], "bo": g["L1_attn_bo"],
        "mgate": g["L1_ffn_w_gate"], "mshup": g["L1_ffn_w_shared_up"], "mshdown": g["L1_ffn_w_shared_down"],
        "mup": up, "mdown": down,
        "had": had.astype(f), "ident": np.eye(P, dtype=f),
        "before": (query < key).astype(f),
        "bandm": np.concatenate([diagonal, below, diagonal], axis=1).astype(f),
        "causal": np.where(key > query, -1e30, 0.0).astype(f),
        "hilo": np.where(n % 32 < HD, 0.0, -1.0).reshape(P, 1).astype(f),
    }
    nc = bacc.Bacc("TRN2", target_bir_lowering=False, num_devices=1)
    feeds, args = {}, {}
    for name, a in arrays.items():
        a = np.ascontiguousarray(a)
        feeds[name + "_dram"] = a
        args[name] = nc.dram_tensor(name + "_dram", a.shape, mybir.dt.from_np(a.dtype), kind="ExternalInput").ap()
    out = nc.dram_tensor("out_dram", (TOKENS, C), mybir.dt.float32, kind="ExternalOutput").ap()
    build(nc, **args, out=out)
    got = run(nc, [feeds], core_ids=[0]).results[0]["out_dram"]
    return np.asarray(got).reshape(TOKENS // BATCH, BATCH, C)
```

```python
import concourse.bass as bass
from concourse import mybir
from contextlib import ExitStack

TOKENS, C = 2048, 256
BATCH = 256
INTER = 1024
HEADS, HD = 16, 16
LATENT = 64
EXPERTS, EH, CAP, TOPK = 64, 32, 128, 6
SHARED = 64
WINDOW, ALPHA = 64, 0.5
EPS = 1e-5

P = 128
CK = C // P
TILES = TOKENS // P
GROUP = 512
GT = GROUP // P
GROUPS = TOKENS // GROUP
FJ = INTER // P
MJ = EXPERTS * EH // P
KEYS = 3 * P
BIG = 3.0e38

STAGES = ["F", "A0", "F", "E", "A1", "E"]

USES = {
    "G": {"F": FJ, "A": 4 * 2 + 2 * HEADS, "E": MJ},
    "U": {"F": FJ, "A": 2 * HEADS, "E": MJ},
    "T": {"F": 2, "A": 6, "E": 6},
    "Tf": {"F": 0, "A": 4, "E": 4},
    "A": {"F": 2, "A": 4, "E": 2},
    "h": {"F": FJ, "A": 0, "E": MJ},
    "w": {"F": 0, "A": 0, "E": MJ},
    "head": {"F": 0, "A": 2 * HEADS, "E": 0},
    "quarter": {"F": 0, "A": 4, "E": 0},
    "half": {"F": 0, "A": 2, "E": 0},
    "moe": {"F": 0, "A": 0, "E": 1},
    "unit": {"F": 1, "A": 1, "E": 1},
    "Af": {"F": 0, "A": 2, "E": 0},
}
BEFORE = {"U": 14, "T": 2}
N_T_STEPS = 3


def butterflies():
    where, spare, levels = [P * j for j in range(FJ)], [P * (FJ + j) for j in range(FJ // 2)], []
    for step in (1, 2, 4):
        level, freed = [], []
        for q, (a, b) in enumerate((a, a + step) for a in range(FJ) if not a & step):
            level.append((where[a], where[b], spare[q]))
            freed.append(where[b])
            where[b] = spare[q]
        levels.append(level)
        spare = freed
    return levels, where


BUTTERFLIES, CHUNK_AT = butterflies()


def build(nc, x, fgate, fup, fdown, su_ug, su_dp, ws_ug, ws_dp, q0, o0, kd0, vd0, ql0, vu0,
          q1, k1, v1, o1, bq, bk, bv, bo, mgate, mshup, mshdown, mup, mdown,
          had, ident, before, bandm, causal, hilo, out):
    F32, R32, BF16 = mybir.dt.float32, mybir.dt.float32r, mybir.dt.bfloat16
    I32 = mybir.dt.int32
    ALU, ACT, AX = mybir.AluOpType, mybir.ActivationFunctionType, mybir.AxisListType

    ctx = ExitStack()
    with ctx:
        def sb(name, shape, dt=F32):
            return ctx.enter_context(nc.sbuf_tensor(name, shape, dt))

        def sem(name):
            return ctx.enter_context(nc.semaphore(name))

        xs = sb("xs", [P, TILES * C])
        WA = sb("WA", [P, 12288], R32)
        WM = sb("WM", [P, 4 * MJ * P * CK], R32)
        WT = sb("WT", [P, 6144], R32)
        xn = sb("xn", [P, 2 * 2 * CK * GROUP], R32)
        WR = sb("WR", [P, 4096], R32)
        WF = sb("WF", [P, 3584])
        xh = sb("xh", [P, GT, C])
        aux = sb("aux", [P, 2 * C])
        identf = sb("identf", [P, P])
        hadf = xh[:, 2, :].rearrange("p (s n) -> p s n", s=2)
        identb = sb("identb", [P, P], BF16)
        beforeb = sb("beforeb", [P, P], BF16)
        onesb = sb("onesb", [P, P], BF16)
        causalb = sb("causalb", [P, P], BF16)
        countb = sb("countb", [P, EXPERTS], BF16)
        maskb = sb("maskb", [P, GT, EXPERTS], BF16)
        zero = sb("zero", [P, 1])
        hilos = sb("hilos", [P, 1])
        suc = sb("suc", [P, CK + FJ])
        bqk = sb("bqk", [P, 2, 4])
        st = sb("st", [P, GT, 6])
        mv = sb("mv", [P, GT, 2])
        ve = sb("ve", [P, GT])
        y = sb("y", [P, GT])
        yt = sb("yt", [P, GT])
        nmax = sb("nmax", [P, 3, 2])
        den = sb("den", [P, 2, 2, HEADS])
        top = sb("top", [P, GT, 8])
        tot = sb("tot", [P, GT])

        fg = WA[:, 0:4096].rearrange("p (s c n) -> p s c n", s=2, c=CK)
        fu = WA[:, 4096:8192].rearrange("p (s c n) -> p s c n", s=2, c=CK)
        fd = WA[:, 8192:12288].rearrange("p (s j n) -> p s j n", s=2, j=FJ)
        md = WA[:, 0:8192].rearrange("p (s j n) -> p s j n", s=2, j=MJ)
        shu = WA[:, 8192:8704].rearrange("p (s c n) -> p s c n", s=2, c=CK)
        mg = WA[:, 8704:8960].rearrange("p (s c n) -> p s c n", s=2, c=CK)
        shd = WA[:, 8960:9472].rearrange("p (s n) -> p s n", s=2)
        mw = WM[:, :].rearrange("p (s c v j n) -> p s c v j n", s=2, c=CK, v=2, j=MJ)
        wq = WT[:, 0:2048].rearrange("p (s c n) -> p s c n", s=2, c=CK)
        wk = WT[:, 2048:4096].rearrange("p (s c n) -> p s c n", s=2, c=CK)
        wv = WT[:, 4096:5120].rearrange("p (s c n) -> p s c n", s=2, c=CK)
        wo = WT[:, 5120:6144].rearrange("p (s c n) -> p s c n", s=2, c=CK)
        xnv = xn[:, :].rearrange("p (b s c n) -> p b s c n", b=2, s=2, c=CK)
        hid = WR[:, 0:2048].rearrange("p (b s n) -> p b s n", b=2, s=2)
        shh = WR[:, 2048:3072].rearrange("p (s n) -> p s n", s=2)
        Qs = WR[:, 0:1024].rearrange("p (t n) -> p t n", t=4)
        KA = WR[:, 1024:2048].rearrange("p (t n) -> p t n", t=4)
        KB = WR[:, 2048:3072].rearrange("p (t n) -> p t n", t=4)
        cT = WR[:, 3072:4096].rearrange("p (s c n) -> p s c n", s=2, c=CK)
        sw = WF[:, 0:1024].rearrange("p (b n) -> p b n", b=2)
        wrep = WF[:, 1024:1536]
        sh = WF[:, 1536:2048]
        w2 = WF[:, 2048:2560].rearrange("p (t d e) -> p t d e", t=GT, d=2)
        lg = WF[:, 2560:2824].rearrange("p (t e) -> p t e", t=GT)
        lr = WF[:, 2824:3088].rearrange("p (t e) -> p t e", t=GT)
        sg = WF[:, 3088:3344].rearrange("p (t e) -> p t e", t=GT)
        Vs = WF[:, 0:1024].rearrange("p (t h n) -> p t h n", t=2, h=HEADS)
        Pr = WF[:, 1024:1792].rearrange("p (b n) -> p b n", b=2)
        PT = WF[:, 1792:2560].rearrange("p (b n) -> p b n", b=2)
        cn = xh[:, 0:2, :]
        sums = xh[:, 2:4, :].rearrange("p t n -> p (t n)")
        qf = WF[:, 2560:3072].rearrange("p (t n) -> p t n", t=2)
        kf = WF[:, 3072:3584].rearrange("p (t n) -> p t n", t=2)
        SLOT = 1536
        tmp = [WF[:, 3072:3584], xh[:, 0:2, :].rearrange("p a n -> p (a n)")]

        banks = [ctx.enter_context(nc.psum_tensor(f"bank{n}", [P, 512], F32)) for n in range(8)]

        def G(n): return banks[n % 2]
        def U(n): return banks[2 + n % 2]
        def T(n): return banks[4 + n % 2]
        def A(n): return banks[6 + n % 2]

        def S(n): return banks[(0, 1, 3)[n % 3]]
        TURNED = banks[2]

        AHEAD = 2
        PARTS_BEFORE = {0: [(0, 0), (1, 0)], 1: [(0, 1)], 2: [(1, 1)], 9: [(0, 2)], 10: [(1, 2)], 17: [(0, 3)], 18: [(1, 3)],
                        26: [(0, 4)], 27: [(1, 4)], 33: [(0, 5)], 34: [(1, 5)], 41: [(0, 6)], 42: [(1, 6)],
                        49: [(0, 7)], 50: [(1, 7)]}
        ORDER = []
        for k in range(4 * HEADS):
            ORDER += PARTS_BEFORE.get(k, []) + [k]
        VALUES_T, CONTEXT_T, NORM_T = (0, 3, 5, 9), (4, 6, 10, 11), (1, 7)
        VALUES_TF, CONTEXT_TF = (0, 1, 3, 5), (2, 4, 6, 7)

        def score_use(item):
            return ORDER.index(item)

        consts = sem("consts")
        xload = sem("xload")
        set_up = sem("set_up")
        cast = sem("cast")
        stage_full = [sem("stage_full0"), sem("stage_full1")]
        stage_done = sem("stage_done")
        w_high = sem("w_high")
        weights = sem("weights")
        g_full, g_done = sem("g_full"), sem("g_done")
        u_full, u_done = sem("u_full"), sem("u_done")
        t_full, t_done = sem("t_full"), sem("t_done")
        a_full, a_done = sem("a_full"), sem("a_done")
        stats = sem("stats")
        rstd = sem("rstd")
        xh_full, xh_read = sem("xh_full"), sem("xh_read")
        xn_high = sem("xn_high")
        xn_read = sem("xn_read")
        h_high = sem("h_high")
        h_ready = sem("h_ready")
        h_read = sem("h_read")
        weighted = sem("weighted")
        chosen = sem("chosen")
        sigm = sem("sigm")
        wmade = sem("wmade")
        sh_act, sh_high, sh_ready = sem("sh_act"), sem("sh_high"), sem("sh_ready")
        q_ready, k_ready = sem("q_ready"), sem("k_ready")
        maxed = sem("maxed")
        pv_done = sem("pv_done")
        shared = sem("shared")
        ctx_made = sem("ctx_made")
        ctx_high = sem("ctx_high")
        stored = sem("stored")
        banded = sem("banded")
        auxl = sem("auxl")

        RING = 2

        def kind(s):
            return STAGES[s][0]

        def base(what, s):
            return BEFORE.get(what, 0) + GROUPS * sum(USES[what][kind(r)] for r in range(s))

        def at(what, s, i, p, n=0):
            per = USES[what][kind(s)]
            return i * (2 * per) + (base(what, s) + p * per + n)

        def static(what, s, p, n=0):
            return base(what, s) + p * USES[what][kind(s)] + n

        def filled(index, k=1):
            return index + k

        def free(index):
            return index + 1

        def made(index):
            return index + 1 + RING

        def score_free(s, i, n):
            return at("G", s, i, 0, max(0, n - 3 + 1)) + RING

        def norm_use(s, p):
            return {"F": (p, 0), "A": (0, NORM_T[p]), "E": (p, 4)}[kind(s)]

        def group(i, p):
            return i * 2 + p

        def following(i, p):
            return i * 2 + 1 if p == 0 else 2 - i * 2

        def xt(g, t, n=1):
            return xs[:, bass.ds(g * (GT * C) + t * C, n * C)]

        block = ctx.enter_context(nc.Block())

        def spread(src, lo, n):
            return src[lo:lo + n].partition_broadcast(P)

        pieces = []
        for m, w in ((0, fgate), (1, fup)):
            for jh in range(2):
                pieces.append([(0, 1024, P, w.rearrange("(c p) n -> p c n", p=P)[:, :, jh * 512:(jh + 1) * 512]),
                               (1024, 512, P, spread(ws_ug, m * INTER + jh * 512, 512))])
        for ch in range(2):
            pieces.append([(0, 1024, P, fdown.rearrange("(j p) n -> p j n", p=P)[:, :, ch * P:(ch + 1) * P]),
                           (1024, P, P, spread(ws_dp, ch * P, P))])
        pieces.append([(0, 512, P, q0.rearrange("(c p) n -> p c n", p=P)),
                       (512, 512, P, o0.rearrange("(c p) n -> p c n", p=P))])
        pieces.append([(k * C, C, LATENT, w) for k, w in enumerate((kd0, vd0, ql0, vu0))])
        mupv = mup.rearrange("(c p) n -> p c n", p=P)
        for c in range(CK):
            for k in range(4):
                pieces.append([(0, 1024, P, mupv[:, c, k * 1024:(k + 1) * 1024])])
        FIRST_PIECES = len(pieces)
        pieces.append([(0, 512, P, q1.rearrange("(c p) n -> p c n", p=P)), (512, 512, P, k1.rearrange("(c p) n -> p c n", p=P))])
        pieces.append([(0, 512, P, v1.rearrange("(c p) n -> p c n", p=P)), (512, 512, P, o1.rearrange("(c p) n -> p c n", p=P))])
        mdv = mdown.rearrange("(j p) n -> p j n", p=P)
        for k in range(4):
            pieces.append([(0, 1024, P, mdv[:, 4 * k:4 * k + 4, :])])
        pieces.append([(0, 256, P, mshup.rearrange("(c p) n -> p c n", p=P)),
                       (256, 128, P, mgate.rearrange("(c p) n -> p c n", p=P)),
                       (384, 256, SHARED, mshdown)])

        def slot(n):
            return WF[:, (n % 2) * SLOT:(n % 2 + 1) * SLOT]

        def stage_value(n):
            return 16 * sum(len(pieces[m]) for m in range(n % 2, n + 1, 2))

        def load_pieces(eng, first, last):
            for n in range(first, last):
                eng.wait_ge(stage_done, free(n))
                for lo, w, parts, src in pieces[n]:
                    dst = slot(n)[0:parts, lo:lo + w]
                    if len(src.shape) == 3:
                        dst = dst.rearrange("p (a n) -> p a n", a=src.shape[1])
                    eng.dma_start(dst, src).then_inc(stage_full[n % 2], 16)

        def three(v, a):
            return v.rearrange("p (a n) -> p a n", a=a)

        def doubled(w, c):
            return [w[:, s, c, :].rearrange("p (h r d) -> p h r d", h=HEADS, r=2) for s in range(2)]

        def splits(n):
            v = slot(n)
            if n == 6 or n == FIRST_PIECES or n == FIRST_PIECES + 1:
                todo = []
                mats = {6: (("q", 0.125), ("o", 1.0)), FIRST_PIECES: (("q", 0.25), ("k", 1.0)),
                        FIRST_PIECES + 1: (("v", 1.0), ("o", 1.0))}[n]
                for m, (name, scale) in enumerate(mats):
                    src = v[:, m * 512:(m + 1) * 512]
                    if name in "qk":
                        w = wq if name == "q" else wk
                        for c in range(CK):
                            sv = src[:, c * C:(c + 1) * C].rearrange("p (h d) -> p h d", h=HEADS)
                            hi, lo = doubled(w, c)
                            for r in range(2):
                                todo.append((sv, hi[:, :, r, :], lo[:, :, r, :], scale))
                    else:
                        w = wv if name == "v" else wo
                        todo.append((three(src, CK), w[:, 0, :, :], w[:, 1, :, :], scale))
                return todo
            if 8 <= n < FIRST_PIECES:
                c, k = (n - 8) // 4, (n - 8) % 4
                hi, lo = (mw[:, s, c, k // 2, (k % 2) * 8:(k % 2) * 8 + 8, :].rearrange("p j n -> p (j n)") for s in range(2))
                return [(v[:, 0:1024], hi, lo, 1.0)]
            if n < FIRST_PIECES + 6:
                k = n - FIRST_PIECES - 2
                hi, lo = (md[:, s, 4 * k:4 * k + 4, :].rearrange("p j n -> p (j n)") for s in range(2))
                return [(v[:, 0:1024], hi, lo, 0.5)]
            return [(three(v[:, 0:256], CK), shu[:, 0, :, :], shu[:, 1, :, :], 1.0),
                    (three(v[:, 256:384], CK), mg[:, 0, :, :], mg[:, 1, :, :], 1.0),
                    (v[0:SHARED, 384:640], shd[0:SHARED, 0, :], shd[0:SHARED, 1, :], 0.5)]

        DERIVED = [2, 2, 2, 2, 8, 8, None, 8]

        def highs(n):
            return sum((DERIVED[m] if m < 8 and m != 6 else len(splits(m))) for m in range(n))

        def split_high(eng, n):
            eng.wait_ge(stage_full[n % 2], stage_value(n))
            for src, hi, lo, scale in splits(n):
                eng.activation(hi, src, ACT.Copy, scale=scale).then_inc(w_high, 1)

        def split_low(eng, n):
            todo = splits(n)
            for k, (src, hi, lo, scale) in enumerate(todo):
                eng.wait_ge(w_high, highs(n) + k + 1)
                ins = eng.scalar_tensor_tensor(lo, src, scale, hi.bitcast(F32), ALU.mult, ALU.subtract)
            ins.then_inc(stage_done, 1)

        @block.sync
        def _(sp):
            sp.dma_start(identf[:, :], ident).then_inc(consts, 16)
            sp.dma_start(hadf[:, 0, :], had).then_inc(consts, 16)
            sp.dma_start(aux[:, 0:KEYS], bandm).then_inc(consts, 16)
            sp.dma_start(hilos[:, :], hilo).then_inc(consts, 16)
            sp.dma_start(suc[:, 0:CK], su_ug).then_inc(consts, 16)
            sp.dma_start(suc[:, CK:CK + FJ], su_dp).then_inc(consts, 16)
            sp.dma_start(xh[:, 0, 0:P], before).then_inc(consts, 16)
            sp.dma_start(xh[:, 0, P:2 * P], causal).then_inc(consts, 16)
            load_pieces(sp, 0, 2)
            sp.dma_start(xs[:, :].rearrange("p (t n) -> p t n", t=TILES),
                         x.rearrange("(t p) n -> p t n", p=P)).then_inc(xload, 16)
            load_pieces(sp, 2, FIRST_PIECES)
            if len(STAGES) > 3:
                sp.wait_ge(a_done, made(base("A", 3) - 1))
                sp.dma_start(aux[:, 0:C], bv.partition_broadcast(P)).then_inc(auxl, 16)
                sp.dma_start(aux[:, C:2 * C], bo.partition_broadcast(P)).then_inc(auxl, 16)
                sp.dma_start(bqk[:, 0, :], bq).then_inc(auxl, 16)
                sp.dma_start(bqk[:, 1, :], bk).then_inc(auxl, 16)
                load_pieces(sp, FIRST_PIECES, len(pieces))
            s = len(STAGES) - 1
            outv = out.rearrange("(t p) n -> p t n", p=P)
            per = USES["A"][kind(s)]
            with sp.Fori(0, GROUPS // 2) as i:
                for p in range(2):
                    sp.wait_ge(a_done, made(at("A", s, i, p, per - 1)))
                    sp.dma_start(outv[:, bass.ds(group(i, p) * GT, GT), :],
                                 xt(group(i, p), 0, GT).rearrange("p (t n) -> p t n", t=GT)).then_inc(stored, 16)
            sp.wait_ge(stored, 16 * GROUPS)

        @block.gpsimd
        def _(pool):
            pool.memset(onesb[:, :], 1.0)
            pool.memset(bqk[:, :, :], 0.0)
            pool.memset(zero[:, :], 0.0)
            pool.memset(yt[:, :], 1.0).then_inc(set_up, 1)
            pool.wait_ge(consts, 16 * 8)

            def newton(s, i, p):
                pool.wait_ge(stats, filled(at("unit", s, i, p) + 1))
                for _ in range(N_T_STEPS):
                    pool.tensor_tensor(yt[:, :], y[:, :], y[:, :], ALU.mult)
                    pool.drain()
                    pool.tensor_tensor(yt[:, :], yt[:, :], ve[:, :], ALU.mult)
                    pool.drain()
                    pool.tensor_scalar(yt[:, :], yt[:, :], -0.5, 1.5, ALU.mult, ALU.add)
                    pool.drain()
                    last = pool.tensor_tensor(y[:, :], y[:, :], yt[:, :], ALU.mult)
                    if _ < N_T_STEPS - 1:
                        pool.drain()
                last.then_inc(rstd, 1)
                pool.drain()

            def stack_keys(s, i, q):
                pair = slice(2 * (q % 2), 2 * (q % 2) + 2)
                pool.wait_ge(g_done, made(at("G", s, i, 0, score_use((1, q)))))
                pool.tensor_tensor(KA[:, pair, :], kf[:, :, :], zero[:, 0:1].unsqueeze(2).broadcast_to([P, 2, C]), ALU.add)
                pool.drain()
                pool.tensor_tensor(KB[:, pair, :], kf[:, :, :], KA[:, pair, :].bitcast(F32), ALU.subtract)\
                    .then_inc(k_ready, 1)

            newton(0, 0, -1)
            for s in range(len(STAGES)):
                with pool.Fori(0, GROUPS // 2) as i:
                    for p in range(2):
                        if kind(s) == "A":
                            stack_keys(s, i, 4 * p)
                            stack_keys(s, i, 4 * p + 1)
                        newton(s, i, p)
                        if kind(s) == "A":
                            stack_keys(s, i, 4 * p + 2)
                            stack_keys(s, i, 4 * p + 3)

        def normalise(s, i, p, first=False):
            return 0 if first else at("unit", s, i, p) + 1

        @block.scalar
        def _(act):
            act.wait_ge(consts, 16 * 8)
            act.activation(identb[:, :], identf[:, :], ACT.Copy)
            act.activation(beforeb[:, :], xh[:, 0, 0:P], ACT.Copy)
            act.activation(causalb[:, :], xh[:, 0, P:2 * P], ACT.Copy)
            act.activation(hadf[:, 1, :], hadf[:, 0, :], ACT.Copy, scale=-1.0).then_inc(cast, 1)
            act.wait_ge(set_up, 1)

            for n in range(4):
                m, jh = n // 2, n % 2
                w = fg if m == 0 else fu
                for c in range(CK):
                    k = 2 * n + c
                    act.wait_ge(u_done, made(k))
                    act.activation(w[:, 0, c, jh * 512:(jh + 1) * 512], tmp[k % 2], ACT.Copy).then_inc(w_high, 1)
            for ch in range(2):
                for j in range(FJ):
                    act.wait_ge(banded, 8 * ch + j + 1)
                    act.activation(fd[:, 0, j, ch * P:(ch + 1) * P], tmp[j % 2][:, 0:P], ACT.Copy,
                                   scale=0.25).then_inc(w_high, 1)
            split_high(act, 6)
            for m in range(2):
                act.wait_ge(u_full, 12 + m + 1)
                for c in range(CK):
                    src = U(12 + m)[:, c * C:(c + 1) * C]
                    if m == 0:
                        hi = doubled(wk, c)[0]
                        for r in range(2):
                            act.activation(hi[:, :, r, :], src.rearrange("p (h d) -> p h d", h=HEADS), ACT.Copy)\
                               .then_inc(w_high, 1)
                    else:
                        for r in range(2):
                            act.activation(wv[:, 0, c, r * P:(r + 1) * P], src[:, r * P:(r + 1) * P], ACT.Copy)\
                               .then_inc(w_high, 1)
            for n in range(8, FIRST_PIECES):
                split_high(act, n)

            def xn_highs(s, i, p, first=False):
                v = 0 if first else at("unit", s, i, p) + 1
                buf = 0 if first else (p + 1) % 2
                tn = 0 if first else static("T", s, *norm_use(s, p))
                act.wait_ge(xh_read, made(v * GT + GT - 1))
                act.wait_ge(xn_read, free(v))
                for c in range(CK):
                    act.activation(xnv[:, buf, 0, c, :], T(tn + c)[:, :], ACT.Copy).then_inc(xn_high, 1)

            def chunk(s, i, p, j):
                n, h = at("G", s, i, p, j), at("h", s, i, p, j)
                ns, b = static("G", s, p, j), static("h", s, p, j) % 2
                act.wait_ge(g_full, filled(n))
                act.wait_ge(h_ready, free(h))
                act.activation(sw[:, b, :], G(ns)[:, :], ACT.Silu).then_inc(g_done, 1)

            def chunk_high(s, i, p, j):
                h, b = at("h", s, i, p, j), static("h", s, p, j) % 2
                if kind(s) == "F":
                    act.wait_ge(u_done, made(at("U", s, i, p, j)))
                else:
                    act.wait_ge(weighted, filled(at("w", s, i, p, j)))
                act.wait_ge(h_read, free(h))
                act.activation(hid[:, b, 0, :], sw[:, b, :], ACT.Copy).then_inc(h_high, 1)

            def ffn(s, i, p):
                for j in range(FJ):
                    chunk(s, i, p, j)
                    chunk_high(s, i, p, j)
                    if j == 5:
                        xn_highs(s, i, p)

            def experts(s, i, p):
                act.wait_ge(t_done, made(at("T", s, i, p, 0)))
                act.activation(sg[:, :, :], lg[:, :, 0:EXPERTS], ACT.Sigmoid).then_inc(sigm, 1)
                act.wait_ge(t_full, filled(at("Tf", s, i, p, 1)))
                act.activation(sh[0:SHARED, :], T(static("T", s, p, 1))[SHARED:2 * SHARED, :], ACT.Silu)\
                   .then_inc(sh_act, 1)
                act.wait_ge(t_done, made(at("T", s, i, p, 1)))
                act.activation(shh[0:SHARED, 0, :], sh[0:SHARED, :], ACT.Copy).then_inc(sh_high, 1)
                for j in range(MJ):
                    chunk(s, i, p, j)
                    chunk_high(s, i, p, j)
                    if j == 12:
                        xn_highs(s, i, p)

            def projected(s, i, item):
                m, q = item
                n = score_use(item)
                act.wait_ge((q_ready, k_ready)[m], free(at("quarter", s, i, 0, q)))
                act.wait_ge(g_full, filled(at("G", s, i, 0, n)))
                for t in range(2):
                    col = 2 * (q % 2) + t
                    ins = act.activation((qf, kf)[m][:, t, :], S(n)[:, t * C:(t + 1) * C], ACT.Identity,
                                         bias=bqk[:, m, col:col + 1])
                ins.then_inc(g_done, 1)

            def exps(s, i, k):
                sc = S(score_use(k))
                b, h = k // HEADS % 2, k % HEADS
                act.wait_ge(maxed, filled(at("head", s, i, 0, k)))
                act.wait_ge(u_full, at("U", s, i, 0, k) - 1)
                act.activation(Pr[:, k % 2, 0:P], sc[:, 0:P], ACT.Exp, bias=nmax[:, k % 3, 0:1],
                               accum_out=den[:, b, 0, h:h + 1])
                act.activation(Pr[:, k % 2, P:KEYS], sc[:, P:KEYS], ACT.Exp, bias=nmax[:, k % 3, 1:2],
                               accum_out=den[:, b, 1, h:h + 1]).then_inc(g_done, 1)

            def ctx_highs(s, i, b):
                act.wait_ge(ctx_made, filled(at("half", s, i, 0, b)))
                act.activation(cT[:, 0, :, :].rearrange("p c n -> p (c n)"), cn.rearrange("p t n -> p (t n)"),
                               ACT.Copy).then_inc(ctx_high, 1)

            def evacuate(s, i, k):
                act.wait_ge(u_full, filled(at("U", s, i, 0, k)))
                act.wait_ge(pv_done, free(at("head", s, i, 0, k)))
                act.activation(PT[:, k % 2, :], TURNED[:, 0:KEYS], ACT.Copy).then_inc(u_done, 1)

            def attention(s, i):
                for k in range(4 * HEADS):
                    if k == 0:
                        for item in PARTS_BEFORE[0]:
                            projected(s, i, item)
                    exps(s, i, k)
                    for item in PARTS_BEFORE.get(k + 1, []):
                        projected(s, i, item)
                    if STAGES[s] == "A0" and k >= 1:
                        evacuate(s, i, k - 1)
                    if k >= HEADS and k % HEADS == 4:
                        ctx_highs(s, i, k // HEADS - 1)
                    if k % (2 * HEADS) == 13:
                        xn_highs(s, i, k // (2 * HEADS))
                if STAGES[s] == "A0":
                    evacuate(s, i, 4 * HEADS - 1)
                ctx_highs(s, i, 3)

            xn_highs(0, 0, 0, first=True)
            for s in range(len(STAGES)):
                if s == 3:
                    for n in range(FIRST_PIECES, len(pieces)):
                        split_high(act, n)
                if STAGES[s] == "A1":
                    act.wait_ge(auxl, 64)
                    act.activation(bqk[:, 0, :], bqk[:, 0, :], ACT.Copy, scale=0.25)
                    act.drain()
                with act.Fori(0, GROUPS // 2) as i:
                    if kind(s) == "A":
                        attention(s, i)
                    else:
                        for p in range(2):
                            (ffn if kind(s) == "F" else experts)(s, i, p)

        @block.vector
        def _(dve):
            for ring in (g_done, u_done, t_done, a_done, xh_read, xn_read, h_ready, h_read, pv_done, stage_done):
                dve.sem_inc(ring, RING)
            dve.sem_inc(q_ready, 1)
            dve.sem_inc(k_ready, 1)
            dve.memset(countb[:, :], 0.0)

            def scale_up(n):
                m, jh = n // 2, n % 2
                w = fg if m == 0 else fu
                for c in range(CK):
                    k = 2 * n + c
                    dve.wait_ge(u_full, k + 1)
                    if c == 0:
                        dve.wait_ge(stage_full[n % 2], stage_value(n))
                    dve.scalar_tensor_tensor(tmp[k % 2], U(k)[:, :], suc[:, c:c + 1], slot(n)[:, 1024:SLOT],
                                             ALU.mult, ALU.mult).then_inc(u_done, 1)
                    dve.wait_ge(w_high, k + 1)
                    ins = dve.tensor_tensor(w[:, 1, c, jh * 512:(jh + 1) * 512], tmp[k % 2],
                                            w[:, 0, c, jh * 512:(jh + 1) * 512].bitcast(F32), ALU.subtract)
                ins.then_inc(stage_done, 1)

            dve.wait_ge(consts, 16 * 8)
            dve.wait_ge(cast, 1)
            for n in range(4):
                scale_up(n)

            for ch in range(2):
                n = 4 + ch
                v = slot(n)
                dve.wait_ge(stage_full[n % 2], stage_value(n))
                dve.drain()
                dve.tensor_copy(tmp[1][:, 256:384], v[:, 1024:1024 + P])
                dve.drain()
                for level in BUTTERFLIES:
                    for a, b, d in level:
                        dve.tensor_tensor(v[:, d:d + P], v[:, a:a + P], v[:, b:b + P], ALU.subtract)
                    dve.drain()
                    for a, b, d in level:
                        ins = dve.tensor_tensor(v[:, a:a + P], v[:, a:a + P], v[:, b:b + P], ALU.add)
                    if level is not BUTTERFLIES[-1]:
                        dve.drain()
                ins.then_inc(weights, 1)
                for j in range(FJ):
                    bank, col = 8 + 2 * ch + j // 4, (j % 4) * P
                    if j % 4 == 0:
                        dve.wait_ge(u_full, bank + 1)
                    ins = dve.scalar_tensor_tensor(tmp[j % 2][:, 0:P], U(bank)[:, col:col + P],
                                                   suc[:, CK + j:CK + j + 1], tmp[1][:, 256:384],
                                                   ALU.mult, ALU.mult).then_inc(banded, 1)
                    dve.wait_ge(w_high, 8 + 8 * ch + j + 1)
                    ins = dve.scalar_tensor_tensor(fd[:, 1, j, ch * P:(ch + 1) * P], tmp[j % 2][:, 0:P], 0.25,
                                                   fd[:, 0, j, ch * P:(ch + 1) * P].bitcast(F32),
                                                   ALU.mult, ALU.subtract)
                    if j % 4 == 3:
                        ins.then_inc(u_done, 1)
                dve.drain()
                dve.sem_inc(stage_done, 1)
            split_low(dve, 6)
            for m in range(2):
                for c in range(CK):
                    src = U(12 + m)[:, c * C:(c + 1) * C]
                    for r in range(2):
                        dve.wait_ge(w_high, highs(7) + 4 * m + 2 * c + r + 1)
                        if c == 0 and r == 0:
                            dve.wait_ge(w_high, highs(7) + 4 * m + 4)
                        if m == 0:
                            hi, lo = doubled(wk, c)
                            ins = dve.tensor_tensor(lo[:, :, r, :], src.rearrange("p (h d) -> p h d", h=HEADS),
                                                    hi[:, :, r, :].bitcast(F32), ALU.subtract)
                        else:
                            ins = dve.tensor_tensor(wv[:, 1, c, r * P:(r + 1) * P], src[:, r * P:(r + 1) * P],
                                                    wv[:, 0, c, r * P:(r + 1) * P].bitcast(F32), ALU.subtract)
                ins.then_inc(u_done, 1)
            dve.drain()
            dve.sem_inc(stage_done, 1)
            for n in range(8, FIRST_PIECES):
                split_low(dve, n)
            dve.drain()

            QUERIES_AT = {2: 1, 9: 2, 17: 3, 26: 4, 34: 5, 41: 6, 49: 7}

            def group_stats(g):
                dve.drain()
                for t in range(GT):
                    dve.bn_stats(st[:, t, :], xt(g, t))
                dve.drain()
                for t in range(GT):
                    dve.bn_aggr(mv[:, t, :], st[:, t, :])
                dve.drain()
                dve.tensor_scalar(ve[:, :], mv[:, :, 1], EPS, None, ALU.add)
                dve.drain()
                dve.tensor_scalar(y[:, :].bitcast(I32), ve[:, :].bitcast(I32), 1, None, ALU.arith_shift_right)
                dve.drain()
                dve.tensor_scalar(y[:, :].bitcast(I32), y[:, :].bitcast(I32), -1.0, float(0x5F3759DF),
                                  ALU.mult, ALU.add).then_inc(stats, 1)

            def xhats(s, i, p, first=False):
                v = 0 if first else at("unit", s, i, p) + 1
                g = 0 if first else following(i, p)
                dve.wait_ge(xh_read, v * GT + RING)
                dve.wait_ge(rstd, v + 1)
                for t in range(GT):
                    dve.tensor_scalar(xh[:, t, :], xt(g, t), mv[:, t, 0:1], y[:, t:t + 1],
                                      ALU.subtract, ALU.mult).then_inc(xh_full, 1)

            def xn_lows(s, i, p, first=False):
                v = 0 if first else at("unit", s, i, p) + 1
                buf = 0 if first else (p + 1) % 2
                tn = 0 if first else static("T", s, *norm_use(s, p))
                for c in range(CK):
                    dve.wait_ge(xn_high, v * CK + c + 1)
                    dve.tensor_tensor(xnv[:, buf, 1, c, :], T(tn + c)[:, :], xnv[:, buf, 0, c, :].bitcast(F32),
                                      ALU.subtract).then_inc(t_done, 1)

            def product(s, i, p, j):
                n, b = static("U", s, p, j), static("h", s, p, j) % 2
                dve.wait_ge(g_done, made(at("G", s, i, p, j)))
                dve.wait_ge(u_full, filled(at("U", s, i, p, j)))
                dve.tensor_tensor(sw[:, b, :], sw[:, b, :], U(n)[:, :], ALU.mult).then_inc(u_done, 1)

            def low(s, i, p, j):
                b = static("h", s, p, j) % 2
                dve.wait_ge(h_high, filled(at("h", s, i, p, j)))
                dve.tensor_tensor(hid[:, b, 1, :], sw[:, b, :], hid[:, b, 0, :].bitcast(F32), ALU.subtract)\
                   .then_inc(h_ready, 1)

            def residual(s, i, p, n, pair):
                if kind(s) == "A":
                    dve.wait_ge(a_full, filled(at("Af", s, i, p, pair)))
                else:
                    dve.wait_ge(h_read, made(at("h", s, i, p, USES["h"][kind(s)] - 1)))
                dve.tensor_tensor(xt(group(i, p), 2 * pair, 2), xt(group(i, p), 2 * pair, 2),
                                  A(static("A", s, p, n))[:, :], ALU.add).then_inc(a_done, 1)

            def ffn(s, i, p):
                for j in range(FJ):
                    product(s, i, p, j)
                    low(s, i, p, j)
                    if j == 0 and p == 1:
                        residual(s, i, 0, 0, 0)
                        residual(s, i, 0, 1, 1)
                    if j == 1:
                        group_stats(following(i, p))
                    if j == 3:
                        xhats(s, i, p)
                    if j == 5:
                        xn_lows(s, i, p)
                if p == 1:
                    residual(s, i, p, 0, 0)
                    residual(s, i, p, 1, 1)

            def route(s, i, p):
                dve.drain()
                dve.memset(lg[:, :, EXPERTS:EXPERTS + 2], BIG)
                dve.wait_ge(t_full, filled(at("Tf", s, i, p, 0)))
                dve.tensor_scalar(lg[:, :, 0:EXPERTS], three(T(static("T", s, p, 0))[:, 0:GT * EXPERTS], GT), 17.5, None,
                                  ALU.min).then_inc(t_done, 1)
                dve.drain()
                for t in range(GT):
                    dve.max(top[:, t, :], lg[:, t, :])
                dve.drain()
                for t in range(GT):
                    dve.match_replace(out=lr[:, t, :], in_to_replace=top[:, t, :], in_values=lg[:, t, :],
                                      imm_value=-BIG)
                dve.drain()
                dve.tensor_tensor(maskb[:, :, :], lr[:, :, 0:EXPERTS], lg[:, :, 0:EXPERTS], ALU.not_equal)\
                   .then_inc(chosen, 1)

            def share(s, i, p):
                dve.wait_ge(sh_act, filled(at("moe", s, i, p)))
                dve.tensor_tensor(sh[0:SHARED, :], sh[0:SHARED, :], T(static("T", s, p, 1))[0:SHARED, :], ALU.mult)\
                   .then_inc(t_done, 1)

            def share_low(s, i, p):
                dve.wait_ge(sh_high, filled(at("moe", s, i, p)))
                dve.tensor_tensor(shh[0:SHARED, 1, :], sh[0:SHARED, :], shh[0:SHARED, 0, :].bitcast(F32), ALU.subtract)\
                   .then_inc(sh_ready, 1)

            def weigh(s, i, p):
                dve.wait_ge(sigm, filled(at("moe", s, i, p)))
                dve.tensor_tensor(sg[:, :, :], sg[:, :, :], maskb[:, :, :], ALU.mult)
                dve.drain()
                dve.tensor_reduce(tot[:, :], sg[:, :, :], AX.X, ALU.add)
                dve.drain()
                dve.reciprocal(tot[:, :], tot[:, :])
                dve.drain()
                dve.tensor_tensor(sg[:, :, :], sg[:, :, :], tot[:, :].unsqueeze(2).broadcast_to([P, GT, EXPERTS]), ALU.mult)
                dve.drain()
                dve.wait_ge(t_full, filled(at("Tf", s, i, p, 2)))
                pos = three(T(static("T", s, p, 2))[:, 0:GT * EXPERTS], GT)
                for d in range(2):
                    ins = dve.scalar_tensor_tensor(w2[:, :, d, :], pos, float(CAP), sg[:, :, :], ALU.is_lt, ALU.mult)
                ins.then_inc(t_done, 1)
                dve.tensor_reduce(lr[:, 0, 0:EXPERTS], maskb[:, :, :].rearrange("p t e -> p e t"), AX.X, ALU.add)
                dve.drain()
                dve.tensor_tensor(countb[:, :], countb[:, :], lr[:, 0, 0:EXPERTS], ALU.add).then_inc(wmade, 1)

            def weights_across(s, i, p):
                dve.wait_ge(t_full, filled(at("Tf", s, i, p, 3)))
                dve.tensor_copy(wrep, T(static("T", s, p, 3))[:, :]).then_inc(t_done, 1)
                dve.drain()

            def experts(s, i, p):
                route(s, i, p)
                if p == 1:
                    residual(s, i, 0, 0, 0)
                    residual(s, i, 0, 1, 1)
                share(s, i, p)
                share_low(s, i, p)
                weigh(s, i, p)
                weights_across(s, i, p)
                for j in range(MJ):
                    b = static("h", s, p, j) % 2
                    product(s, i, p, j)
                    dve.wait_ge(u_done, made(at("U", s, i, p, j)))
                    dve.tensor_tensor(sw[:, b, :], sw[:, b, :], wrep, ALU.mult).then_inc(weighted, 1)
                    low(s, i, p, j)
                    if j == 6:
                        group_stats(following(i, p))
                    if j == 9:
                        xhats(s, i, p)
                    if j == 12:
                        xn_lows(s, i, p)
                if p == 1:
                    residual(s, i, p, 0, 0)
                    residual(s, i, p, 1, 1)

            def stack_queries(s, i, q):
                pair = slice(2 * (q % 2), 2 * (q % 2) + 2)
                dve.wait_ge(g_done, made(at("G", s, i, 0, score_use((0, q)))))
                dve.tensor_copy(Qs[:, pair, :], qf[:, :, :])
                dve.drain()
                dve.scalar_tensor_tensor(Qs[:, pair, :], Qs[:, pair, :].bitcast(F32), hilos[:, 0:1], qf[:, :, :],
                                         ALU.mult, ALU.add).then_inc(q_ready, 1)

            def maxima(s, i, k):
                n = score_use(k)
                sc = S(n)
                dve.wait_ge(g_full, filled(at("G", s, i, 0, n)))
                if STAGES[s] == "A0":
                    dve.tensor_tensor(sc[:, 0:KEYS], sc[:, 0:KEYS], aux[:, 0:KEYS], ALU.mult)
                    dve.drain()
                dve.tensor_reduce(nmax[:, k % 3, 0:1], sc[:, 0:P], AX.X, ALU.max, negate=True)
                dve.tensor_reduce(nmax[:, k % 3, 1:2], sc[:, P:KEYS], AX.X, ALU.max, negate=True).then_inc(maxed, 1)

            def evacuate(s, i, k):
                dve.wait_ge(u_full, filled(at("U", s, i, 0, k)))
                dve.wait_ge(pv_done, free(at("head", s, i, 0, k)))
                dve.tensor_copy(PT[:, k % 2, :], TURNED[:, 0:KEYS]).then_inc(u_done, 1)

            def sums_leave(s, i, b):
                dve.wait_ge(pv_done, made(at("head", s, i, 0, HEADS * b + HEADS - 1)))
                dve.tensor_copy(sums, A(static("A", s, 0, 2 * b))[:, :]).then_inc(a_done, 1)

            def values(s, i, b):
                dve.wait_ge(t_full, filled(at("Tf", s, i, 0, VALUES_TF[b])))
                for e in range(2):
                    def every_other(v):
                        return v.rearrange("p t (h e d) -> p t h e d", e=2, d=HD)[:, :, :, e, :]
                    src = every_other(three(T(static("T", s, 0, VALUES_T[b]))[:, :], 2))
                    dst = Vs.rearrange("p t (h e) n -> p t h e n", e=2)[:, :, :, e, e * HD:(e + 1) * HD]
                    if STAGES[s] == "A0":
                        ins = dve.tensor_copy(dst, src)
                    else:
                        bias = aux[:, 0:C].rearrange("p (h e d) -> p h e d", e=2, d=HD)[:, :, e, :]
                        ins = dve.tensor_tensor(dst, src, bias.unsqueeze(1).broadcast_to([P, 2, HEADS // 2, HD]), ALU.add)
                ins.then_inc(t_done, 1)

            def shares(s, i, b):
                d = den[:, b % 2, :, :]
                dve.reciprocal(d, d)
                dve.drain()
                dve.tensor_copy(cn[:, :, :].rearrange("p t (h d) -> p (t h) d", h=HEADS),
                                d.rearrange("p t h -> p (t h)").unsqueeze(2).broadcast_to([P, 2 * HEADS, HD]))\
                   .then_inc(shared, 1)

            def context(s, i, b):
                dve.wait_ge(t_full, filled(at("Tf", s, i, 0, CONTEXT_TF[b])))
                dve.tensor_tensor(cn.rearrange("p t n -> p (t n)"), sums, T(static("T", s, 0, CONTEXT_T[b]))[:, :],
                                  ALU.mult).then_inc(ctx_made, 1)

            def ctx_lows(s, i, b):
                dve.wait_ge(ctx_high, filled(at("half", s, i, 0, b)))
                dve.tensor_tensor(cT[:, 1, :, :].rearrange("p c n -> p (c n)"), cn.rearrange("p t n -> p (t n)"),
                                  cT[:, 0, :, :].rearrange("p c n -> p (c n)").bitcast(F32), ALU.subtract)\
                   .then_inc(t_done, 1)

            def output(s, i, b):
                if STAGES[s] == "A1":
                    pair = xt(group(i, b // 2), 2 * (b % 2), 2)
                    dve.tensor_tensor(pair.rearrange("p (t n) -> p t n", t=2), pair.rearrange("p (t n) -> p t n", t=2),
                                      aux[:, C:2 * C].unsqueeze(1).broadcast_to([P, 2, C]), ALU.add)
                    dve.drain()
                residual(s, i, b // 2, 2 * (b % 2) + 1, b % 2)

            def attention(s, i):
                stack_queries(s, i, 0)
                maxima(s, i, 0)
                values(s, i, 0)
                for k in range(1, AHEAD):
                    maxima(s, i, k)
                for k in range(4 * HEADS):
                    b, p = k // HEADS, k // (2 * HEADS)
                    if k + AHEAD < 4 * HEADS:
                        maxima(s, i, k + AHEAD)
                    if STAGES[s] == "A1":
                        evacuate(s, i, k)
                    if k >= HEADS and k % HEADS == 0:
                        sums_leave(s, i, b - 1)
                        values(s, i, b)
                        shares(s, i, b - 1)
                    if k >= HEADS and k % HEADS == 3:
                        context(s, i, b - 1)
                    if k >= HEADS and k % HEADS == 5:
                        ctx_lows(s, i, b - 1)
                    if k >= HEADS and k % HEADS == 7:
                        output(s, i, b - 1)
                    if k % (2 * HEADS) == 8:
                        group_stats(following(i, p))
                    if k % (2 * HEADS) == 11:
                        xhats(s, i, p)
                    if k % (2 * HEADS) == 13:
                        xn_lows(s, i, p)
                    if k in QUERIES_AT:
                        stack_queries(s, i, QUERIES_AT[k])
                sums_leave(s, i, 3)
                shares(s, i, 3)
                context(s, i, 3)
                ctx_lows(s, i, 3)
                output(s, i, 3)

            dve.wait_ge(xload, 16)
            group_stats(0)
            xhats(0, 0, 0, first=True)
            xn_lows(0, 0, 0, first=True)
            for s in range(len(STAGES)):
                if s == 3:
                    for n in range(FIRST_PIECES, len(pieces)):
                        split_low(dve, n)
                    dve.drain()
                if STAGES[s] == "A1":
                    dve.wait_ge(auxl, 64)
                if kind(s) == "A":
                    dve.drain()
                    dve.memset(WF[:, 0:2 * HEADS * 2 * HD], 0.0)
                    dve.drain()
                if kind(s) == "E":
                    dve.drain()
                    dve.memset(countb[:, :], 0.0)
                with dve.Fori(0, GROUPS // 2) as i:
                    if kind(s) == "A":
                        attention(s, i)
                    else:
                        for p in range(2):
                            (ffn if kind(s) == "F" else experts)(s, i, p)

        @block.tensor
        def _(pe):
            pe.wait_ge(cast, 1)
            pe.wait_ge(set_up, 1)
            pe.wait_ge(consts, 16 * 8)
            for n in range(4):
                v = slot(n)
                pe.wait_ge(stage_full[n % 2], stage_value(n))
                for a in range(CK):
                    pe.wait_ge(u_done, free(2 * n + a))
                    for b in range(CK):
                        mm = pe.matmul(U(2 * n + a)[:, :], hadf[:, a & b, :], v[:, b * 512:(b + 1) * 512],
                                       start=(b == 0), stop=(b == CK - 1))
                    mm.then_inc(u_full, 1)
            for ch in range(2):
                v = slot(4 + ch)
                pe.wait_ge(weights, ch + 1)
                for half in range(2):
                    pe.wait_ge(u_done, free(8 + 2 * ch + half))
                    for q in range(4):
                        at_col = CHUNK_AT[4 * half + q]
                        mm = pe.matmul(U(8 + 2 * ch + half)[:, q * P:(q + 1) * P], hadf[:, 0, :],
                                       v[:, at_col:at_col + P], start=True, stop=True)
                    mm.then_inc(u_full, 1)
            v = slot(7)
            pe.wait_ge(stage_full[1], stage_value(7))
            for m in range(2):
                pe.wait_ge(u_done, free(12 + m))
                for c in range(CK):
                    mm = pe.matmul(U(12 + m)[:, c * C:(c + 1) * C], v[0:LATENT, m * C + c * P:m * C + (c + 1) * P],
                                   v[0:LATENT, (2 + m) * C:(3 + m) * C], start=True, stop=True)
                mm.then_inc(u_full, 1)

            def transposes(s, i, p, first=False):
                v = 0 if first else at("unit", s, i, p) + 1
                unit, n = (0, 0) if first else norm_use(s, p)
                ti = 0 if first else at("T", s, i, unit, n)
                tn = 0 if first else static("T", s, unit, n)
                pe.wait_ge(t_done, free(ti + 1))
                for t in range(GT):
                    pe.wait_ge(xh_full, v * GT + t + 1)
                    for c in range(CK):
                        mm = pe.transpose(T(tn + c)[:, t * P:(t + 1) * P], xh[:, t, c * P:(c + 1) * P], identf[:, :])
                    mm.then_inc(xh_read, 1)

            def xn_ready(s, i, p):
                if kind(s) == "A" and p == 1:
                    pe.wait_ge(t_done, made(at("T", s, i, 0, NORM_T[0] + 1)))
                else:
                    pe.wait_ge(t_done, made(at("T", s, i, p) - 1))

            PASSES = ((0, 0), (1, 0), (0, 1))

            def up(bank, w, c_of, rhs, n):
                k = 0
                for c in range(CK):
                    for a, b in PASSES:
                        mm = pe.matmul(bank, c_of(w, a, c), rhs(b, c), start=(k == 0), stop=(k == 3 * CK - 1))
                        k += 1
                return mm

            def down(bank_of, src_of, w_of, first, last, before_low=None):
                for a, b in ((0, 0), (0, 1), (1, 0)):
                    if a == 1 and before_low is not None:
                        before_low()
                    for t in range(GT):
                        mm = pe.matmul(bank_of(t // 2)[:, (t % 2) * C:(t % 2 + 1) * C], src_of(a, t), w_of(b),
                                       start=(first and a == 0 and b == 0 and t % 2 == 0),
                                       stop=(last and a == 1), skip_group_check=True)
                        yield mm

            def ups(s, i, p, j, gate, upw):
                buf = p
                rhs = lambda b, c: xnv[:, buf, b, c, :]
                pe.wait_ge(g_done, free(at("G", s, i, p, j)))
                up(G(static("G", s, p, j))[:, :], gate, lambda w, a, c: w[:, a, c, j * P:(j + 1) * P], rhs, 0)\
                    .then_inc(g_full, 1)
                pe.wait_ge(u_done, free(at("U", s, i, p, j)))
                up(U(static("U", s, p, j))[:, :], upw, lambda w, a, c: w[:, a, c, j * P:(j + 1) * P], rhs, 0)\
                    .then_inc(u_full, 1)

            def downs(s, i, p, j, w, first, last):
                b = static("h", s, p, j) % 2
                h = at("h", s, i, p, j)
                n = static("A", s, p)
                if first:
                    pe.wait_ge(a_done, free(at("A", s, i, p, 1)))
                pe.wait_ge(h_high, filled(h))
                k = 0
                for mm in down(lambda pair: A(n + pair), lambda a, t: hid[:, b, a, t * P:(t + 1) * P],
                               lambda part: w[:, part, j, :], first, last,
                               lambda: pe.wait_ge(h_ready, made(h))):
                    k += 1
                    if last and k == 1:
                        mm.then_inc(xn_read, 1)
                mm.then_inc(h_read, 1)

            def ffn(s, i, p):
                xn_ready(s, i, p)
                for j in range(FJ):
                    ups(s, i, p, j, fg, fu)
                    if j == 0 and p == 1:
                        downs(s, i, 0, FJ - 1, fd, False, True)
                    if j >= 1:
                        downs(s, i, p, j - 1, fd, j == 1, False)
                    if j == 5:
                        transposes(s, i, p)
                if p == 1:
                    downs(s, i, p, FJ - 1, fd, False, True)

            def experts(s, i, p):
                xn_ready(s, i, p)
                pe.wait_ge(t_done, free(at("T", s, i, p, 0)))
                for t in range(GT):
                    k = 0
                    for c in range(CK):
                        for a, b in PASSES:
                            mm = pe.matmul(T(static("T", s, p, 0))[:, t * EXPERTS:(t + 1) * EXPERTS],
                                           xnv[:, p, a, c, t * P:(t + 1) * P], mg[:, b, c, :],
                                           start=(k == 0), stop=(k == 3 * CK - 1))
                            k += 1
                mm.then_inc(t_full, 1)
                pe.wait_ge(t_done, free(at("T", s, i, p, 1)))
                up(T(static("T", s, p, 1))[:, :], shu, lambda w, a, c: w[:, a, c, :], lambda b, c: xnv[:, p, b, c, :], 0)\
                    .then_inc(t_full, 1)
                mj = lambda w, a, c, v, j: w[:, a, c, v, j, :]

                def ups_m(j):
                    rhs = lambda b, c: xnv[:, p, b, c, :]
                    pe.wait_ge(g_done, free(at("G", s, i, p, j)))
                    up(G(static("G", s, p, j))[:, :], mw, lambda w, a, c: w[:, a, c, 0, j, :], rhs, 0).then_inc(g_full, 1)
                    pe.wait_ge(u_done, free(at("U", s, i, p, j)))
                    up(U(static("U", s, p, j))[:, :], mw, lambda w, a, c: w[:, a, c, 1, j, :], rhs, 0).then_inc(u_full, 1)

                if p == 1:
                    downs(s, i, 0, MJ - 1, md, False, True)
                ups_m(0)
                pe.wait_ge(t_done, free(at("T", s, i, p, 2)))
                pe.wait_ge(chosen, filled(at("moe", s, i, p)))
                for t in range(GT):
                    dst = T(static("T", s, p, 2))[:, t * EXPERTS:(t + 1) * EXPERTS]
                    pe.matmul(dst, onesb[:, :], countb[:, :], start=True, stop=False)
                    for r in range(t):
                        pe.matmul(dst, onesb[:, :], maskb[:, r, :], start=False, stop=False)
                    mm = pe.matmul(dst, beforeb[:, :], maskb[:, t, :], start=False, stop=True)
                mm.then_inc(t_full, 1)
                ups_m(1)
                pe.wait_ge(t_done, free(at("T", s, i, p, 3)))
                pe.wait_ge(wmade, filled(at("moe", s, i, p)))
                for t in range(GT):
                    mm = pe.transpose(T(static("T", s, p, 3))[:, t * P:(t + 1) * P],
                                      w2[:, t, :, :].rearrange("p d e -> p (d e)"), identf[:, :])
                mm.then_inc(t_full, 1)
                n = static("A", s, p)
                pe.wait_ge(a_done, free(at("A", s, i, p, 1)))
                pe.wait_ge(sh_ready, filled(at("moe", s, i, p)))
                for mm in down(lambda pair: A(n + pair), lambda a, t: shh[0:SHARED, a, t * P:(t + 1) * P],
                               lambda part: shd[0:SHARED, part, :], True, False):
                    pass
                for j in range(MJ):
                    if j >= 2:
                        ups_m(j)
                    if j >= 1:
                        downs(s, i, p, j - 1, md, False, False)
                    if j == 12:
                        transposes(s, i, p)
                if p == 1:
                    downs(s, i, p, MJ - 1, md, False, True)

            def project(s, i, item):
                m, q = item
                n, p, b = score_use(item), q // 4, q // 2 % 2
                if item == (0, 0) or item == (0, 4):
                    xn_ready(s, i, p)
                pe.wait_ge(g_done, score_free(s, i, n))
                for t in range(2):
                    col = 2 * (q % 2) + t
                    mm = up(S(n)[:, t * C:(t + 1) * C], (wq, wk)[m],
                            lambda w_, a, c: w_[:, a, c, col * P:(col + 1) * P],
                            lambda r, c: xnv[:, p, r, c, b * BATCH:(b + 1) * BATCH], 0)
                mm.then_inc(g_full, 1)

            def values(s, i, b):
                n = VALUES_T[b]
                pe.wait_ge(t_done, free(at("T", s, i, 0, n)))
                for t in range(2):
                    k = 0
                    for c in range(CK):
                        for a, r in PASSES:
                            lo = (b % 2) * BATCH + t * P
                            mm = pe.matmul(T(static("T", s, 0, n))[:, t * C:(t + 1) * C], xnv[:, b // 2, a, c, lo:lo + P],
                                           wv[:, r, c, :], start=(k == 0), stop=(k == 3 * CK - 1))
                            k += 1
                mm.then_inc(t_full, 1)

            def scores(s, i, k):
                n = score_use(k)
                h = k % HEADS
                t, rows = h // 4, slice(32 * (h % 4), 32 * (h % 4) + 32)
                bank = S(n)
                pe.wait_ge(g_done, score_free(s, i, n))
                if k % 8 == 0:
                    pe.wait_ge(q_ready, at("quarter", s, i, 0, k // 8) + 2)
                    pe.wait_ge(k_ready, at("quarter", s, i, 0, k // 8) + 2)
                queries = [Qs[rows, t, q * P:(q + 1) * P] for q in range(2)]
                pe.matmul(bank[:, 0:P], queries[0], KA[rows, t, 0:P], start=True, stop=False, skip_group_check=True)
                pe.matmul(bank[:, P:KEYS], queries[1], KA[rows, t, :], start=False, stop=False, skip_group_check=True)
                diagonals = bank[:, 0:2 * BATCH].rearrange("p (a n) -> p a n", a=2)[:, :, 0:P]
                pe.matmul(diagonals, identb[:, :], causalb[:, :].unsqueeze(1).broadcast_to([P, 2, P]), start=False,
                          stop=False, skip_group_check=True)
                pe.matmul(bank[:, 0:P], queries[0], KB[rows, t, 0:P], start=False, stop=True, skip_group_check=True)
                pe.matmul(bank[:, P:KEYS], queries[1], KB[rows, t, :], start=False, stop=True, skip_group_check=True)\
                    .then_inc(g_full, 1)

            def turn(s, i, k):
                pe.wait_ge(g_done, made(at("G", s, i, 0, score_use(k))))
                pe.wait_ge(u_done, at("U", s, i, 0, k) + RING)
                for c in range(3):
                    mm = pe.transpose(TURNED[:, c * P:(c + 1) * P], Pr[:, k % 2, c * P:(c + 1) * P], identf[:, :])
                mm.then_inc(u_full, 1)

            def mix(s, i, k):
                b, h = k // HEADS, k % HEADS
                bank = A(static("A", s, 0, 2 * b))
                if h == 0:
                    pe.wait_ge(a_done, free(at("A", s, i, 0, 2 * b)))
                    pe.wait_ge(t_done, made(at("T", s, i, 0, VALUES_T[b])))
                pe.wait_ge(u_done, made(at("U", s, i, 0, k)))
                strip = slice(32 * (h % 8 // 2), 32 * (h % 8 // 2) + 32)
                dst = bank[strip, (h // 8) * C:(h // 8 + 1) * C]
                pe.matmul(dst, Vs[:, 0, h, :], PT[:, k % 2, 0:2 * P], start=(h % 2 == 0), stop=False, skip_group_check=True)
                pe.matmul(dst[:, P:2 * P], Vs[:, 1, h, :], PT[:, k % 2, 2 * P:KEYS], start=False, stop=(h % 2 == 1),
                          skip_group_check=True).then_inc(pv_done, 1)

            def turn_shares(s, i, b):
                n = CONTEXT_T[b]
                pe.wait_ge(shared, filled(at("half", s, i, 0, b)))
                pe.wait_ge(t_done, free(at("T", s, i, 0, n)))
                for c in range(CK):
                    for t in range(2):
                        lo = c * BATCH + t * P
                        mm = pe.transpose(T(static("T", s, 0, n))[:, lo:lo + P], cn[:, t, c * P:(c + 1) * P], identf[:, :])
                mm.then_inc(t_full, 1)

            def project_out(s, i, b):
                n = 2 * b + 1
                pe.wait_ge(t_done, made(at("T", s, i, 0, CONTEXT_T[b])))
                pe.wait_ge(a_done, free(at("A", s, i, 0, n)))
                for t in range(2):
                    k = 0
                    for c in range(CK):
                        for a, r in PASSES:
                            mm = pe.matmul(A(static("A", s, 0, n))[:, t * C:(t + 1) * C], cT[:, a, c, t * P:(t + 1) * P],
                                           wo[:, r, c, :], start=(k == 0), stop=(k == 3 * CK - 1))
                            if b % 2 == 1 and t == 0 and k == 0:
                                mm.then_inc(xn_read, 1)
                            k += 1
                mm.then_inc(a_full, 1)

            def attention(s, i):
                def score(k):
                    for item in PARTS_BEFORE.get(k, []):
                        project(s, i, item)
                    scores(s, i, k)

                project(s, i, (0, 0))
                project(s, i, (1, 0))
                values(s, i, 0)
                scores(s, i, 0)
                for k in range(1, AHEAD):
                    score(k)
                for k in range(4 * HEADS):
                    b, p = k // HEADS, k // (2 * HEADS)
                    if k + AHEAD < 4 * HEADS:
                        score(k + AHEAD)
                    turn(s, i, k)
                    if k >= 1:
                        mix(s, i, k - 1)
                    if b < 3 and k % HEADS == HEADS - 1:
                        values(s, i, b + 1)
                    if b >= 1 and k % HEADS == 2:
                        turn_shares(s, i, b - 1)
                    if b >= 1 and k % HEADS == 7:
                        project_out(s, i, b - 1)
                    if k % (2 * HEADS) == 12:
                        transposes(s, i, p)
                mix(s, i, 4 * HEADS - 1)
                turn_shares(s, i, 3)
                project_out(s, i, 3)

            transposes(0, 0, 0, first=True)
            for s in range(len(STAGES)):
                if s == 0:
                    pe.wait_ge(stage_done, FIRST_PIECES + RING)
                if s == 3:
                    pe.wait_ge(stage_done, len(pieces) + RING)
                with pe.Fori(0, GROUPS // 2) as i:
                    if kind(s) == "A":
                        attention(s, i)
                    else:
                        for p in range(2):
                            (ffn if kind(s) == "F" else experts)(s, i, p)


def kernel(**inputs):
    import numpy as np
    import concourse.bacc as bacc
    from concourse.bass_utils import run_bass_kernel_spmd as run

    g = {k: np.asarray(v) for k, v in inputs.items()}

    def stacked(b):
        return np.repeat(b.reshape(4, 4, 1, HD), 2, axis=2).reshape(4, P).T

    up = g["L1_ffn_w_up"].reshape(EXPERTS, C, 2, MJ, 2).transpose(1, 2, 3, 4, 0).reshape(C, 2 * MJ * P)
    down = g["L1_ffn_w_down"].reshape(EXPERTS, MJ, 2, C).transpose(1, 2, 0, 3).reshape(MJ * P, C)

    n = np.arange(P)
    bits = np.array([[bin(a & b).count("1") % 2 for b in range(P)] for a in range(P)])
    had = np.where(bits == 1, -1.0, 1.0) / np.sqrt(C)
    query, key = n[:, None], n[None, :]
    diagonal = np.where(np.abs(query - key) < WINDOW, 1.0 + ALPHA, 1.0)
    below = np.where(query + P - key < WINDOW, 1.0 + ALPHA, 1.0)
    f = np.float32
    arrays = {
        "x": g["L0_attn_hidden_states"].reshape(TOKENS, C),
        "fgate": g["L0_ffn_W_gate"].T, "fup": g["L0_ffn_W_up"].T, "fdown": g["L0_ffn_W_down"].T,
        "su_ug": g["L0_ffn_SU_ug"].reshape(CK, P).T, "su_dp": g["L0_ffn_SU_dp"].reshape(FJ, P).T,
        "ws_ug": np.concatenate([g["L0_ffn_Wscale_ug"][INTER:], g["L0_ffn_Wscale_ug"][:INTER]]),
        "ws_dp": g["L0_ffn_Wscale_dp"],
        "q0": g["L0_attn_w_q"].T, "o0": g["L0_attn_w_out"].T,
        "kd0": g["L0_attn_w_k_down"], "vd0": g["L0_attn_w_v_down"],
        "ql0": g["L0_attn_q_to_latent"].transpose(2, 0, 1).reshape(LATENT, C),
        "vu0": g["L0_attn_v_up"].transpose(1, 0, 2).reshape(LATENT, C),
        "q1": g["L1_attn_wq"].T, "k1": g["L1_attn_wk"].T, "v1": g["L1_attn_wv"].T, "o1": g["L1_attn_wo"].T,
        "bq": stacked(g["L1_attn_bq"]), "bk": stacked(g["L1_attn_bk"]), "bv": g["L1_attn_bv"], "bo": g["L1_attn_bo"],
        "mgate": g["L1_ffn_w_gate"], "mshup": g["L1_ffn_w_shared_up"], "mshdown": g["L1_ffn_w_shared_down"],
        "mup": up, "mdown": down,
        "had": had.astype(f), "ident": np.eye(P, dtype=f),
        "before": (query < key).astype(f),
        "bandm": np.concatenate([diagonal, below, diagonal], axis=1).astype(f),
        "causal": np.where(key > query, -1e30, 0.0).astype(f),
        "hilo": np.where(n % 32 < HD, 0.0, -1.0).reshape(P, 1).astype(f),
    }
    nc = bacc.Bacc("TRN2", target_bir_lowering=False, num_devices=1)
    feeds, args = {}, {}
    for name, a in arrays.items():
        a = np.ascontiguousarray(a)
        feeds[name + "_dram"] = a
        args[name] = nc.dram_tensor(name + "_dram", a.shape, mybir.dt.from_np(a.dtype), kind="ExternalInput").ap()
    out = nc.dram_tensor("out_dram", (TOKENS, C), mybir.dt.float32, kind="ExternalOutput").ap()
    build(nc, **args, out=out)
    got = run(nc, [feeds], core_ids=[0]).results[0]["out_dram"]
    return np.asarray(got).reshape(TOKENS // BATCH, BATCH, C)
```

```python
import concourse.bass as bass
from concourse import mybir
from contextlib import ExitStack

TOKENS, C = 2048, 256
BATCH = 256
INTER = 1024
HEADS, HD = 16, 16
LATENT = 64
EXPERTS, EH, CAP, TOPK = 64, 32, 128, 6
SHARED = 64
WINDOW, ALPHA = 64, 0.5
EPS = 1e-5

P = 128
CK = C // P
TILES = TOKENS // P
GROUP = 512
GT = GROUP // P
GROUPS = TOKENS // GROUP
FJ = INTER // P
MJ = EXPERTS * EH // P
KEYS = 3 * P
BIG = 3.0e38

STAGES = ["F", "A0", "F", "E", "A1", "E"]

USES = {
    "G": {"F": FJ, "A": 4 * 2 + 2 * HEADS, "E": MJ},
    "U": {"F": FJ, "A": 2 * HEADS, "E": MJ},
    "T": {"F": 2, "A": 8, "E": 6},
    "Tf": {"F": 0, "A": 6, "E": 4},
    "A": {"F": 2, "A": 2, "E": 2},
    "h": {"F": FJ, "A": 0, "E": MJ},
    "w": {"F": 0, "A": 0, "E": MJ},
    "head": {"F": 0, "A": 2 * HEADS, "E": 0},
    "quarter": {"F": 0, "A": 4, "E": 0},
    "half": {"F": 0, "A": 2, "E": 0},
    "moe": {"F": 0, "A": 0, "E": 1},
    "unit": {"F": 1, "A": 1, "E": 1},
}
BEFORE = {"U": 14, "T": 2}
N_T_STEPS = 3


def butterflies():
    where, spare, levels = [P * j for j in range(FJ)], [P * (FJ + j) for j in range(FJ // 2)], []
    for step in (1, 2, 4):
        level, freed = [], []
        for q, (a, b) in enumerate((a, a + step) for a in range(FJ) if not a & step):
            level.append((where[a], where[b], spare[q]))
            freed.append(where[b])
            where[b] = spare[q]
        levels.append(level)
        spare = freed
    return levels, where


BUTTERFLIES, CHUNK_AT = butterflies()


def build(nc, x, fgate, fup, fdown, su_ug, su_dp, ws_ug, ws_dp, q0, o0, kd0, vd0, ql0, vu0,
          q1, k1, v1, o1, bq, bk, bv, bo, mgate, mshup, mshdown, mup, mdown,
          had, ident, before, bandm, causal, hilo, out):
    F32, R32, BF16 = mybir.dt.float32, mybir.dt.float32r, mybir.dt.bfloat16
    I32 = mybir.dt.int32
    ALU, ACT, AX = mybir.AluOpType, mybir.ActivationFunctionType, mybir.AxisListType

    ctx = ExitStack()
    with ctx:
        def sb(name, shape, dt=F32):
            return ctx.enter_context(nc.sbuf_tensor(name, shape, dt))

        def sem(name):
            return ctx.enter_context(nc.semaphore(name))

        xs = sb("xs", [P, TILES * C])
        WA = sb("WA", [P, 12288], R32)
        WM = sb("WM", [P, 4 * MJ * P * CK], R32)
        WT = sb("WT", [P, 6144], R32)
        xn = sb("xn", [P, 2 * 2 * CK * GROUP], R32)
        WR = sb("WR", [P, 4096], R32)
        WF = sb("WF", [P, 3584])
        xh = sb("xh", [P, GT, C])
        aux = sb("aux", [P, 2 * C])
        identf = sb("identf", [P, P])
        hadf = xh[:, 2, :].rearrange("p (s n) -> p s n", s=2)
        identb = sb("identb", [P, P], BF16)
        beforeb = sb("beforeb", [P, P], BF16)
        onesb = sb("onesb", [P, P], BF16)
        causalb = sb("causalb", [P, P], BF16)
        countb = sb("countb", [P, EXPERTS], BF16)
        maskb = sb("maskb", [P, GT, EXPERTS], BF16)
        zero = sb("zero", [P, 1])
        quarter = sb("quarter", [P, 1])
        hilos = sb("hilos", [P, 1])
        suc = sb("suc", [P, CK + FJ])
        bqk = sb("bqk", [P, 2, 4])
        st = sb("st", [P, GT, 6])
        mv = sb("mv", [P, GT, 2])
        ve = sb("ve", [P, GT])
        y = sb("y", [P, GT])
        yt = sb("yt", [P, GT])
        nmax = sb("nmax", [P, 3, 2])
        den = sb("den", [P, 2, 2, HEADS])
        top = sb("top", [P, GT, 8])
        tot = sb("tot", [P, GT])
        row = xh[:, 3, :]

        fg = WA[:, 0:4096].rearrange("p (s c n) -> p s c n", s=2, c=CK)
        fu = WA[:, 4096:8192].rearrange("p (s c n) -> p s c n", s=2, c=CK)
        fd = WA[:, 8192:12288].rearrange("p (s j n) -> p s j n", s=2, j=FJ)
        md = WA[:, 0:8192].rearrange("p (s j n) -> p s j n", s=2, j=MJ)
        shu = WA[:, 8192:8704].rearrange("p (s c n) -> p s c n", s=2, c=CK)
        mg = WA[:, 8704:8960].rearrange("p (s c n) -> p s c n", s=2, c=CK)
        shd = WA[:, 8960:9472].rearrange("p (s n) -> p s n", s=2)
        mw = WM[:, :].rearrange("p (s c v j n) -> p s c v j n", s=2, c=CK, v=2, j=MJ)
        wq = WT[:, 0:2048].rearrange("p (s c n) -> p s c n", s=2, c=CK)
        wk = WT[:, 2048:4096].rearrange("p (s c n) -> p s c n", s=2, c=CK)
        wv = WT[:, 4096:5120].rearrange("p (s c n) -> p s c n", s=2, c=CK)
        wo = WT[:, 5120:6144].rearrange("p (s c n) -> p s c n", s=2, c=CK)
        xnv = xn[:, :].rearrange("p (b s c n) -> p b s c n", b=2, s=2, c=CK)
        hid = WR[:, 0:2048].rearrange("p (b s n) -> p b s n", b=2, s=2)
        shh = WR[:, 2048:3072].rearrange("p (s n) -> p s n", s=2)
        Qs = WR[:, 0:1024].rearrange("p (t n) -> p t n", t=4)
        KA = WR[:, 1024:2048].rearrange("p (t n) -> p t n", t=4)
        KB = WR[:, 2048:3072].rearrange("p (t n) -> p t n", t=4)
        cT = WR[:, 3072:4096].rearrange("p (s c n) -> p s c n", s=2, c=CK)
        sw = WF[:, 0:1024].rearrange("p (b n) -> p b n", b=2)
        wrep = WF[:, 1024:1536]
        sh = WF[:, 1536:2048]
        w2 = WF[:, 2048:2560].rearrange("p (t d e) -> p t d e", t=GT, d=2)
        lg = WF[:, 2560:2824].rearrange("p (t e) -> p t e", t=GT)
        lr = WF[:, 2824:3088].rearrange("p (t e) -> p t e", t=GT)
        sg = WF[:, 3088:3344].rearrange("p (t e) -> p t e", t=GT)
        Vs = WF[:, 0:1024].rearrange("p (t h n) -> p t h n", t=2, h=HEADS)
        Pr = WF[:, 1024:1792].rearrange("p (b n) -> p b n", b=2)
        PT = WF[:, 1792:2560].rearrange("p (b n) -> p b n", b=2)
        cn = xh[:, 0:2, :]
        sums = xh[:, 2:4, :].rearrange("p t n -> p (t n)")
        qf = WF[:, 2560:3072].rearrange("p (t n) -> p t n", t=2)
        kf = WF[:, 3072:3584].rearrange("p (t n) -> p t n", t=2)
        SLOT = 1536
        tmp = [WF[:, 3072:3584], xh[:, 0:2, :].rearrange("p a n -> p (a n)")]

        banks = [ctx.enter_context(nc.psum_tensor(f"bank{n}", [P, 512], F32)) for n in range(8)]

        def G(n): return banks[n % 2]
        def U(n): return banks[2 + n % 2]
        def T(n): return banks[4 + n % 2]
        def A(n): return banks[6 + n % 2]

        def S(n): return banks[(0, 1, 3)[n % 3]]
        TURNED = (banks[2], banks[7])
        SUMS = banks[6]

        AHEAD = 2
        PARTS_BEFORE = {0: [(0, 0), (1, 0)], 1: [(0, 1)], 2: [(1, 1)], 9: [(0, 2)], 10: [(1, 2)], 17: [(0, 3)], 18: [(1, 3)],
                        26: [(0, 4)], 27: [(1, 4)], 33: [(0, 5)], 34: [(1, 5)], 41: [(0, 6)], 42: [(1, 6)],
                        49: [(0, 7)], 50: [(1, 7)]}
        ORDER = []
        for k in range(4 * HEADS):
            ORDER += PARTS_BEFORE.get(k, []) + [k]
        VALUES_T, CONTEXT_T, OUTPUT_T, NORM_T = (0, 3, 6, 11), (4, 7, 12, 14), (5, 8, 13, 15), (1, 9)
        VALUES_TF, CONTEXT_TF, OUTPUT_TF = (0, 1, 4, 7), (2, 5, 8, 10), (3, 6, 9, 11)

        def score_use(item):
            return ORDER.index(item)

        consts = sem("consts")
        xload = sem("xload")
        set_up = sem("set_up")
        cast = sem("cast")
        stage_full = [sem("stage_full0"), sem("stage_full1")]
        late_full = [sem("late_full0"), sem("late_full1"), sem("late_full2")]
        stage_done = sem("stage_done")
        side_full = [sem("side_full0"), sem("side_full1")]
        side_done = sem("side_done")
        next_full, next_done = sem("next_full"), sem("next_done")
        w_high = sem("w_high")
        weights = sem("weights")
        g_full, g_done = sem("g_full"), sem("g_done")
        u_full, u_done = sem("u_full"), sem("u_done")
        t_full, t_done = sem("t_full"), sem("t_done")
        a_done = sem("a_done")
        stats = sem("stats")
        rstd = sem("rstd")
        xh_full, xh_read = sem("xh_full"), sem("xh_read")
        xn_high = sem("xn_high")
        xn_read = sem("xn_read")
        h_high = sem("h_high")
        h_ready = sem("h_ready")
        h_read = sem("h_read")
        weighted = sem("weighted")
        chosen = sem("chosen")
        sigm = sem("sigm")
        wmade = sem("wmade")
        sh_act, sh_high, sh_ready = sem("sh_act"), sem("sh_high"), sem("sh_ready")
        q_high = sem("q_high")
        q_ready, k_ready = sem("q_ready"), sem("k_ready")
        maxed = sem("maxed")
        pv_done = sem("pv_done")
        shared = sem("shared")
        ctx_made = sem("ctx_made")
        ctx_high = sem("ctx_high")
        stored = sem("stored")
        banded = sem("banded")
        scaled = sem("scaled")
        auxl = sem("auxl")

        RING = 2

        def kind(s):
            return STAGES[s][0]

        def base(what, s):
            return BEFORE.get(what, 0) + GROUPS * sum(USES[what][kind(r)] for r in range(s))

        def at(what, s, i, p, n=0):
            per = USES[what][kind(s)]
            return i * (2 * per) + (base(what, s) + p * per + n)

        def static(what, s, p, n=0):
            return base(what, s) + p * USES[what][kind(s)] + n

        def filled(index, k=1):
            return index + k

        def free(index):
            return index + 1

        def made(index):
            return index + 1 + RING

        def score_free(s, i, n):
            return at("G", s, i, 0, max(0, n - 3 + 1)) + RING

        def norm_use(s, p):
            return {"F": (p, 0), "A": (0, NORM_T[p]), "E": (p, 4)}[kind(s)]

        def group(i, p):
            return i * 2 + p

        def following(i, p):
            return i * 2 + 1 if p == 0 else 2 - i * 2

        def xt(g, t, n=1):
            return xs[:, bass.ds(g * (GT * C) + t * C, n * C)]

        block = ctx.enter_context(nc.Block())

        def spread(src, lo, n):
            return src[lo:lo + n].partition_broadcast(P)

        pieces = []
        for m, w in ((0, fgate), (1, fup)):
            for jh in range(2):
                pieces.append([(0, 1024, P, w.rearrange("(c p) n -> p c n", p=P)[:, :, jh * 512:(jh + 1) * 512]),
                               (1024, 512, P, spread(ws_ug, m * INTER + jh * 512, 512))])
        for ch in range(2):
            pieces.append([(0, 1024, P, fdown.rearrange("(j p) n -> p j n", p=P)[:, :, ch * P:(ch + 1) * P]),
                           (1024, P, P, spread(ws_dp, ch * P, P))])
        pieces.append([(0, 512, P, q0.rearrange("(c p) n -> p c n", p=P)),
                       (512, 512, P, o0.rearrange("(c p) n -> p c n", p=P))])
        pieces.append([(k * C, C, LATENT, w) for k, w in enumerate((kd0, vd0, ql0, vu0))])
        FIRST_PIECES = len(pieces)
        pieces.append([(0, 256, P, mshup.rearrange("(c p) n -> p c n", p=P)),
                       (256, 128, P, mgate.rearrange("(c p) n -> p c n", p=P)),
                       (384, 256, SHARED, mshdown)])
        mdv = mdown.rearrange("(j p) n -> p j n", p=P)
        for k in range(4):
            pieces.append([(0, 1024, P, mdv[:, 4 * k:4 * k + 4, :])])
        side = [WF[:, 1024:2048], WF[:, 2048:3072]]
        LATE = (side[1], side[0], WF[:, 0:1024])

        def slot(n):
            if n >= FIRST_PIECES:
                return LATE[(n - FIRST_PIECES) % 3]
            return WF[:, (n % 2) * SLOT:(n % 2 + 1) * SLOT]

        def landed(n):
            return late_full[(n - FIRST_PIECES) % 3] if n >= FIRST_PIECES else stage_full[n % 2]

        def stage_value(n):
            if n >= FIRST_PIECES:
                return 16 * sum(len(pieces[m]) for m in range(FIRST_PIECES, n + 1) if (m - n) % 3 == 0)
            return 16 * sum(len(pieces[m]) for m in range(n % 2, n + 1, 2))

        def load_piece(eng, n):
            for lo, w, parts, src in pieces[n]:
                dst = slot(n)[0:parts, lo:lo + w]
                if len(src.shape) == 3:
                    dst = dst.rearrange("p (a n) -> p a n", a=src.shape[1])
                eng.dma_start(dst, src).then_inc(landed(n), 16)

        def load_pieces(eng, first, last):
            for n in range(first, last):
                eng.wait_ge(stage_done, free(n))
                load_piece(eng, n)

        def three(v, a):
            return v.rearrange("p (a n) -> p a n", a=a)

        def doubled(w, c):
            return [w[:, s, c, :].rearrange("p (h r d) -> p h r d", h=HEADS, r=2) for s in range(2)]

        def splits(n):
            v = slot(n)
            if n == 6:
                q, o = v[:, 0:512], v[:, 512:1024]
                todo = []
                for c in range(CK):
                    sv = q[:, c * C:(c + 1) * C].rearrange("p (h d) -> p h d", h=HEADS)
                    hi, lo = doubled(wq, c)
                    for r in range(2):
                        todo.append((sv, hi[:, :, r, :], lo[:, :, r, :], 0.125))
                todo.append((three(o, CK), wo[:, 0, :, :], wo[:, 1, :, :], 1.0))
                return todo
            if n > FIRST_PIECES:
                k = n - FIRST_PIECES - 1
                hi, lo = (md[:, s, 4 * k:4 * k + 4, :].rearrange("p j n -> p (j n)") for s in range(2))
                return [(v[:, 0:1024], hi, lo, 0.5)]
            return [(three(v[:, 0:256], CK), shu[:, 0, :, :], shu[:, 1, :, :], 1.0),
                    (three(v[:, 256:384], CK), mg[:, 0, :, :], mg[:, 1, :, :], 1.0),
                    (v[0:SHARED, 384:640], shd[0:SHARED, 0, :], shd[0:SHARED, 1, :], 0.5)]

        DERIVED = [2, 2, 2, 2, 8, 8, None, 8]

        def highs(n):
            return sum((DERIVED[m] if m < 8 and m != 6 else len(splits(m))) for m in range(n))

        def split_high(eng, n):
            eng.wait_ge(landed(n), stage_value(n))
            for src, hi, lo, scale in splits(n):
                eng.activation(hi, src, ACT.Copy, scale=scale).then_inc(w_high, 1)

        def split_low(eng, n):
            todo = splits(n)
            for k, (src, hi, lo, scale) in enumerate(todo):
                eng.wait_ge(w_high, highs(n) + k + 1)
                ins = eng.scalar_tensor_tensor(lo, src, scale, hi.bitcast(F32), ALU.mult, ALU.subtract)
            ins.then_inc(stage_done, 1)

        @block.sync
        def _(sp):
            sp.dma_start(identf[:, :], ident).then_inc(consts, 16)
            sp.dma_start(hadf[:, 0, :], had).then_inc(consts, 16)
            sp.dma_start(aux[:, 0:KEYS], bandm).then_inc(consts, 16)
            sp.dma_start(hilos[:, :], hilo).then_inc(consts, 16)
            sp.dma_start(suc[:, 0:CK], su_ug).then_inc(consts, 16)
            sp.dma_start(suc[:, CK:CK + FJ], su_dp).then_inc(consts, 16)
            sp.dma_start(xh[:, 0, 0:P], before).then_inc(consts, 16)
            sp.dma_start(xh[:, 0, P:2 * P], causal).then_inc(consts, 16)
            load_pieces(sp, 0, 2)
            sp.dma_start(xs[:, :].rearrange("p (t n) -> p t n", t=TILES),
                         x.rearrange("(t p) n -> p t n", p=P)).then_inc(xload, 16)
            load_pieces(sp, 2, FIRST_PIECES)
            sp.wait_ge(stage_done, FIRST_PIECES + RING)
            with sp.Fori(0, CK) as i:
                for k in range(4):
                    sp.wait_ge(side_done, i * 4 + (k + 1))
                    sp.dma_start(side[k % 2], mup[bass.ds(i * P, P), k * 1024:(k + 1) * 1024]).then_inc(side_full[k % 2], 16)
            if len(STAGES) > 2:
                sp.wait_ge(t_done, made(base("T", 2) - 1))
                sp.dma_start(aux[:, 0:C], bv.partition_broadcast(P)).then_inc(auxl, 16)
                sp.dma_start(aux[:, C:2 * C], bo.partition_broadcast(P)).then_inc(auxl, 16)
                sp.dma_start(bqk[:, 0, :], bq).then_inc(auxl, 16)
                sp.dma_start(bqk[:, 1, :], bk).then_inc(auxl, 16)
                load_piece(sp, FIRST_PIECES)
                with sp.Fori(0, CK) as i:
                    sp.wait_ge(next_done, i + 1)
                    for m, w in enumerate((q1, k1, v1, o1)):
                        sp.dma_start(side[0][:, m * C:(m + 1) * C], w[bass.ds(i * P, P), :]).then_inc(next_full, 16)
            if len(STAGES) > 3:
                sp.wait_ge(next_done, CK + 1)
                load_piece(sp, FIRST_PIECES + 1)
                sp.wait_ge(a_done, made(base("A", 3) - 1))
                load_piece(sp, FIRST_PIECES + 2)
                for n in range(FIRST_PIECES + 3, len(pieces)):
                    sp.wait_ge(stage_done, free(n - 1))
                    load_piece(sp, n)
            s = len(STAGES) - 1
            outv = out.rearrange("(t p) n -> p t n", p=P)
            per = USES["A"][kind(s)]
            with sp.Fori(0, GROUPS // 2) as i:
                for p in range(2):
                    if kind(s) == "A":
                        sp.wait_ge(t_done, made(at("T", s, i, 0, OUTPUT_T[2 * p + 1])))
                    else:
                        sp.wait_ge(a_done, made(at("A", s, i, p, per - 1)))
                    sp.dma_start(outv[:, bass.ds(group(i, p) * GT, GT), :],
                                 xt(group(i, p), 0, GT).rearrange("p (t n) -> p t n", t=GT)).then_inc(stored, 16)
            sp.wait_ge(stored, 16 * GROUPS)

        @block.gpsimd
        def _(pool):
            pool.memset(onesb[:, :], 1.0)
            pool.memset(bqk[:, :, :], 0.0)
            pool.memset(zero[:, :], 0.0)
            pool.memset(quarter[:, :], 0.25)
            pool.memset(yt[:, :], 1.0).then_inc(set_up, 1)
            pool.wait_ge(consts, 16 * 8)

            def newton(s, i, p):
                pool.wait_ge(stats, filled(at("unit", s, i, p) + 1))
                for _ in range(N_T_STEPS):
                    pool.tensor_tensor(yt[:, :], y[:, :], y[:, :], ALU.mult)
                    pool.drain()
                    pool.tensor_tensor(yt[:, :], yt[:, :], ve[:, :], ALU.mult)
                    pool.drain()
                    pool.tensor_scalar(yt[:, :], yt[:, :], -0.5, 1.5, ALU.mult, ALU.add)
                    pool.drain()
                    last = pool.tensor_tensor(y[:, :], y[:, :], yt[:, :], ALU.mult)
                    if _ < N_T_STEPS - 1:
                        pool.drain()
                last.then_inc(rstd, 1)
                pool.drain()

            def stack(s, i, q):
                pair = slice(2 * (q % 2), 2 * (q % 2) + 2)
                pool.wait_ge(g_done, made(at("G", s, i, 0, score_use((0, q)))))
                pool.tensor_tensor(Qs[:, pair, :], qf[:, :, :], zero[:, 0:1].unsqueeze(2).broadcast_to([P, 2, C]), ALU.add)\
                    .then_inc(q_high, 1)
                pool.wait_ge(g_done, made(at("G", s, i, 0, score_use((1, q)))))
                pool.tensor_tensor(KA[:, pair, :], kf[:, :, :], zero[:, 0:1].unsqueeze(2).broadcast_to([P, 2, C]), ALU.add)
                pool.drain()
                pool.tensor_tensor(KB[:, pair, :], kf[:, :, :], KA[:, pair, :].bitcast(F32), ALU.subtract)\
                    .then_inc(k_ready, 1)

            def spread_over(column, n):
                return column[:, 0:1].broadcast_to([P, n])

            def halves(hi, lo, src, shape):
                z = zero[:, 0:1].unsqueeze(2).broadcast_to(shape) if len(shape) == 3 else spread_over(zero, shape[1])
                pool.tensor_tensor(hi, src, z, ALU.add)
                pool.drain()
                return pool.tensor_tensor(lo, src, hi.bitcast(F32), ALU.subtract)

            def split_up(i, k):
                pool.wait_ge(side_full[k % 2], i * 32 + 16 * (k // 2 + 1))
                half = 2 * MJ * P * CK
                hi, lo = (WM[:, bass.ds(i * (half // CK) + s * half + k * 1024, 1024)] for s in range(2))
                halves(hi, lo, side[k % 2], [P, 1024]).then_inc(side_done, 1)

            def split_next(i):
                src = [side[0][:, m * C:(m + 1) * C] for m in range(4)]
                pool.wait_ge(next_full, i * 64 + 64)
                pool.tensor_tensor(src[0], src[0], spread_over(quarter, C), ALU.mult)
                pool.drain()
                for m in range(2):
                    sv = src[m].rearrange("p (h d) -> p h d", h=HEADS)
                    hi, lo = (WT[:, bass.ds(i * 512 + (m * 2048 + s * 1024), 512)]
                              .rearrange("p (h r d) -> p h r d", h=HEADS, r=2) for s in range(2))
                    for r in range(2):
                        halves(hi[:, :, r, :], lo[:, :, r, :], sv, [P, HEADS, HD])
                for m in range(2):
                    hi, lo = (WT[:, bass.ds(i * C + (4096 + m * 1024 + s * 512), C)] for s in range(2))
                    last = halves(hi, lo, src[2 + m], [P, C])
                last.then_inc(next_done, 1)

            newton(0, 0, -1)
            for s in range(len(STAGES)):
                with pool.Fori(0, GROUPS // 2) as i:
                    for p in range(2):
                        if kind(s) == "A":
                            stack(s, i, 4 * p)
                            stack(s, i, 4 * p + 1)
                        newton(s, i, p)
                        if s == 0:
                            split_up(i, 2 * p)
                            split_up(i, 2 * p + 1)
                        if s == 2 and p == 0:
                            split_next(i)
                        if kind(s) == "A":
                            stack(s, i, 4 * p + 2)
                            stack(s, i, 4 * p + 3)

        def normalise(s, i, p, first=False):
            return 0 if first else at("unit", s, i, p) + 1

        @block.scalar
        def _(act):
            act.wait_ge(consts, 16 * 8)
            act.activation(identb[:, :], identf[:, :], ACT.Copy)
            act.activation(beforeb[:, :], xh[:, 0, 0:P], ACT.Copy)
            act.activation(causalb[:, :], xh[:, 0, P:2 * P], ACT.Copy)
            act.activation(hadf[:, 1, :], hadf[:, 0, :], ACT.Copy, scale=-1.0).then_inc(cast, 1)
            act.wait_ge(set_up, 1)

            for n in range(4):
                m, jh = n // 2, n % 2
                w = fg if m == 0 else fu
                for c in range(CK):
                    k = 2 * n + c
                    act.wait_ge(u_done, made(k))
                    act.activation(w[:, 0, c, jh * 512:(jh + 1) * 512], tmp[k % 2], ACT.Copy).then_inc(w_high, 1)
            for ch in range(2):
                for j in range(FJ):
                    if j % 4 == 0:
                        act.wait_ge(scaled, 2 * ch + j // 4 + 1)
                    act.activation(fd[:, 0, j, ch * P:(ch + 1) * P], tmp[j // 4][:, (j % 4) * P:(j % 4 + 1) * P],
                                   ACT.Copy, scale=suc[:, CK + j:CK + j + 1]).then_inc(w_high, 1)
            split_high(act, 6)
            for m in range(2):
                act.wait_ge(u_full, 12 + m + 1)
                for c in range(CK):
                    src = U(12 + m)[:, c * C:(c + 1) * C]
                    if m == 0:
                        hi = doubled(wk, c)[0]
                        for r in range(2):
                            act.activation(hi[:, :, r, :], src.rearrange("p (h d) -> p h d", h=HEADS), ACT.Copy)\
                               .then_inc(w_high, 1)
                    else:
                        for r in range(2):
                            act.activation(wv[:, 0, c, r * P:(r + 1) * P], src[:, r * P:(r + 1) * P], ACT.Copy)\
                               .then_inc(w_high, 1)
            def xn_highs(s, i, p, first=False):
                v = 0 if first else at("unit", s, i, p) + 1
                buf = 0 if first else (p + 1) % 2
                tn = 0 if first else static("T", s, *norm_use(s, p))
                act.wait_ge(xh_read, made(v * GT + GT - 1))
                act.wait_ge(xn_read, free(v))
                for c in range(CK):
                    act.activation(xnv[:, buf, 0, c, :], T(tn + c)[:, :], ACT.Copy).then_inc(xn_high, 1)

            def chunk(s, i, p, j):
                n, h = at("G", s, i, p, j), at("h", s, i, p, j)
                ns, b = static("G", s, p, j), static("h", s, p, j) % 2
                act.wait_ge(g_full, filled(n))
                act.wait_ge(h_ready, free(h))
                act.activation(sw[:, b, :], G(ns)[:, :], ACT.Silu).then_inc(g_done, 1)

            def chunk_high(s, i, p, j):
                h, b = at("h", s, i, p, j), static("h", s, p, j) % 2
                if kind(s) == "F":
                    act.wait_ge(u_done, made(at("U", s, i, p, j)))
                else:
                    act.wait_ge(weighted, filled(at("w", s, i, p, j)))
                act.wait_ge(h_read, free(h))
                act.activation(hid[:, b, 0, :], sw[:, b, :], ACT.Copy).then_inc(h_high, 1)

            def ffn(s, i, p):
                for j in range(FJ):
                    chunk(s, i, p, j)
                    chunk_high(s, i, p, j)
                    if j == 5:
                        xn_highs(s, i, p)

            def experts(s, i, p):
                act.wait_ge(t_done, made(at("T", s, i, p, 0)))
                act.activation(sg[:, :, :], lg[:, :, 0:EXPERTS], ACT.Sigmoid).then_inc(sigm, 1)
                act.wait_ge(t_full, filled(at("Tf", s, i, p, 1)))
                act.activation(sh[0:SHARED, :], T(static("T", s, p, 1))[SHARED:2 * SHARED, :], ACT.Silu)\
                   .then_inc(sh_act, 1)
                act.wait_ge(t_done, made(at("T", s, i, p, 1)))
                act.activation(shh[0:SHARED, 0, :], sh[0:SHARED, :], ACT.Copy).then_inc(sh_high, 1)
                for j in range(MJ):
                    chunk(s, i, p, j)
                    chunk_high(s, i, p, j)
                    if j == 12:
                        xn_highs(s, i, p)

            def projected(s, i, item):
                m, q = item
                n = score_use(item)
                act.wait_ge((q_ready, k_ready)[m], free(at("quarter", s, i, 0, q)))
                act.wait_ge(g_full, filled(at("G", s, i, 0, n)))
                for t in range(2):
                    col = 2 * (q % 2) + t
                    ins = act.activation((qf, kf)[m][:, t, :], S(n)[:, t * C:(t + 1) * C], ACT.Identity,
                                         bias=bqk[:, m, col:col + 1])
                ins.then_inc(g_done, 1)

            def exps(s, i, k):
                sc = S(score_use(k))
                b, h = k // HEADS % 2, k % HEADS
                act.wait_ge(maxed, filled(at("head", s, i, 0, k)))
                act.wait_ge(u_full, at("U", s, i, 0, k) - 1)
                act.activation(Pr[:, k % 2, 0:P], sc[:, 0:P], ACT.Exp, bias=nmax[:, k % 3, 0:1],
                               accum_out=den[:, b, 0, h:h + 1])
                act.activation(Pr[:, k % 2, P:KEYS], sc[:, P:KEYS], ACT.Exp, bias=nmax[:, k % 3, 1:2],
                               accum_out=den[:, b, 1, h:h + 1]).then_inc(g_done, 1)

            def ctx_highs(s, i, b):
                act.wait_ge(ctx_made, filled(at("half", s, i, 0, b)))
                act.activation(cT[:, 0, :, :].rearrange("p c n -> p (c n)"), cn.rearrange("p t n -> p (t n)"),
                               ACT.Copy).then_inc(ctx_high, 1)

            def evacuate(s, i, k):
                act.wait_ge(u_full, filled(at("U", s, i, 0, k)))
                act.wait_ge(pv_done, free(at("head", s, i, 0, k)))
                act.activation(PT[:, k % 2, :], TURNED[k % 2][:, 0:KEYS], ACT.Copy).then_inc(u_done, 1)

            def attention(s, i):
                for k in range(4 * HEADS):
                    if k == 0:
                        for item in PARTS_BEFORE[0]:
                            projected(s, i, item)
                    exps(s, i, k)
                    for item in PARTS_BEFORE.get(k + 1, []):
                        projected(s, i, item)
                    if STAGES[s] == "A0" and k >= 1:
                        evacuate(s, i, k - 1)
                    if k >= HEADS and k % HEADS == 6:
                        ctx_highs(s, i, k // HEADS - 1)
                    if k % (2 * HEADS) == 14:
                        xn_highs(s, i, k // (2 * HEADS))
                if STAGES[s] == "A0":
                    evacuate(s, i, 4 * HEADS - 1)
                ctx_highs(s, i, 3)

            xn_highs(0, 0, 0, first=True)
            for s in range(len(STAGES)):
                if s == 1:
                    act.wait_ge(side_done, 4 * CK + RING)
                if s == 3:
                    for n in range(FIRST_PIECES, len(pieces)):
                        split_high(act, n)
                if STAGES[s] == "A1":
                    act.wait_ge(auxl, 64)
                    act.activation(bqk[:, 0, :], bqk[:, 0, :], ACT.Copy, scale=0.25)
                    act.drain()
                with act.Fori(0, GROUPS // 2) as i:
                    if kind(s) == "A":
                        attention(s, i)
                    else:
                        for p in range(2):
                            (ffn if kind(s) == "F" else experts)(s, i, p)

        @block.vector
        def _(dve):
            for ring in (g_done, u_done, t_done, a_done, xh_read, xn_read, h_ready, h_read, pv_done, stage_done, side_done):
                dve.sem_inc(ring, RING)
            dve.sem_inc(q_ready, 1)
            dve.sem_inc(k_ready, 1)
            dve.sem_inc(next_done, 1)
            dve.memset(countb[:, :], 0.0)

            def tile_stats(g, t):
                dve.bn_stats(st[:, t, :], xt(g, t))

            def seeds():
                dve.drain()
                for t in range(GT):
                    dve.bn_aggr(mv[:, t, :], st[:, t, :])
                dve.drain()
                dve.tensor_scalar(ve[:, :], mv[:, :, 1], EPS, None, ALU.add)
                dve.drain()
                dve.tensor_scalar(y[:, :].bitcast(I32), ve[:, :].bitcast(I32), 1, None, ALU.arith_shift_right)
                dve.drain()
                dve.tensor_scalar(y[:, :].bitcast(I32), y[:, :].bitcast(I32), -1.0, float(0x5F3759DF),
                                  ALU.mult, ALU.add).then_inc(stats, 1)

            def group_stats(g):
                dve.drain()
                for t in range(GT):
                    tile_stats(g, t)
                seeds()

            def scale_up(n):
                m, jh = n // 2, n % 2
                w = fg if m == 0 else fu
                for c in range(CK):
                    k = 2 * n + c
                    dve.wait_ge(u_full, k + 1)
                    if c == 0:
                        dve.wait_ge(stage_full[n % 2], stage_value(n))
                    dve.scalar_tensor_tensor(tmp[k % 2], U(k)[:, :], suc[:, c:c + 1], slot(n)[:, 1024:SLOT],
                                             ALU.mult, ALU.mult).then_inc(u_done, 1)
                    dve.wait_ge(w_high, k + 1)
                    ins = dve.tensor_tensor(w[:, 1, c, jh * 512:(jh + 1) * 512], tmp[k % 2],
                                            w[:, 0, c, jh * 512:(jh + 1) * 512].bitcast(F32), ALU.subtract)
                ins.then_inc(stage_done, 1)

            dve.wait_ge(consts, 16 * 8)
            dve.wait_ge(cast, 1)
            for n in range(4):
                scale_up(n)

            for ch in range(2):
                n = 4 + ch
                v = slot(n)
                dve.wait_ge(stage_full[n % 2], stage_value(n))
                dve.tensor_copy(row[:, ch * P:(ch + 1) * P], v[:, 1024:1024 + P])
                dve.drain()
                for level in BUTTERFLIES:
                    for a, b, d in level:
                        dve.tensor_tensor(v[:, d:d + P], v[:, a:a + P], v[:, b:b + P], ALU.subtract)
                    dve.drain()
                    for a, b, d in level:
                        ins = dve.tensor_tensor(v[:, a:a + P], v[:, a:a + P], v[:, b:b + P], ALU.add)
                    if level is not BUTTERFLIES[-1]:
                        dve.drain()
                ins.then_inc(weights, 1)
            for ch in range(2):
                for half in range(2):
                    bank = 8 + 2 * ch + half
                    dve.wait_ge(u_full, bank + 1)
                    if ch == 1:
                        dve.wait_ge(w_high, 8 + 4 * half + 4)
                        dve.drain()
                    dve.scalar_tensor_tensor(three(tmp[half], 4), three(U(bank)[:, :], 4), 0.25,
                                             row[:, ch * P:(ch + 1) * P].unsqueeze(1).broadcast_to([P, 4, P]),
                                             ALU.mult, ALU.mult).then_inc(scaled, 1)
                for half in range(2):
                    for q in range(4):
                        j = 4 * half + q
                        dve.wait_ge(w_high, 8 + 8 * ch + j + 1)
                        ins = dve.scalar_tensor_tensor(fd[:, 1, j, ch * P:(ch + 1) * P], tmp[half][:, q * P:(q + 1) * P],
                                                       suc[:, CK + j:CK + j + 1],
                                                       fd[:, 0, j, ch * P:(ch + 1) * P].bitcast(F32),
                                                       ALU.mult, ALU.subtract)
                    ins.then_inc(u_done, 1)
                dve.drain()
                dve.sem_inc(stage_done, 1)
            dve.wait_ge(xload, 16)
            group_stats(0)
            split_low(dve, 6)
            for m in range(2):
                for c in range(CK):
                    src = U(12 + m)[:, c * C:(c + 1) * C]
                    for r in range(2):
                        dve.wait_ge(w_high, highs(7) + 4 * m + 2 * c + r + 1)
                        if c == 0 and r == 0:
                            dve.wait_ge(w_high, highs(7) + 4 * m + 4)
                        if m == 0:
                            hi, lo = doubled(wk, c)
                            ins = dve.tensor_tensor(lo[:, :, r, :], src.rearrange("p (h d) -> p h d", h=HEADS),
                                                    hi[:, :, r, :].bitcast(F32), ALU.subtract)
                        else:
                            ins = dve.tensor_tensor(wv[:, 1, c, r * P:(r + 1) * P], src[:, r * P:(r + 1) * P],
                                                    wv[:, 0, c, r * P:(r + 1) * P].bitcast(F32), ALU.subtract)
                ins.then_inc(u_done, 1)
            dve.drain()
            dve.sem_inc(stage_done, 1)
            QUERIES_AT = {2: 1, 10: 2, 19: 3, 28: 4, 35: 5, 42: 6, 51: 7}

            def xhats(s, i, p, first=False, tiles=range(GT)):
                v = 0 if first else at("unit", s, i, p) + 1
                g = 0 if first else following(i, p)
                dve.wait_ge(xh_read, v * GT + RING)
                dve.wait_ge(rstd, v + 1)
                for t in tiles:
                    dve.tensor_scalar(xh[:, t, :], xt(g, t), mv[:, t, 0:1], y[:, t:t + 1],
                                      ALU.subtract, ALU.mult).then_inc(xh_full, 1)

            def xn_lows(s, i, p, first=False, chunks=range(CK)):
                v = 0 if first else at("unit", s, i, p) + 1
                buf = 0 if first else (p + 1) % 2
                tn = 0 if first else static("T", s, *norm_use(s, p))
                for c in chunks:
                    dve.wait_ge(xn_high, v * CK + c + 1)
                    dve.tensor_tensor(xnv[:, buf, 1, c, :], T(tn + c)[:, :], xnv[:, buf, 0, c, :].bitcast(F32),
                                      ALU.subtract).then_inc(t_done, 1)

            def product(s, i, p, j):
                n, b = static("U", s, p, j), static("h", s, p, j) % 2
                dve.wait_ge(g_done, made(at("G", s, i, p, j)))
                dve.wait_ge(u_full, filled(at("U", s, i, p, j)))
                dve.tensor_tensor(sw[:, b, :], sw[:, b, :], U(n)[:, :], ALU.mult).then_inc(u_done, 1)

            def low(s, i, p, j):
                b = static("h", s, p, j) % 2
                dve.wait_ge(h_high, filled(at("h", s, i, p, j)))
                dve.tensor_tensor(hid[:, b, 1, :], sw[:, b, :], hid[:, b, 0, :].bitcast(F32), ALU.subtract)\
                   .then_inc(h_ready, 1)

            def residual(s, i, p, n, pair):
                dve.wait_ge(h_read, made(at("h", s, i, p, USES["h"][kind(s)] - 1)))
                dve.tensor_tensor(xt(group(i, p), 2 * pair, 2), xt(group(i, p), 2 * pair, 2),
                                  A(static("A", s, p, n))[:, :], ALU.add).then_inc(a_done, 1)

            def ffn(s, i, p):
                for j in range(FJ):
                    product(s, i, p, j)
                    low(s, i, p, j)
                    if j == 0 and p == 1:
                        residual(s, i, 0, 0, 0)
                        residual(s, i, 0, 1, 1)
                    if j == 1:
                        group_stats(following(i, p))
                    if j == 3:
                        xhats(s, i, p)
                    if j == 5:
                        xn_lows(s, i, p)
                if p == 1:
                    residual(s, i, p, 0, 0)
                    residual(s, i, p, 1, 1)

            def route(s, i, p):
                dve.drain()
                dve.memset(lg[:, :, EXPERTS:EXPERTS + 2], BIG)
                dve.wait_ge(t_full, filled(at("Tf", s, i, p, 0)))
                dve.tensor_scalar(lg[:, :, 0:EXPERTS], three(T(static("T", s, p, 0))[:, 0:GT * EXPERTS], GT), 17.5, None,
                                  ALU.min).then_inc(t_done, 1)
                dve.drain()
                for t in range(GT):
                    dve.max(top[:, t, :], lg[:, t, :])
                dve.drain()
                for t in range(GT):
                    dve.match_replace(out=lr[:, t, :], in_to_replace=top[:, t, :], in_values=lg[:, t, :],
                                      imm_value=-BIG)
                dve.drain()
                dve.tensor_tensor(maskb[:, :, :], lr[:, :, 0:EXPERTS], lg[:, :, 0:EXPERTS], ALU.not_equal)\
                   .then_inc(chosen, 1)

            def share(s, i, p):
                dve.wait_ge(sh_act, filled(at("moe", s, i, p)))
                dve.tensor_tensor(sh[0:SHARED, :], sh[0:SHARED, :], T(static("T", s, p, 1))[0:SHARED, :], ALU.mult)\
                   .then_inc(t_done, 1)

            def share_low(s, i, p):
                dve.wait_ge(sh_high, filled(at("moe", s, i, p)))
                dve.tensor_tensor(shh[0:SHARED, 1, :], sh[0:SHARED, :], shh[0:SHARED, 0, :].bitcast(F32), ALU.subtract)\
                   .then_inc(sh_ready, 1)

            def weigh(s, i, p):
                dve.wait_ge(sigm, filled(at("moe", s, i, p)))
                dve.tensor_tensor(sg[:, :, :], sg[:, :, :], maskb[:, :, :], ALU.mult)
                dve.drain()
                dve.tensor_reduce(tot[:, :], sg[:, :, :], AX.X, ALU.add)
                dve.drain()
                dve.reciprocal(tot[:, :], tot[:, :])
                dve.drain()
                dve.tensor_tensor(sg[:, :, :], sg[:, :, :], tot[:, :].unsqueeze(2).broadcast_to([P, GT, EXPERTS]), ALU.mult)
                dve.drain()
                dve.wait_ge(t_full, filled(at("Tf", s, i, p, 2)))
                pos = three(T(static("T", s, p, 2))[:, 0:GT * EXPERTS], GT)
                for d in range(2):
                    ins = dve.scalar_tensor_tensor(w2[:, :, d, :], pos, float(CAP), sg[:, :, :], ALU.is_lt, ALU.mult)
                ins.then_inc(t_done, 1)
                dve.tensor_reduce(lr[:, 0, 0:EXPERTS], maskb[:, :, :].rearrange("p t e -> p e t"), AX.X, ALU.add)
                dve.drain()
                dve.tensor_tensor(countb[:, :], countb[:, :], lr[:, 0, 0:EXPERTS], ALU.add).then_inc(wmade, 1)

            def weights_across(s, i, p):
                dve.wait_ge(t_full, filled(at("Tf", s, i, p, 3)))
                dve.tensor_copy(wrep, T(static("T", s, p, 3))[:, :]).then_inc(t_done, 1)
                dve.drain()

            def experts(s, i, p):
                route(s, i, p)
                if p == 1:
                    residual(s, i, 0, 0, 0)
                    residual(s, i, 0, 1, 1)
                share(s, i, p)
                share_low(s, i, p)
                weigh(s, i, p)
                weights_across(s, i, p)
                for j in range(MJ):
                    b = static("h", s, p, j) % 2
                    product(s, i, p, j)
                    dve.wait_ge(u_done, made(at("U", s, i, p, j)))
                    dve.tensor_tensor(sw[:, b, :], sw[:, b, :], wrep, ALU.mult).then_inc(weighted, 1)
                    low(s, i, p, j)
                    if j == 6:
                        group_stats(following(i, p))
                    if j == 9:
                        xhats(s, i, p)
                    if j == 12:
                        xn_lows(s, i, p)
                if p == 1:
                    residual(s, i, p, 0, 0)
                    residual(s, i, p, 1, 1)

            def stack_queries(s, i, q):
                pair = slice(2 * (q % 2), 2 * (q % 2) + 2)
                dve.wait_ge(q_high, filled(at("quarter", s, i, 0, q)))
                dve.scalar_tensor_tensor(Qs[:, pair, :], Qs[:, pair, :].bitcast(F32), hilos[:, 0:1], qf[:, :, :],
                                         ALU.mult, ALU.add).then_inc(q_ready, 1)

            def band(s, i, k):
                if STAGES[s] == "A0":
                    n = score_use(k)
                    dve.wait_ge(g_full, filled(at("G", s, i, 0, n)))
                    dve.tensor_tensor(S(n)[:, 0:KEYS], S(n)[:, 0:KEYS], aux[:, 0:KEYS], ALU.mult).then_inc(banded, 1)

            def maxima(s, i, k):
                n = score_use(k)
                sc = S(n)
                if STAGES[s] == "A0":
                    dve.wait_ge(banded, i * (4 * HEADS) + (k + 1))
                else:
                    dve.wait_ge(g_full, filled(at("G", s, i, 0, n)))
                dve.tensor_reduce(nmax[:, k % 3, 0:1], sc[:, 0:P], AX.X, ALU.max, negate=True)
                dve.tensor_reduce(nmax[:, k % 3, 1:2], sc[:, P:KEYS], AX.X, ALU.max, negate=True).then_inc(maxed, 1)

            def evacuate(s, i, k):
                dve.wait_ge(u_full, filled(at("U", s, i, 0, k)))
                dve.wait_ge(pv_done, free(at("head", s, i, 0, k)))
                dve.tensor_copy(PT[:, k % 2, :], TURNED[k % 2][:, 0:KEYS]).then_inc(u_done, 1)

            def sums_leave(s, i, b):
                dve.wait_ge(pv_done, made(at("head", s, i, 0, HEADS * b + HEADS - 1)))
                dve.tensor_copy(sums, SUMS[:, :]).then_inc(a_done, 1)

            def values(s, i, b):
                if b >= 1:
                    dve.wait_ge(pv_done, made(at("head", s, i, 0, HEADS * b - 1)))
                dve.wait_ge(t_full, filled(at("Tf", s, i, 0, VALUES_TF[b])))
                for e in range(2):
                    def every_other(v):
                        return v.rearrange("p t (h e d) -> p t h e d", e=2, d=HD)[:, :, :, e, :]
                    src = every_other(three(T(static("T", s, 0, VALUES_T[b]))[:, :], 2))
                    dst = Vs.rearrange("p t (h e) n -> p t h e n", e=2)[:, :, :, e, e * HD:(e + 1) * HD]
                    if STAGES[s] == "A0":
                        ins = dve.tensor_copy(dst, src)
                    else:
                        bias = aux[:, 0:C].rearrange("p (h e d) -> p h e d", e=2, d=HD)[:, :, e, :]
                        ins = dve.tensor_tensor(dst, src, bias.unsqueeze(1).broadcast_to([P, 2, HEADS // 2, HD]), ALU.add)
                ins.then_inc(t_done, 1)

            def shares(s, i, b):
                d = den[:, b % 2, :, :]
                dve.reciprocal(d, d)
                dve.drain()
                dve.tensor_copy(cn[:, :, :].rearrange("p t (h d) -> p (t h) d", h=HEADS),
                                d.rearrange("p t h -> p (t h)").unsqueeze(2).broadcast_to([P, 2 * HEADS, HD]))\
                   .then_inc(shared, 1)

            def context(s, i, b):
                dve.wait_ge(t_full, filled(at("Tf", s, i, 0, CONTEXT_TF[b])))
                dve.tensor_tensor(cn.rearrange("p t n -> p (t n)"), sums, T(static("T", s, 0, CONTEXT_T[b]))[:, :],
                                  ALU.mult).then_inc(ctx_made, 1)

            def ctx_lows(s, i, b):
                dve.wait_ge(ctx_high, filled(at("half", s, i, 0, b)))
                dve.tensor_tensor(cT[:, 1, :, :].rearrange("p c n -> p (c n)"), cn.rearrange("p t n -> p (t n)"),
                                  cT[:, 0, :, :].rearrange("p c n -> p (c n)").bitcast(F32), ALU.subtract)\
                   .then_inc(t_done, 1)

            def output(s, i, b):
                pair = xt(group(i, b // 2), 2 * (b % 2), 2)
                if STAGES[s] == "A1":
                    dve.tensor_tensor(pair.rearrange("p (t n) -> p t n", t=2), pair.rearrange("p (t n) -> p t n", t=2),
                                      aux[:, C:2 * C].unsqueeze(1).broadcast_to([P, 2, C]), ALU.add)
                    dve.drain()
                dve.wait_ge(t_full, filled(at("Tf", s, i, 0, OUTPUT_TF[b])))
                dve.tensor_tensor(pair, pair, T(static("T", s, 0, OUTPUT_T[b]))[:, :], ALU.add).then_inc(t_done, 1)

            def attention(s, i):
                stack_queries(s, i, 0)
                band(s, i, 0)
                maxima(s, i, 0)
                values(s, i, 0)
                for k in range(1, AHEAD):
                    band(s, i, k)
                    maxima(s, i, k)
                for k in range(4 * HEADS):
                    b, p = k // HEADS, k // (2 * HEADS)
                    if k + AHEAD < 4 * HEADS:
                        band(s, i, k + AHEAD)
                        maxima(s, i, k + AHEAD)
                    if STAGES[s] == "A1":
                        evacuate(s, i, k)
                    u = k % (2 * HEADS)
                    if k >= HEADS:
                        if k % HEADS == 0:
                            values(s, i, b)
                            sums_leave(s, i, b - 1)
                        if k % HEADS == 2:
                            shares(s, i, b - 1)
                        if k % HEADS == 5:
                            context(s, i, b - 1)
                        if k % HEADS == 7:
                            ctx_lows(s, i, b - 1)
                        if k % HEADS == 9:
                            output(s, i, b - 1)
                    if 3 <= u < 3 + GT:
                        tile_stats(following(i, p), u - 3)
                    if u == 3 + GT:
                        seeds()
                    if u == 11 or u == 12:
                        xhats(s, i, p, tiles=range(2 * (u - 11), 2 * (u - 11) + 2))
                    if u == 14 or u == 15:
                        xn_lows(s, i, p, chunks=[u - 14])
                    if k in QUERIES_AT:
                        stack_queries(s, i, QUERIES_AT[k])
                sums_leave(s, i, 3)
                shares(s, i, 3)
                context(s, i, 3)
                ctx_lows(s, i, 3)
                output(s, i, 3)

            xhats(0, 0, 0, first=True)
            xn_lows(0, 0, 0, first=True)
            for s in range(len(STAGES)):
                if s == 3:
                    for n in range(FIRST_PIECES, len(pieces)):
                        split_low(dve, n)
                    dve.drain()
                if STAGES[s] == "A1":
                    dve.wait_ge(auxl, 64)
                if s == 1:
                    dve.wait_ge(side_done, 4 * CK + RING)
                if kind(s) == "A":
                    dve.drain()
                    dve.memset(WF[:, 0:2 * HEADS * 2 * HD], 0.0)
                    dve.drain()
                if kind(s) == "E":
                    dve.drain()
                    dve.memset(countb[:, :], 0.0)
                with dve.Fori(0, GROUPS // 2) as i:
                    if kind(s) == "A":
                        attention(s, i)
                    else:
                        for p in range(2):
                            (ffn if kind(s) == "F" else experts)(s, i, p)

        @block.tensor
        def _(pe):
            pe.wait_ge(cast, 1)
            pe.wait_ge(set_up, 1)
            pe.wait_ge(consts, 16 * 8)
            for n in range(4):
                v = slot(n)
                pe.wait_ge(stage_full[n % 2], stage_value(n))
                for a in range(CK):
                    pe.wait_ge(u_done, free(2 * n + a))
                    for b in range(CK):
                        mm = pe.matmul(U(2 * n + a)[:, :], hadf[:, a & b, :], v[:, b * 512:(b + 1) * 512],
                                       start=(b == 0), stop=(b == CK - 1))
                    mm.then_inc(u_full, 1)
            for ch in range(2):
                v = slot(4 + ch)
                pe.wait_ge(weights, ch + 1)
                for half in range(2):
                    pe.wait_ge(u_done, free(8 + 2 * ch + half))
                    for q in range(4):
                        at_col = CHUNK_AT[4 * half + q]
                        mm = pe.matmul(U(8 + 2 * ch + half)[:, q * P:(q + 1) * P], hadf[:, 0, :],
                                       v[:, at_col:at_col + P], start=True, stop=True)
                    mm.then_inc(u_full, 1)
            v = slot(7)
            pe.wait_ge(stage_full[1], stage_value(7))
            for m in range(2):
                pe.wait_ge(u_done, free(12 + m))
                for c in range(CK):
                    mm = pe.matmul(U(12 + m)[:, c * C:(c + 1) * C], v[0:LATENT, m * C + c * P:m * C + (c + 1) * P],
                                   v[0:LATENT, (2 + m) * C:(3 + m) * C], start=True, stop=True)
                mm.then_inc(u_full, 1)

            def transposes(s, i, p, first=False):
                v = 0 if first else at("unit", s, i, p) + 1
                unit, n = (0, 0) if first else norm_use(s, p)
                ti = 0 if first else at("T", s, i, unit, n)
                tn = 0 if first else static("T", s, unit, n)
                pe.wait_ge(t_done, free(ti + 1))
                for t in range(GT):
                    pe.wait_ge(xh_full, v * GT + t + 1)
                    for c in range(CK):
                        mm = pe.transpose(T(tn + c)[:, t * P:(t + 1) * P], xh[:, t, c * P:(c + 1) * P], identf[:, :])
                    mm.then_inc(xh_read, 1)

            def xn_ready(s, i, p):
                if kind(s) == "A" and p == 1:
                    pe.wait_ge(t_done, made(at("T", s, i, 0, NORM_T[0] + 1)))
                else:
                    pe.wait_ge(t_done, made(at("T", s, i, p) - 1))

            PASSES = ((0, 0), (1, 0), (0, 1))

            def up(bank, w, c_of, rhs, n):
                k = 0
                for c in range(CK):
                    for a, b in PASSES:
                        mm = pe.matmul(bank, c_of(w, a, c), rhs(b, c), start=(k == 0), stop=(k == 3 * CK - 1))
                        k += 1
                return mm

            def down(bank_of, src_of, w_of, first, last, before_low=None):
                for a, b in ((0, 0), (0, 1), (1, 0)):
                    if a == 1 and before_low is not None:
                        before_low()
                    for t in range(GT):
                        mm = pe.matmul(bank_of(t // 2)[:, (t % 2) * C:(t % 2 + 1) * C], src_of(a, t), w_of(b),
                                       start=(first and a == 0 and b == 0 and t % 2 == 0),
                                       stop=(last and a == 1), skip_group_check=True)
                        yield mm

            def ups(s, i, p, j, gate, upw):
                buf = p
                rhs = lambda b, c: xnv[:, buf, b, c, :]
                pe.wait_ge(g_done, free(at("G", s, i, p, j)))
                up(G(static("G", s, p, j))[:, :], gate, lambda w, a, c: w[:, a, c, j * P:(j + 1) * P], rhs, 0)\
                    .then_inc(g_full, 1)
                pe.wait_ge(u_done, free(at("U", s, i, p, j)))
                up(U(static("U", s, p, j))[:, :], upw, lambda w, a, c: w[:, a, c, j * P:(j + 1) * P], rhs, 0)\
                    .then_inc(u_full, 1)

            def downs(s, i, p, j, w, first, last):
                b = static("h", s, p, j) % 2
                h = at("h", s, i, p, j)
                n = static("A", s, p)
                if first:
                    pe.wait_ge(a_done, free(at("A", s, i, p, 1)))
                pe.wait_ge(h_high, filled(h))
                k = 0
                for mm in down(lambda pair: A(n + pair), lambda a, t: hid[:, b, a, t * P:(t + 1) * P],
                               lambda part: w[:, part, j, :], first, last,
                               lambda: pe.wait_ge(h_ready, made(h))):
                    k += 1
                    if last and k == 1:
                        mm.then_inc(xn_read, 1)
                mm.then_inc(h_read, 1)

            def ffn(s, i, p):
                xn_ready(s, i, p)
                for j in range(FJ):
                    ups(s, i, p, j, fg, fu)
                    if j == 0 and p == 1:
                        downs(s, i, 0, FJ - 1, fd, False, True)
                    if j >= 1:
                        downs(s, i, p, j - 1, fd, j == 1, False)
                    if j == 5:
                        transposes(s, i, p)
                if p == 1:
                    downs(s, i, p, FJ - 1, fd, False, True)

            def experts(s, i, p):
                xn_ready(s, i, p)
                pe.wait_ge(t_done, free(at("T", s, i, p, 0)))
                for t in range(GT):
                    k = 0
                    for c in range(CK):
                        for a, b in PASSES:
                            mm = pe.matmul(T(static("T", s, p, 0))[:, t * EXPERTS:(t + 1) * EXPERTS],
                                           xnv[:, p, a, c, t * P:(t + 1) * P], mg[:, b, c, :],
                                           start=(k == 0), stop=(k == 3 * CK - 1))
                            k += 1
                mm.then_inc(t_full, 1)
                pe.wait_ge(t_done, free(at("T", s, i, p, 1)))
                up(T(static("T", s, p, 1))[:, :], shu, lambda w, a, c: w[:, a, c, :], lambda b, c: xnv[:, p, b, c, :], 0)\
                    .then_inc(t_full, 1)
                mj = lambda w, a, c, v, j: w[:, a, c, v, j, :]

                def ups_m(j):
                    rhs = lambda b, c: xnv[:, p, b, c, :]
                    pe.wait_ge(g_done, free(at("G", s, i, p, j)))
                    up(G(static("G", s, p, j))[:, :], mw, lambda w, a, c: w[:, a, c, 0, j, :], rhs, 0).then_inc(g_full, 1)
                    pe.wait_ge(u_done, free(at("U", s, i, p, j)))
                    up(U(static("U", s, p, j))[:, :], mw, lambda w, a, c: w[:, a, c, 1, j, :], rhs, 0).then_inc(u_full, 1)

                if p == 1:
                    downs(s, i, 0, MJ - 1, md, False, True)
                ups_m(0)
                pe.wait_ge(t_done, free(at("T", s, i, p, 2)))
                pe.wait_ge(chosen, filled(at("moe", s, i, p)))
                for t in range(GT):
                    dst = T(static("T", s, p, 2))[:, t * EXPERTS:(t + 1) * EXPERTS]
                    pe.matmul(dst, onesb[:, :], countb[:, :], start=True, stop=False)
                    for r in range(t):
                        pe.matmul(dst, onesb[:, :], maskb[:, r, :], start=False, stop=False)
                    mm = pe.matmul(dst, beforeb[:, :], maskb[:, t, :], start=False, stop=True)
                mm.then_inc(t_full, 1)
                ups_m(1)
                pe.wait_ge(t_done, free(at("T", s, i, p, 3)))
                pe.wait_ge(wmade, filled(at("moe", s, i, p)))
                for t in range(GT):
                    mm = pe.transpose(T(static("T", s, p, 3))[:, t * P:(t + 1) * P],
                                      w2[:, t, :, :].rearrange("p d e -> p (d e)"), identf[:, :])
                mm.then_inc(t_full, 1)
                n = static("A", s, p)
                pe.wait_ge(a_done, free(at("A", s, i, p, 1)))
                pe.wait_ge(sh_ready, filled(at("moe", s, i, p)))
                for mm in down(lambda pair: A(n + pair), lambda a, t: shh[0:SHARED, a, t * P:(t + 1) * P],
                               lambda part: shd[0:SHARED, part, :], True, False):
                    pass
                pe.wait_ge(stage_done, len(pieces) + RING)
                for j in range(MJ):
                    if j >= 2:
                        ups_m(j)
                    if j >= 1:
                        downs(s, i, p, j - 1, md, False, False)
                    if j == 12:
                        transposes(s, i, p)
                if p == 1:
                    downs(s, i, p, MJ - 1, md, False, True)

            def project(s, i, item):
                m, q = item
                n, p, b = score_use(item), q // 4, q // 2 % 2
                if item == (0, 0) or item == (0, 4):
                    xn_ready(s, i, p)
                pe.wait_ge(g_done, score_free(s, i, n))
                for t in range(2):
                    col = 2 * (q % 2) + t
                    mm = up(S(n)[:, t * C:(t + 1) * C], (wq, wk)[m],
                            lambda w_, a, c: w_[:, a, c, col * P:(col + 1) * P],
                            lambda r, c: xnv[:, p, r, c, b * BATCH:(b + 1) * BATCH], 0)
                mm.then_inc(g_full, 1)

            def values(s, i, b):
                n = VALUES_T[b]
                pe.wait_ge(t_done, free(at("T", s, i, 0, n)))
                for t in range(2):
                    k = 0
                    for c in range(CK):
                        for a, r in PASSES:
                            lo = (b % 2) * BATCH + t * P
                            mm = pe.matmul(T(static("T", s, 0, n))[:, t * C:(t + 1) * C], xnv[:, b // 2, a, c, lo:lo + P],
                                           wv[:, r, c, :], start=(k == 0), stop=(k == 3 * CK - 1))
                            k += 1
                mm.then_inc(t_full, 1)

            def scores(s, i, k):
                n = score_use(k)
                h = k % HEADS
                t, rows = h // 4, slice(32 * (h % 4), 32 * (h % 4) + 32)
                bank = S(n)
                pe.wait_ge(g_done, score_free(s, i, n))
                if k % 8 == 0:
                    pe.wait_ge(q_ready, at("quarter", s, i, 0, k // 8) + 2)
                    pe.wait_ge(k_ready, at("quarter", s, i, 0, k // 8) + 2)
                queries = [Qs[rows, t, q * P:(q + 1) * P] for q in range(2)]
                pe.matmul(bank[:, 0:P], queries[0], KA[rows, t, 0:P], start=True, stop=False, skip_group_check=True)
                pe.matmul(bank[:, P:KEYS], queries[1], KA[rows, t, :], start=False, stop=False, skip_group_check=True)
                diagonals = bank[:, 0:2 * BATCH].rearrange("p (a n) -> p a n", a=2)[:, :, 0:P]
                pe.matmul(diagonals, identb[:, :], causalb[:, :].unsqueeze(1).broadcast_to([P, 2, P]), start=False,
                          stop=False, skip_group_check=True)
                pe.matmul(bank[:, 0:P], queries[0], KB[rows, t, 0:P], start=False, stop=True, skip_group_check=True)
                pe.matmul(bank[:, P:KEYS], queries[1], KB[rows, t, :], start=False, stop=True, skip_group_check=True)\
                    .then_inc(g_full, 1)

            def turn(s, i, k):
                pe.wait_ge(g_done, made(at("G", s, i, 0, score_use(k))))
                pe.wait_ge(u_done, free(at("U", s, i, 0, k)))
                for c in range(3):
                    mm = pe.transpose(TURNED[k % 2][:, c * P:(c + 1) * P], Pr[:, k % 2, c * P:(c + 1) * P], identf[:, :])
                mm.then_inc(u_full, 1)

            def mix(s, i, k):
                b, h = k // HEADS, k % HEADS
                bank = SUMS
                if h == 0:
                    pe.wait_ge(a_done, at("A", s, i, 0, b) + RING)
                    pe.wait_ge(t_done, made(at("T", s, i, 0, VALUES_T[b])))
                pe.wait_ge(u_done, made(at("U", s, i, 0, k)))
                strip = slice(32 * (h % 8 // 2), 32 * (h % 8 // 2) + 32)
                dst = bank[strip, (h // 8) * C:(h // 8 + 1) * C]
                pe.matmul(dst, Vs[:, 0, h, :], PT[:, k % 2, 0:2 * P], start=(h % 2 == 0), stop=False, skip_group_check=True)
                pe.matmul(dst[:, P:2 * P], Vs[:, 1, h, :], PT[:, k % 2, 2 * P:KEYS], start=False, stop=(h % 2 == 1),
                          skip_group_check=True).then_inc(pv_done, 1)

            def turn_shares(s, i, b):
                n = CONTEXT_T[b]
                pe.wait_ge(shared, filled(at("half", s, i, 0, b)))
                pe.wait_ge(t_done, free(at("T", s, i, 0, n)))
                for c in range(CK):
                    for t in range(2):
                        lo = c * BATCH + t * P
                        mm = pe.transpose(T(static("T", s, 0, n))[:, lo:lo + P], cn[:, t, c * P:(c + 1) * P], identf[:, :])
                mm.then_inc(t_full, 1)

            def project_out(s, i, b):
                n = OUTPUT_T[b]
                pe.wait_ge(t_done, made(at("T", s, i, 0, CONTEXT_T[b])))
                for t in range(2):
                    k = 0
                    for c in range(CK):
                        for a, r in PASSES:
                            mm = pe.matmul(T(static("T", s, 0, n))[:, t * C:(t + 1) * C], cT[:, a, c, t * P:(t + 1) * P],
                                           wo[:, r, c, :], start=(k == 0), stop=(k == 3 * CK - 1))
                            if b % 2 == 1 and t == 0 and k == 0:
                                mm.then_inc(xn_read, 1)
                            k += 1
                mm.then_inc(t_full, 1)

            def attention(s, i):
                def score(k):
                    for item in PARTS_BEFORE.get(k, []):
                        project(s, i, item)
                    scores(s, i, k)

                project(s, i, (0, 0))
                project(s, i, (1, 0))
                pe.wait_ge(a_done, at("A", s, i, 0, 0) + RING)
                values(s, i, 0)
                scores(s, i, 0)
                for k in range(1, AHEAD):
                    score(k)
                for k in range(4 * HEADS):
                    b, p = k // HEADS, k // (2 * HEADS)
                    if k + AHEAD < 4 * HEADS:
                        score(k + AHEAD)
                    turn(s, i, k)
                    if k >= 1:
                        mix(s, i, k - 1)
                    if b < 3 and k % HEADS == HEADS - 1:
                        values(s, i, b + 1)
                    if b >= 1 and k % HEADS == 4:
                        turn_shares(s, i, b - 1)
                    if b >= 1 and k % HEADS == 8:
                        project_out(s, i, b - 1)
                    if k % (2 * HEADS) == 13:
                        transposes(s, i, p)
                mix(s, i, 4 * HEADS - 1)
                turn_shares(s, i, 3)
                project_out(s, i, 3)

            transposes(0, 0, 0, first=True)
            for s in range(len(STAGES)):
                if s == 0:
                    pe.wait_ge(stage_done, 6 + RING)
                if s == 1:
                    pe.wait_ge(stage_done, FIRST_PIECES + RING)
                if s == 3:
                    pe.wait_ge(side_done, 4 * CK + RING)
                    pe.wait_ge(stage_done, FIRST_PIECES + 1 + RING)
                if s == 4:
                    pe.wait_ge(next_done, CK + 1)
                with pe.Fori(0, GROUPS // 2) as i:
                    if kind(s) == "A":
                        attention(s, i)
                    else:
                        for p in range(2):
                            (ffn if kind(s) == "F" else experts)(s, i, p)


def kernel(**inputs):
    import numpy as np
    import concourse.bacc as bacc
    from concourse.bass_utils import run_bass_kernel_spmd as run

    g = {k: np.asarray(v) for k, v in inputs.items()}

    def stacked(b):
        return np.repeat(b.reshape(4, 4, 1, HD), 2, axis=2).reshape(4, P).T

    up = g["L1_ffn_w_up"].reshape(EXPERTS, C, 2, MJ, 2).transpose(1, 2, 3, 4, 0).reshape(C, 2 * MJ * P)
    down = g["L1_ffn_w_down"].reshape(EXPERTS, MJ, 2, C).transpose(1, 2, 0, 3).reshape(MJ * P, C)

    n = np.arange(P)
    bits = np.array([[bin(a & b).count("1") % 2 for b in range(P)] for a in range(P)])
    had = np.where(bits == 1, -1.0, 1.0) / np.sqrt(C)
    query, key = n[:, None], n[None, :]
    diagonal = np.where(np.abs(query - key) < WINDOW, 1.0 + ALPHA, 1.0)
    below = np.where(query + P - key < WINDOW, 1.0 + ALPHA, 1.0)
    f = np.float32
    arrays = {
        "x": g["L0_attn_hidden_states"].reshape(TOKENS, C),
        "fgate": g["L0_ffn_W_gate"].T, "fup": g["L0_ffn_W_up"].T, "fdown": g["L0_ffn_W_down"].T,
        "su_ug": g["L0_ffn_SU_ug"].reshape(CK, P).T, "su_dp": g["L0_ffn_SU_dp"].reshape(FJ, P).T,
        "ws_ug": np.concatenate([g["L0_ffn_Wscale_ug"][INTER:], g["L0_ffn_Wscale_ug"][:INTER]]),
        "ws_dp": g["L0_ffn_Wscale_dp"],
        "q0": g["L0_attn_w_q"].T, "o0": g["L0_attn_w_out"].T,
        "kd0": g["L0_attn_w_k_down"], "vd0": g["L0_attn_w_v_down"],
        "ql0": g["L0_attn_q_to_latent"].transpose(2, 0, 1).reshape(LATENT, C),
        "vu0": g["L0_attn_v_up"].transpose(1, 0, 2).reshape(LATENT, C),
        "q1": g["L1_attn_wq"].T, "k1": g["L1_attn_wk"].T, "v1": g["L1_attn_wv"].T, "o1": g["L1_attn_wo"].T,
        "bq": stacked(g["L1_attn_bq"]), "bk": stacked(g["L1_attn_bk"]), "bv": g["L1_attn_bv"], "bo": g["L1_attn_bo"],
        "mgate": g["L1_ffn_w_gate"], "mshup": g["L1_ffn_w_shared_up"], "mshdown": g["L1_ffn_w_shared_down"],
        "mup": up, "mdown": down,
        "had": had.astype(f), "ident": np.eye(P, dtype=f),
        "before": (query < key).astype(f),
        "bandm": np.concatenate([diagonal, below, diagonal], axis=1).astype(f),
        "causal": np.where(key > query, -1e30, 0.0).astype(f),
        "hilo": np.where(n % 32 < HD, 0.0, -1.0).reshape(P, 1).astype(f),
    }
    nc = bacc.Bacc("TRN2", target_bir_lowering=False, num_devices=1)
    feeds, args = {}, {}
    for name, a in arrays.items():
        a = np.ascontiguousarray(a)
        feeds[name + "_dram"] = a
        args[name] = nc.dram_tensor(name + "_dram", a.shape, mybir.dt.from_np(a.dtype), kind="ExternalInput").ap()
    out = nc.dram_tensor("out_dram", (TOKENS, C), mybir.dt.float32, kind="ExternalOutput").ap()
    build(nc, **args, out=out)
    got = run(nc, [feeds], core_ids=[0]).results[0]["out_dram"]
    return np.asarray(got).reshape(TOKENS // BATCH, BATCH, C)
```
